# Optimizing a Trainium2 kernel written in Bass

```python
import numpy as np
import jax
import jax.numpy as jnp

def _softmax(x, axis=-1):
    return jax.nn.softmax(x, axis=axis)

def _gelu(x):
    return jax.nn.gelu(x, approximate=True)

def _silu(x):
    return jax.nn.silu(x)

def _sigmoid(x):
    return jax.nn.sigmoid(x)

def _layernorm(x, axis=-1, eps=1e-05):
    m = jnp.mean(x, axis=axis, keepdims=True)
    v = jnp.var(x, axis=axis, keepdims=True)
    return (x - m) / jnp.sqrt(v + eps)

def _scatter_add(tgt, idx, src, axis=0):
    return tgt.at[idx].add(src)

def _segment_sum(src, seg, n):
    return jax.ops.segment_sum(src, seg, n)
kernel_name = 'mk_xattn_ffn_d2_seqx_r4_8f49d8'

def setup_inputs(seed: int=0):
    np.random.seed(seed)
    _w = jnp.asarray

    def _rec_inputs():
        import jax
        import jax.numpy as jnp
        _rk = jax.random.key(seed)
        x = 7.22e-05 + 1 * jax.random.normal(jax.random.fold_in(_rk, 1), (8, 256, 256), jnp.float32)
        _lenS = 256 - jax.random.randint(jax.random.fold_in(_rk, 7), (8,), 0, max(1, 256 // 4) + 1, jnp.int32)
        _lenS2 = 256 - jax.random.randint(jax.random.fold_in(_rk, 8), (8,), 0, max(1, 256 // 4) + 1, jnp.int32)
        _ctx_768P = jax.random.normal(jax.random.fold_in(_rk, 11), (8, 16, 192), jnp.float32)
        _ctx_768c = jax.random.dirichlet(jax.random.fold_in(_rk, 511), 0.3 * jnp.ones((16,), jnp.float32), (8, 256))
        _ctx_768t = jnp.einsum('bsk,bkd->bsd', _ctx_768c, _ctx_768P)
        _ctx_768t = _ctx_768t * jax.lax.rsqrt(jnp.mean(jnp.square(_ctx_768t)) + 1e-12) * 0.953939
        ctx_768 = 3.88148e-05 + 0.999967 * (_ctx_768t + 0.3 * jax.random.normal(jax.random.fold_in(_rk, 611), (8, 256, 192), jnp.float32))
        _validS = jnp.arange(256)[None, :] < _lenS[:, None]
        _validS2 = jnp.arange(256)[None, :] < _lenS2[:, None]
        _causal = jnp.tril(jnp.ones((256, 256), dtype=bool))
        mask_BxS_bf1 = jnp.ones((8, 256), dtype=bool)
        mask_BxS2_bf1 = jnp.ones((8, 256), dtype=bool)
        return (x, ctx_768, mask_BxS_bf1, mask_BxS2_bf1)
    x, ctx_768, mask_BxS_bf1, mask_BxS2_bf1 = _rec_inputs()

    def _L0_xattn_setup():
        import jax, jax.numpy as jnp
        import numpy as np
        B, T, DT, G, DV = (16, 128, 256, 144, 192)
        H, DH = (4, 32)
        INNER = H * DH
        HID = 4 * DT
        N_STATE = 64
        K_TOP = 32

        def layernorm(x, g, b, eps=1e-05):
            m = x.mean(-1, keepdims=True)
            v = x.var(-1, keepdims=True)
            return (x - m) * jax.lax.rsqrt(v + eps) * g + b

        def s4d(x, log_dt, A_re, A_im, C_re, C_im, D_skip):
            Bb, L, D = x.shape
            dt = jnp.exp(log_dt)
            A = A_re + 1j * A_im
            C = C_re + 1j * C_im
            dtA = dt[:, None] * A
            dC = C * (jnp.exp(dtA) - 1.0) / A
            powers = jnp.exp(dtA[:, :, None] * jnp.arange(L))
            K = 2.0 * jnp.einsum('dn,dnl->dl', dC, powers).real
            n = 2 * L
            Kf = jnp.fft.rfft(K, n=n, axis=-1)
            xf = jnp.fft.rfft(x, n=n, axis=1)
            y = jnp.fft.irfft(xf * Kf.T[None], n=n, axis=1)[:, :L]
            return y + x * D_skip
        key = jax.random.key(seed)
        ks = jax.random.split(key, 16)
        s = 0.02
        inp = {'x_text': jax.random.normal(ks[0], (B, T, DT), jnp.float32), 'x_vision': jax.random.normal(ks[1], (B, G, DV), jnp.float32), 'text_mask': jnp.ones((B, T), bool), 'vision_mask': jnp.ones((B, G), bool), 'Wq': jax.random.normal(ks[2], (DT, INNER), jnp.float32) * s, 'Wk': jax.random.normal(ks[3], (DV, INNER), jnp.float32) * s, 'Wv': jax.random.normal(ks[4], (DV, DT), jnp.float32) * s, 'W_film_in': jax.random.normal(ks[5], (DT, 2 * DT), jnp.float32) * s, 'b_film_in': jnp.zeros((2 * DT,), jnp.float32), 'W_film_out': jax.random.normal(ks[6], (DT, 2 * DT), jnp.float32) * s, 'b_film_out': jnp.zeros((2 * DT,), jnp.float32), 'g_norm_in': jnp.ones((DT,), jnp.float32), 'b_norm_in': jnp.zeros((DT,), jnp.float32), 'g_norm_out': jnp.ones((DT,), jnp.float32), 'b_norm_out': jnp.zeros((DT,), jnp.float32), 'g_ffn': jnp.ones((DT,), jnp.float32), 'b_ffn': jnp.zeros((DT,), jnp.float32), 'W1': jax.random.normal(ks[7], (DT, HID), jnp.float32) * s, 'b1': jnp.zeros((HID,), jnp.float32), 'W2': jax.random.normal(ks[8], (HID, DT), jnp.float32) * s, 'b2': jnp.zeros((DT,), jnp.float32), 'log_dt': jnp.log(0.001) + jax.random.uniform(ks[9], (DT,), jnp.float32) * (jnp.log(0.1) - jnp.log(0.001)), 'A_re': -0.5 * jnp.ones((DT, N_STATE), jnp.float32), 'A_im': jnp.tile(jnp.pi * jnp.arange(N_STATE, dtype=jnp.float32), (DT, 1)), 'C_re': jax.random.normal(ks[10], (DT, N_STATE), jnp.float32) * 0.5 ** 0.5, 'C_im': jax.random.normal(ks[11], (DT, N_STATE), jnp.float32) * 0.5 ** 0.5, 'D_skip': jax.random.normal(ks[12], (DT,), jnp.float32), 'mod_gate': jnp.array(0.5, jnp.float32)}
        return inp
    _L0_xattn_all = _L0_xattn_setup()
    _L0_xattn_in = {k: v for k, v in _L0_xattn_all.items() if k in ('Wq', 'Wk', 'Wv', 'W_film_in', 'b_film_in', 'W_film_out', 'b_film_out', 'g_norm_in', 'b_norm_in', 'g_norm_out', 'b_norm_out', 'g_ffn', 'b_ffn', 'W1', 'b1', 'W2', 'b2', 'log_dt', 'A_re', 'A_im', 'C_re', 'C_im', 'D_skip', 'mod_gate')}
    del _L0_xattn_all

    def _L0_ffn_setup():
        import jax, jax.numpy as jnp
        import numpy as np
        D = 256
        LW = 16
        DEPTH = 8
        NN = 2 ** DEPTH - 1
        NL = 2 ** DEPTH
        B, S = (2, 256)

        def _fff(x, nw, nb, w1, b1, w2, b2, act):
            node = jnp.zeros(x.shape[:2], dtype=jnp.int32)
            for _ in range(DEPTH):
                logit = jnp.einsum('bsd,bsd->bs', x, nw[node]) + nb[node]
                node = 2 * node + 1 + (logit > 0).astype(jnp.int32)
            leaf = node - NN
            h = act(jnp.einsum('bsd,bsdl->bsl', x, w1[leaf]) + b1[leaf])
            return jnp.einsum('bsl,bsld->bsd', h, w2[leaf]) + b2[leaf]

        def _forward(x, q_nw, q_nb, q_w1, q_b1, q_w2, q_b2, k_nw, k_nb, k_w1, k_b1, k_w2, k_b2, v_nw, v_nb, v_w1, v_b1, v_w2, v_b2, f_nw, f_nb, f_w1, f_b1, f_w2, f_b2):
            mu = jnp.mean(x, -1, keepdims=True)
            sd = jnp.std(x, -1, ddof=1, keepdims=True)
            xn = (x - mu) / jnp.sqrt(sd + 1e-05)
            relu = jax.nn.relu
            q = _fff(xn, q_nw, q_nb, q_w1, q_b1, q_w2, q_b2, relu)
            k = _fff(xn, k_nw, k_nb, k_w1, k_b1, k_w2, k_b2, relu)
            v = _fff(xn, v_nw, v_nb, v_w1, v_b1, v_w2, v_b2, relu)
            att = jax.nn.softmax(jnp.einsum('bqd,bkd->bqk', q, k) / jnp.sqrt(jnp.float32(D)), axis=-1)
            y = xn + jnp.einsum('bqk,bkd->bqd', att, v)
            gelu = lambda t: jax.nn.gelu(t, approximate=False)
            return y + _fff(y, f_nw, f_nb, f_w1, f_b1, f_w2, f_b2, gelu)

        def _make_fff_params(key, scale_in, scale_leaf):
            ks = jax.random.split(key, 4)
            nw = jax.random.normal(ks[0], (NN, D), jnp.float32) * scale_in
            nb = jnp.zeros((NN,), jnp.float32)
            w1 = jax.random.normal(ks[1], (NL, D, LW), jnp.float32) * scale_in
            b1 = jax.random.normal(ks[2], (NL, LW), jnp.float32) * 0.01
            w2 = jax.random.normal(ks[3], (NL, LW, D), jnp.float32) * scale_leaf
            b2 = jnp.zeros((NL, D), jnp.float32)
            return (nw, nb, w1, b1, w2, b2)
        key = jax.random.key(seed)
        kx, kq, kk, kv, kf = jax.random.split(key, 5)
        s_in = 1.0 / np.sqrt(D)
        s_lf = 1.0 / np.sqrt(LW)
        inp = {'x': jax.random.normal(kx, (B, S, D), jnp.float32)}
        for name, kk_ in (('q', kq), ('k', kk), ('v', kv), ('f', kf)):
            nw, nb, w1, b1, w2, b2 = _make_fff_params(kk_, s_in, s_lf)
            inp.update({f'{name}_nw': nw, f'{name}_nb': nb, f'{name}_w1': w1, f'{name}_b1': b1, f'{name}_w2': w2, f'{name}_b2': b2})
        return inp
    _L0_ffn_all = _L0_ffn_setup()
    _L0_ffn_in = {k: v for k, v in _L0_ffn_all.items() if k in ('q_nw', 'q_nb', 'q_w1', 'q_b1', 'q_w2', 'q_b2', 'k_nw', 'k_nb', 'k_w1', 'k_b1', 'k_w2', 'k_b2', 'v_nw', 'v_nb', 'v_w1', 'v_b1', 'v_w2', 'v_b2', 'f_nw', 'f_nb', 'f_w1', 'f_b1', 'f_w2', 'f_b2')}
    del _L0_ffn_all

    def _L1_xattn_setup():
        import jax, jax.numpy as jnp
        import numpy as np
        N_HEADS = 16
        DIM_EMBED = 256
        DIM_CROSS = 192
        DIM_HEAD = DIM_EMBED // N_HEADS
        key = jax.random.key(seed)
        ks = jax.random.split(key, 10)
        B, Sq, Sk = (8, 1024, 77)
        s_e = 1.0 / np.sqrt(DIM_EMBED)
        s_c = 1.0 / np.sqrt(DIM_CROSS)
        return {'x': jax.random.normal(ks[0], (B, Sq, DIM_EMBED), jnp.float32), 'y': jax.random.normal(ks[1], (B, Sk, DIM_CROSS), jnp.float32), 'wq': jax.random.normal(ks[2], (DIM_EMBED, DIM_EMBED), jnp.float32) * s_e, 'bq': jax.random.normal(ks[3], (DIM_EMBED,), jnp.float32) * 0.01, 'wk': jax.random.normal(ks[4], (DIM_CROSS, DIM_EMBED), jnp.float32) * s_c, 'bk': jax.random.normal(ks[5], (DIM_EMBED,), jnp.float32) * 0.01, 'wv': jax.random.normal(ks[6], (DIM_CROSS, DIM_EMBED), jnp.float32) * s_c, 'bv': jax.random.normal(ks[7], (DIM_EMBED,), jnp.float32) * 0.01, 'wo': jax.random.normal(ks[8], (DIM_EMBED, DIM_EMBED), jnp.float32) * s_e, 'bo': jax.random.normal(ks[9], (DIM_EMBED,), jnp.float32) * 0.01}
    _L1_xattn_all = _L1_xattn_setup()
    _L1_xattn_in = {k: v for k, v in _L1_xattn_all.items() if k in ('wq', 'bq', 'wk', 'bk', 'wv', 'bv', 'wo', 'bo')}
    del _L1_xattn_all

    def _L1_ffn_setup():
        import jax, jax.numpy as jnp
        import numpy as np
        K = 4
        ROUTED_SCALING = 1.0
        NORM_TOPK = True

        def _gate(hidden_states, router_w, router_bias):
            logits = jnp.einsum('bsh,he->bse', hidden_states, router_w).astype(jnp.float32)
            scores = jax.nn.softmax(logits, axis=-1)
            corrected = scores + router_bias
            _, top_k_indices = jax.lax.top_k(corrected, K)
            top_k_weights = jnp.take_along_axis(scores, top_k_indices, axis=-1)
            if NORM_TOPK:
                top_k_weights = top_k_weights / (top_k_weights.sum(-1, keepdims=True) + 1e-20)
            top_k_weights = top_k_weights * ROUTED_SCALING
            return (top_k_weights.astype(hidden_states.dtype), top_k_indices)
        key = jax.random.key(seed)
        ks = jax.random.split(key, 9)
        B, S, H, E, I, IS = (2, 256, 256, 8, 128, 512)
        sc = 0.02
        return {'hidden_states': jax.random.normal(ks[0], (B, S, H), jnp.float32), 'router_w': jax.random.normal(ks[1], (H, E), jnp.float32) * sc, 'router_bias': jnp.zeros((), jnp.float32), 'gate_w': jax.random.normal(ks[2], (E, H, I), jnp.float32) * sc, 'up_w': jax.random.normal(ks[3], (E, H, I), jnp.float32) * sc, 'down_w': jax.random.normal(ks[4], (E, I, H), jnp.float32) * sc, 's_gate_w': jax.random.normal(ks[5], (H, IS), jnp.float32) * sc, 's_up_w': jax.random.normal(ks[6], (H, IS), jnp.float32) * sc, 's_down_w': jax.random.normal(ks[7], (IS, H), jnp.float32) * sc}
    _L1_ffn_all = _L1_ffn_setup()
    _L1_ffn_in = {k: v for k, v in _L1_ffn_all.items() if k in ('router_w', 'router_bias', 'gate_w', 'up_w', 'down_w', 's_gate_w', 's_up_w', 's_down_w')}
    del _L1_ffn_all
    return {'x': x, 'ctx_768': ctx_768, 'mask_BxS_bf1': mask_BxS_bf1, 'mask_BxS2_bf1': mask_BxS2_bf1, 'L0_xattn_Wq': _L0_xattn_in['Wq'], 'L0_xattn_Wk': _L0_xattn_in['Wk'], 'L0_xattn_Wv': _L0_xattn_in['Wv'], 'L0_xattn_W_film_in': _L0_xattn_in['W_film_in'], 'L0_xattn_b_film_in': _L0_xattn_in['b_film_in'], 'L0_xattn_W_film_out': _L0_xattn_in['W_film_out'], 'L0_xattn_b_film_out': _L0_xattn_in['b_film_out'], 'L0_xattn_g_norm_in': _L0_xattn_in['g_norm_in'], 'L0_xattn_b_norm_in': _L0_xattn_in['b_norm_in'], 'L0_xattn_g_norm_out': _L0_xattn_in['g_norm_out'], 'L0_xattn_b_norm_out': _L0_xattn_in['b_norm_out'], 'L0_xattn_g_ffn': _L0_xattn_in['g_ffn'], 'L0_xattn_b_ffn': _L0_xattn_in['b_ffn'], 'L0_xattn_W1': _L0_xattn_in['W1'], 'L0_xattn_b1': _L0_xattn_in['b1'], 'L0_xattn_W2': _L0_xattn_in['W2'], 'L0_xattn_b2': _L0_xattn_in['b2'], 'L0_xattn_log_dt': _L0_xattn_in['log_dt'], 'L0_xattn_A_re': _L0_xattn_in['A_re'], 'L0_xattn_A_im': _L0_xattn_in['A_im'], 'L0_xattn_C_re': _L0_xattn_in['C_re'], 'L0_xattn_C_im': _L0_xattn_in['C_im'], 'L0_xattn_D_skip': _L0_xattn_in['D_skip'], 'L0_xattn_mod_gate': _L0_xattn_in['mod_gate'], 'L0_ffn_q_nw': _L0_ffn_in['q_nw'], 'L0_ffn_q_nb': _L0_ffn_in['q_nb'], 'L0_ffn_q_w1': _L0_ffn_in['q_w1'], 'L0_ffn_q_b1': _L0_ffn_in['q_b1'], 'L0_ffn_q_w2': _L0_ffn_in['q_w2'], 'L0_ffn_q_b2': _L0_ffn_in['q_b2'], 'L0_ffn_k_nw': _L0_ffn_in['k_nw'], 'L0_ffn_k_nb': _L0_ffn_in['k_nb'], 'L0_ffn_k_w1': _L0_ffn_in['k_w1'], 'L0_ffn_k_b1': _L0_ffn_in['k_b1'], 'L0_ffn_k_w2': _L0_ffn_in['k_w2'], 'L0_ffn_k_b2': _L0_ffn_in['k_b2'], 'L0_ffn_v_nw': _L0_ffn_in['v_nw'], 'L0_ffn_v_nb': _L0_ffn_in['v_nb'], 'L0_ffn_v_w1': _L0_ffn_in['v_w1'], 'L0_ffn_v_b1': _L0_ffn_in['v_b1'], 'L0_ffn_v_w2': _L0_ffn_in['v_w2'], 'L0_ffn_v_b2': _L0_ffn_in['v_b2'], 'L0_ffn_f_nw': _L0_ffn_in['f_nw'], 'L0_ffn_f_nb': _L0_ffn_in['f_nb'], 'L0_ffn_f_w1': _L0_ffn_in['f_w1'], 'L0_ffn_f_b1': _L0_ffn_in['f_b1'], 'L0_ffn_f_w2': _L0_ffn_in['f_w2'], 'L0_ffn_f_b2': _L0_ffn_in['f_b2'], 'L1_xattn_wq': _L1_xattn_in['wq'], 'L1_xattn_bq': _L1_xattn_in['bq'], 'L1_xattn_wk': _L1_xattn_in['wk'], 'L1_xattn_bk': _L1_xattn_in['bk'], 'L1_xattn_wv': _L1_xattn_in['wv'], 'L1_xattn_bv': _L1_xattn_in['bv'], 'L1_xattn_wo': _L1_xattn_in['wo'], 'L1_xattn_bo': _L1_xattn_in['bo'], 'L1_ffn_router_w': _L1_ffn_in['router_w'], 'L1_ffn_router_bias': _L1_ffn_in['router_bias'], 'L1_ffn_gate_w': _L1_ffn_in['gate_w'], 'L1_ffn_up_w': _L1_ffn_in['up_w'], 'L1_ffn_down_w': _L1_ffn_in['down_w'], 'L1_ffn_s_gate_w': _L1_ffn_in['s_gate_w'], 'L1_ffn_s_up_w': _L1_ffn_in['s_up_w'], 'L1_ffn_s_down_w': _L1_ffn_in['s_down_w']}

def reference(x, ctx_768, mask_BxS_bf1, mask_BxS2_bf1, L0_xattn_Wq, L0_xattn_Wk, L0_xattn_Wv, L0_xattn_W_film_in, L0_xattn_b_film_in, L0_xattn_W_film_out, L0_xattn_b_film_out, L0_xattn_g_norm_in, L0_xattn_b_norm_in, L0_xattn_g_norm_out, L0_xattn_b_norm_out, L0_xattn_g_ffn, L0_xattn_b_ffn, L0_xattn_W1, L0_xattn_b1, L0_xattn_W2, L0_xattn_b2, L0_xattn_log_dt, L0_xattn_A_re, L0_xattn_A_im, L0_xattn_C_re, L0_xattn_C_im, L0_xattn_D_skip, L0_xattn_mod_gate, L0_ffn_q_nw, L0_ffn_q_nb, L0_ffn_q_w1, L0_ffn_q_b1, L0_ffn_q_w2, L0_ffn_q_b2, L0_ffn_k_nw, L0_ffn_k_nb, L0_ffn_k_w1, L0_ffn_k_b1, L0_ffn_k_w2, L0_ffn_k_b2, L0_ffn_v_nw, L0_ffn_v_nb, L0_ffn_v_w1, L0_ffn_v_b1, L0_ffn_v_w2, L0_ffn_v_b2, L0_ffn_f_nw, L0_ffn_f_nb, L0_ffn_f_w1, L0_ffn_f_b1, L0_ffn_f_w2, L0_ffn_f_b2, L1_xattn_wq, L1_xattn_bq, L1_xattn_wk, L1_xattn_bk, L1_xattn_wv, L1_xattn_bv, L1_xattn_wo, L1_xattn_bo, L1_ffn_router_w, L1_ffn_router_bias, L1_ffn_gate_w, L1_ffn_up_w, L1_ffn_down_w, L1_ffn_s_gate_w, L1_ffn_s_up_w, L1_ffn_s_down_w):
    import jax
    import jax.numpy as jnp

    def _L0_xattn_ref(x_text, x_vision, text_mask, vision_mask, Wq, Wk, Wv, W_film_in, b_film_in, W_film_out, b_film_out, g_norm_in, b_norm_in, g_norm_out, b_norm_out, g_ffn, b_ffn, W1, b1, W2, b2, log_dt, A_re, A_im, C_re, C_im, D_skip, mod_gate):
        import jax, jax.numpy as jnp
        import numpy as np
        B, T, DT, G, DV = (16, 128, 256, 144, 192)
        H, DH = (4, 32)
        INNER = H * DH
        HID = 4 * DT
        N_STATE = 64
        K_TOP = 32

        def layernorm(x, g, b, eps=1e-05):
            m = x.mean(-1, keepdims=True)
            v = x.var(-1, keepdims=True)
            return (x - m) * jax.lax.rsqrt(v + eps) * g + b

        def s4d(x, log_dt, A_re, A_im, C_re, C_im, D_skip):
            Bb, L, D = x.shape
            dt = jnp.exp(log_dt)
            A = A_re + 1j * A_im
            C = C_re + 1j * C_im
            dtA = dt[:, None] * A
            dC = C * (jnp.exp(dtA) - 1.0) / A
            powers = jnp.exp(dtA[:, :, None] * jnp.arange(L))
            K = 2.0 * jnp.einsum('dn,dnl->dl', dC, powers).real
            n = 2 * L
            Kf = jnp.fft.rfft(K, n=n, axis=-1)
            xf = jnp.fft.rfft(x, n=n, axis=1)
            y = jnp.fft.irfft(xf * Kf.T[None], n=n, axis=1)[:, :L]
            return y + x * D_skip
        Bb, Tt, D = x_text.shape
        Gg = x_vision.shape[1]
        Q = (x_text @ Wq).reshape(Bb, Tt, H, DH)
        K = (x_vision @ Wk).reshape(Bb, Gg, H, DH)
        scores = jnp.einsum('bthd,bghd->bhtg', Q, K) / np.sqrt(DH).astype(np.float32)
        scores = jnp.where(vision_mask[:, None, None, :], scores, -jnp.inf)
        topv, topi = jax.lax.top_k(scores, K_TOP)
        probs = jax.nn.softmax(topv, axis=-1)
        bi = jnp.arange(Bb)[:, None, None, None]
        hi = jnp.arange(H)[None, :, None, None]
        ti = jnp.arange(Tt)[None, None, :, None]
        attn = jnp.zeros_like(scores).at[bi, hi, ti, topi].set(probs)
        attn_mean = attn.mean(axis=1)
        V = x_vision @ Wv
        c_t = jnp.einsum('btg,bgd->btd', attn_mean, V)
        c_t = c_t * text_mask[..., None]
        x = layernorm(x_text, g_norm_in, b_norm_in)
        scale_in, shift_in = jnp.split(c_t @ W_film_in + b_film_in, 2, axis=-1)
        x = x * (1.0 + mod_gate * scale_in) + mod_gate * shift_in
        y = s4d(x, log_dt, A_re, A_im, C_re, C_im, D_skip)
        scale_out, shift_out = jnp.split(c_t @ W_film_out + b_film_out, 2, axis=-1)
        y = y * (1.0 + mod_gate * scale_out) + mod_gate * shift_out
        xt = x_text + y
        h = layernorm(xt, g_ffn, b_ffn)
        h = jax.nn.gelu(h @ W1 + b1, approximate=False) @ W2 + b2
        xt = xt + h
        return layernorm(xt, g_norm_out, b_norm_out)

    def _L0_ffn_ref(x, q_nw, q_nb, q_w1, q_b1, q_w2, q_b2, k_nw, k_nb, k_w1, k_b1, k_w2, k_b2, v_nw, v_nb, v_w1, v_b1, v_w2, v_b2, f_nw, f_nb, f_w1, f_b1, f_w2, f_b2):
        import jax, jax.numpy as jnp
        import numpy as np
        D = 256
        LW = 16
        DEPTH = 8
        NN = 2 ** DEPTH - 1
        NL = 2 ** DEPTH
        B, S = (2, 256)

        def _fff(x, nw, nb, w1, b1, w2, b2, act):
            node = jnp.zeros(x.shape[:2], dtype=jnp.int32)
            for _ in range(DEPTH):
                logit = jnp.einsum('bsd,bsd->bs', x, nw[node]) + nb[node]
                node = 2 * node + 1 + (logit > 0).astype(jnp.int32)
            leaf = node - NN
            h = act(jnp.einsum('bsd,bsdl->bsl', x, w1[leaf]) + b1[leaf])
            return jnp.einsum('bsl,bsld->bsd', h, w2[leaf]) + b2[leaf]

        def _forward(x, q_nw, q_nb, q_w1, q_b1, q_w2, q_b2, k_nw, k_nb, k_w1, k_b1, k_w2, k_b2, v_nw, v_nb, v_w1, v_b1, v_w2, v_b2, f_nw, f_nb, f_w1, f_b1, f_w2, f_b2):
            mu = jnp.mean(x, -1, keepdims=True)
            sd = jnp.std(x, -1, ddof=1, keepdims=True)
            xn = (x - mu) / jnp.sqrt(sd + 1e-05)
            relu = jax.nn.relu
            q = _fff(xn, q_nw, q_nb, q_w1, q_b1, q_w2, q_b2, relu)
            k = _fff(xn, k_nw, k_nb, k_w1, k_b1, k_w2, k_b2, relu)
            v = _fff(xn, v_nw, v_nb, v_w1, v_b1, v_w2, v_b2, relu)
            att = jax.nn.softmax(jnp.einsum('bqd,bkd->bqk', q, k) / jnp.sqrt(jnp.float32(D)), axis=-1)
            y = xn + jnp.einsum('bqk,bkd->bqd', att, v)
            gelu = lambda t: jax.nn.gelu(t, approximate=False)
            return y + _fff(y, f_nw, f_nb, f_w1, f_b1, f_w2, f_b2, gelu)

        def _make_fff_params(key, scale_in, scale_leaf):
            ks = jax.random.split(key, 4)
            nw = jax.random.normal(ks[0], (NN, D), jnp.float32) * scale_in
            nb = jnp.zeros((NN,), jnp.float32)
            w1 = jax.random.normal(ks[1], (NL, D, LW), jnp.float32) * scale_in
            b1 = jax.random.normal(ks[2], (NL, LW), jnp.float32) * 0.01
            w2 = jax.random.normal(ks[3], (NL, LW, D), jnp.float32) * scale_leaf
            b2 = jnp.zeros((NL, D), jnp.float32)
            return (nw, nb, w1, b1, w2, b2)
        return _forward(x, q_nw, q_nb, q_w1, q_b1, q_w2, q_b2, k_nw, k_nb, k_w1, k_b1, k_w2, k_b2, v_nw, v_nb, v_w1, v_b1, v_w2, v_b2, f_nw, f_nb, f_w1, f_b1, f_w2, f_b2)

    def _L1_xattn_ref(x, y, wq, bq, wk, bk, wv, bv, wo, bo):
        import jax, jax.numpy as jnp
        import numpy as np
        N_HEADS = 16
        DIM_EMBED = 256
        DIM_CROSS = 192
        DIM_HEAD = DIM_EMBED // N_HEADS
        B, Sq, E = x.shape
        H, D = (N_HEADS, DIM_HEAD)
        q = (x @ wq + bq).reshape(B, Sq, H, D).transpose(0, 2, 1, 3)
        k = (y @ wk + bk).reshape(B, -1, H, D).transpose(0, 2, 1, 3)
        v = (y @ wv + bv).reshape(B, -1, H, D).transpose(0, 2, 1, 3)
        scores = jnp.einsum('bhqd,bhkd->bhqk', q, k) / jnp.sqrt(jnp.asarray(D, x.dtype))
        attn = jax.nn.softmax(scores, axis=-1)
        out = jnp.einsum('bhqk,bhkd->bhqd', attn, v)
        out = out.transpose(0, 2, 1, 3).reshape(B, Sq, E)
        return out @ wo + bo

    def _L1_ffn_ref(hidden_states, router_w, router_bias, gate_w, up_w, down_w, s_gate_w, s_up_w, s_down_w):
        import jax, jax.numpy as jnp
        import numpy as np
        K = 4
        ROUTED_SCALING = 1.0
        NORM_TOPK = True

        def _gate(hidden_states, router_w, router_bias):
            logits = jnp.einsum('bsh,he->bse', hidden_states, router_w).astype(jnp.float32)
            scores = jax.nn.softmax(logits, axis=-1)
            corrected = scores + router_bias
            _, top_k_indices = jax.lax.top_k(corrected, K)
            top_k_weights = jnp.take_along_axis(scores, top_k_indices, axis=-1)
            if NORM_TOPK:
                top_k_weights = top_k_weights / (top_k_weights.sum(-1, keepdims=True) + 1e-20)
            top_k_weights = top_k_weights * ROUTED_SCALING
            return (top_k_weights.astype(hidden_states.dtype), top_k_indices)
        B, S, H = hidden_states.shape
        tk_w, tk_i = _gate(hidden_states, router_w, router_bias)
        hf = hidden_states.reshape(-1, H)
        tk_w = tk_w.reshape(-1, K)
        tk_i = tk_i.reshape(-1, K)
        gate_all = jnp.einsum('nh,ehi->nei', hf, gate_w)
        up_all = jnp.einsum('nh,ehi->nei', hf, up_w)
        act = jax.nn.silu(gate_all) * up_all
        down_all = jnp.einsum('nei,eih->neh', act, down_w)
        sel = jnp.take_along_axis(down_all, tk_i[:, :, None], axis=1)
        routed = (sel * tk_w[:, :, None]).sum(axis=1).reshape(B, S, H)
        g = jnp.einsum('bsh,hm->bsm', hidden_states, s_gate_w)
        u = jnp.einsum('bsh,hm->bsm', hidden_states, s_up_w)
        shared = jnp.einsum('bsm,mh->bsh', jax.nn.silu(g) * u, s_down_w)
        return routed + shared
    x = x + _L0_xattn_ref(_layernorm(x, axis=-1), ctx_768, mask_BxS_bf1, mask_BxS2_bf1, L0_xattn_Wq, L0_xattn_Wk, L0_xattn_Wv, L0_xattn_W_film_in, L0_xattn_b_film_in, L0_xattn_W_film_out, L0_xattn_b_film_out, L0_xattn_g_norm_in, L0_xattn_b_norm_in, L0_xattn_g_norm_out, L0_xattn_b_norm_out, L0_xattn_g_ffn, L0_xattn_b_ffn, L0_xattn_W1, L0_xattn_b1, L0_xattn_W2, L0_xattn_b2, L0_xattn_log_dt, L0_xattn_A_re, L0_xattn_A_im, L0_xattn_C_re, L0_xattn_C_im, L0_xattn_D_skip, L0_xattn_mod_gate)
    x = x + _L0_ffn_ref(_layernorm(x, axis=-1), L0_ffn_q_nw, L0_ffn_q_nb, L0_ffn_q_w1, L0_ffn_q_b1, L0_ffn_q_w2, L0_ffn_q_b2, L0_ffn_k_nw, L0_ffn_k_nb, L0_ffn_k_w1, L0_ffn_k_b1, L0_ffn_k_w2, L0_ffn_k_b2, L0_ffn_v_nw, L0_ffn_v_nb, L0_ffn_v_w1, L0_ffn_v_b1, L0_ffn_v_w2, L0_ffn_v_b2, L0_ffn_f_nw, L0_ffn_f_nb, L0_ffn_f_w1, L0_ffn_f_b1, L0_ffn_f_w2, L0_ffn_f_b2)
    x = x + _L1_xattn_ref(_layernorm(x, axis=-1), ctx_768, L1_xattn_wq, L1_xattn_bq, L1_xattn_wk, L1_xattn_bk, L1_xattn_wv, L1_xattn_bv, L1_xattn_wo, L1_xattn_bo)
    x = x + _L1_ffn_ref(_layernorm(x, axis=-1), L1_ffn_router_w, L1_ffn_router_bias, L1_ffn_gate_w, L1_ffn_up_w, L1_ffn_down_w, L1_ffn_s_gate_w, L1_ffn_s_up_w, L1_ffn_s_down_w)
    return x

_drawn_inputs = setup_inputs


def setup_inputs(seed=0):
    import zlib

    import numpy as np

    out = dict(_drawn_inputs(seed))
    spreads = {'L0_xattn_b_film_in': (0.0, 0.1),
     'L0_xattn_b_film_out': (0.0, 0.1),
     'L0_xattn_g_norm_in': (1.0, 0.2),
     'L0_xattn_b_norm_in': (0.0, 0.1),
     'L0_xattn_g_norm_out': (1.0, 0.2),
     'L0_xattn_b_norm_out': (0.0, 0.1),
     'L0_xattn_g_ffn': (1.0, 0.2),
     'L0_xattn_b_ffn': (0.0, 0.1),
     'L0_xattn_b1': (0.0, 0.1),
     'L0_xattn_b2': (0.0, 0.1),
     'L0_xattn_A_re': (-0.5, 0.2),
     'L0_ffn_q_nb': (0.0, 0.1),
     'L0_ffn_q_b2': (0.0, 0.273),
     'L0_ffn_k_nb': (0.0, 0.1),
     'L0_ffn_k_b2': (0.0, 0.1),
     'L0_ffn_v_nb': (0.0, 0.1),
     'L0_ffn_v_b2': (0.0, 0.1),
     'L0_ffn_f_nb': (0.0, 0.1),
     'L0_ffn_f_b2': (0.0, 0.1)}
    factors = {'L0_ffn_q_b1': 16.651,
     'L0_ffn_k_b1': 8.0,
     'L0_ffn_v_b1': 4.566,
     'L0_ffn_f_b1': 8.0,
     'L1_xattn_bq': 52.041,
     'L1_xattn_bk': 64.0,
     'L1_xattn_bv': 8.0,
     'L1_xattn_bo': 8.0,
     'L1_ffn_router_w': 8.0,
     'L1_ffn_gate_w': 8.0,
     'L1_ffn_up_w': 8.0,
     'L1_ffn_down_w': 8.0,
     'L1_ffn_s_gate_w': 7.139,
     'L1_ffn_s_up_w': 6.976,
     'L1_ffn_s_down_w': 7.014}
    for name, (base, spread) in spreads.items():
        noise = np.random.default_rng([zlib.crc32(name.encode()), seed]).standard_normal(out[name].shape)
        drawn = base * np.exp(spread * noise) if base else spread * noise
        out[name] = jnp.asarray(drawn.astype(out[name].dtype))
    for name, factor in factors.items():
        out[name] = (out[name] * factor).astype(out[name].dtype)
    return out
```

```python
from contextlib import ExitStack

import numpy as np

import concourse.bass as bass
from concourse import mybir

ALU = mybir.AluOpType
ACT = mybir.ActivationFunctionType
AX_X = mybir.AxisListType.X
F32 = mybir.dt.float32
BF16 = mybir.dt.bfloat16
I32 = mybir.dt.int32
U8 = mybir.dt.uint8

P = 128
B = 8
S = 256
D = 256
DCTX = 192
CP = DCTX // 2
ST = S // P
DC = D // P
NT = B * ST
H0, DH0, TOPK = 4, 32, 32
HID = 4 * D
HC = HID // P
NSTATE = 64
NA, NCP = 32, 8
NEG_MASK = -1e30
NEG_TAKEN = -3e38
EPS = 1e-5
NN, NL, LW, DEPTH = 255, 256, 16, 8
FH = NL * LW
FC = FH // P
H1, DH1 = 16, 16
NE, EI, TOPE = 8, 128, 4
SI = 512

LOG2E = 1.4426950408889634
LN2_HI, LN2_LO = 0.693145751953125, 1.42860682030941723e-6
ROUND = 12582912.0
INV_2PI = 0.15915494309189535
PI2_A, PI2_B = 6.28125, 0.0019340515136718750
PI2_C = 6.283185307179586 - PI2_A - PI2_B


class Signal:

    def __init__(self, handle, per=1):
        self.s = handle
        self.per = per


def reached(eng, signal, i, k=None):
    eng.wait_ge(signal.s, i * signal.per + (signal.per if k is None else k))


def reached_apart(eng, signal, i, k=None):
    wait_apart(eng, signal.s, i * signal.per + (signal.per if k is None else k))


def released(eng, signal, i):
    eng.wait_ge(signal.s, i * signal.per)


def wait_apart(eng, handle, value):
    eng.to_reg(value)
    eng.wait_ge(handle, 1)
    eng.wait_ge(handle, value)


class Chain:

    def __init__(self, eng, handle, turn=0, per=0):
        self.eng, self.s, self.base, self.per, self.n = eng, handle, turn * per, per, 0

    def mark(self, ins):
        self.n += 1
        ins.then_inc(self.s, 1)
        return self.n

    def wait(self, n=None):
        self.eng.wait_ge(self.s, self.base + (self.n if n is None else n))

    def __call__(self, ins):
        self.mark(ins)
        self.wait()

    def wait_apart(self):
        wait_apart(self.eng, self.s, self.base + self.n)

    def end(self):
        assert self.n == self.per, f"the turn has {self.n} steps"
GL = 16
NG = NL // GL
GH = GL * LW
TMAX = (B * S + NG * (P - 1)) // P
TILES = TMAX + -TMAX % 4
PLACES = TILES * P
W1COLS = DC * GH + GH // P
XW = D + GL
ZERO_FILLS = 4


class Core:

    def __init__(self, nc, ctx, dram):
        self.nc, self.ctx, self.dram, self.own = nc, ctx, dram, []
        self.x = self.sb(ctx, "x_tokens", [P, NT, D])
        self.ctxT = self.sb(ctx, "ctx_T", [CP, 2, B * S])
        self.ident = self.sb(ctx, "identity", [P, P])
        self.ones = self.sb(ctx, "ones_row", [P, P])
        self.ones_bf = self.sb(ctx, "ones_row_bf16", [P, P], BF16)
        self.minus_half = self.sb(ctx, "minus_half", [P, ST])
        self.plus_half = self.sb(ctx, "plus_half", [P, ST])
        self.loads = [self.sem("x_loaded"), self.sem("ctx_loaded")]
        self.setup = self.sem("constants_set")
        self.zeroed = self.sem("places_zeroed")
        self.sorted_x = {f: nc.dram_tensor(f"sorted_x_{f}", (PLACES, XW), F32, kind="Internal").ap()
                         for f in "qkvf"}
        self.sorted_y = {f: nc.dram_tensor(f"sorted_y_{f}", (PLACES, D), F32, kind="Internal").ap()
                         for f in "qkvf"}
        self.zero = self.sb(ctx, "zero_row", [P, XW])

    def sb(self, ctx, name, shape, dt=F32):
        return ctx.enter_context(self.nc.sbuf_tensor(name, shape, dt))

    def ps(self, ctx, name, shape, dt=F32):
        return ctx.enter_context(self.nc.psum_tensor(name, shape, dt))

    def sem(self, name):
        handle = self.nc.alloc_semaphore(name=name)
        self.own.append(handle)
        return handle

    def phase(self, stage, *args, **kwargs):
        self.own = []
        stage(self, *args, **kwargs)
        self.nc.clear_and_free_semaphores(self.own)
        self.nc.all_engine_barrier()

    def flag(self, name, per=1):
        return Signal(self.sem(name), per)


def row(ap):
    return ap.rearrange("(a n) -> a n", a=1)


def rstd_of(pool, steps, out, var, minus_half):
    steps(pool.tensor_scalar(out, var, EPS, None, ALU.add))
    return pool.tensor_tensor(out, out, minus_half, ALU.pow)


def spectrum(core, ctx, kr, ki):
    nc, dram = core.nc, core.dram
    with ExitStack() as own:
        HD = D // 2
        logdt = core.sb(own, "s4_logdt", [P, HD])
        are = core.sb(own, "s4_A_re", [P, HD])
        aim = core.sb(own, "s4_A_im", [P, HD])
        cre = core.sb(own, "s4_C_re", [P, HD])
        cim = core.sb(own, "s4_C_im", [P, HD])
        dskip = core.sb(own, "s4_D_skip", [1, D])
        kdft = core.sb(own, "s4_kernel_dft", [NA, NCP, 2, S])
        tmp = [core.sb(own, f"s4_t{n}", [P, HD]) for n in range(8)]
        tint = core.sb(own, "s4_int", [P, HD], I32)
        dt = core.sb(own, "s4_dt", [P, HD])
        ea = core.sb(own, "s4_exp_a", [P, HD])
        em1 = core.sb(own, "s4_expm1_a", [P, HD])
        s_half = core.sb(own, "s4_sin_half", [P, HD])
        s_quart = core.sb(own, "s4_sin_quarter", [P, HD])
        bhalf = core.sb(own, "s4_b_half", [P, HD])
        dcr = core.sb(own, "s4_dC_re", [P, HD])
        dci = core.sb(own, "s4_dC_im", [P, HD])
        zr = core.sb(own, "s4_Z_re", [P, NCP, HD])
        zi = core.sb(own, "s4_Z_im", [P, NCP, HD])
        gr = core.sb(own, "s4_G_re", [P, NCP, HD])
        gi = core.sb(own, "s4_minus_G_im", [P, NCP, HD])
        wr = core.sb(own, "s4_W_re", [P, NA, HD])
        wi = core.sb(own, "s4_W_im", [P, NA, HD])
        sq = [core.sb(own, f"s4_square{n}", [P, 2, HD]) for n in range(2)]
        part = [core.sb(own, f"s4_product{n}", [P, NA // 2, HD]) for n in range(2)]
        ksb = core.sb(own, "s4_K", [NA, D, NCP])
        pk = core.ps(own, "s4_K_ps", [NA, 2, HD * NCP])
        pf = core.ps(own, "s4_spectrum_ps", [P, 2, 2 * S])
        zero = core.zero
        loaded, chain = core.sem("s4_loaded"), core.sem("s4_steps")
        asked, given = core.sem("s4_act_asked"), core.sem("s4_act_given")
        tables, kdone, kevac, fdone = (core.sem(f"s4_{n}") for n in ("tables", "k", "k_evac", "f"))

        with nc.Block() as block:
            @block.sync
            def _(sp):
                for h in range(2):
                    sp.dma_start(logdt[64 * h:64 * h + 64, :],
                                 dram["L0_xattn_log_dt"][h * HD:(h + 1) * HD]
                                 .partition_broadcast(64)).then_inc(loaded, 16)
                for t, name in ((are, "A_reT"), (aim, "A_imT"), (cre, "C_reT"), (cim, "C_imT")):
                    sp.dma_start(t[:], dram[name]).then_inc(loaded, 16)
                sp.dma_start(dskip[:], row(dram["L0_xattn_D_skip"])).then_inc(loaded, 16)
                sp.dma_start(kdft[:], dram["kernel_dft"]).then_inc(loaded, 16)
                sp.dma_start(core.x[:], dram["x"].rearrange("b (t p) d -> p (b t) d", p=P)
                             ).then_inc(core.loads[0], 16)
                for c in range(2):
                    sp.dma_start(core.ctxT[:, c, :].rearrange("p (b s) -> p b s", b=B),
                                 dram["ctxT"][:, c * CP:(c + 1) * CP, :].rearrange("b p s -> p b s")
                                 ).then_inc(core.loads[1], 16)

                sp.wait_ge(core.setup, 6)
                for t in core.sorted_x.values():
                    sp.dma_start(t.rearrange("(p r) c -> p r c", p=P),
                                 zero[:].unsqueeze(1).to_broadcast([P, TILES, XW])
                                 ).then_inc(core.zeroed, 16)

            @block.gpsimd
            def _(pool):
                pool.memset(zero[:], 0.0).then_inc(core.setup, 1)
                pool.memset(core.ident[:], 0.0).then_inc(core.setup, 1)
                pool.memset(core.ones[:], 1.0).then_inc(core.setup, 1)
                pool.memset(core.ones_bf[:], 1.0).then_inc(core.setup, 1)
                pool.memset(core.minus_half[:], -0.5).then_inc(core.setup, 1)
                pool.memset(core.plus_half[:], 0.5).then_inc(core.setup, 1)
                pool.wait_ge(core.setup, 6)
                pool.affine_select(out=core.ident[:], in_=core.ident[:], compare_op=ALU.not_equal,
                                   fill=1.0, base=0, pattern=[[-1, P]], channel_multiplier=1
                                   ).then_inc(core.setup, 1)

            @block.scalar
            def _(act):
                act.wait_ge(asked, 1)
                act.activation(em1[:], tmp[6][:], ACT.Tanh, scale=0.5).then_inc(given, 1)
                act.wait_ge(asked, 2)
                act.activation(s_half[:], bhalf[:], ACT.Sin).then_inc(given, 1)
                act.activation(s_quart[:], bhalf[:], ACT.Sin, scale=0.5).then_inc(given, 1)

            @block.vector
            def _(dve):
                do = Chain(dve, chain)

                def exp(out, x):
                    c, n, r, p = (t[:] for t in tmp[:4])
                    do(dve.tensor_scalar(c, x, -87.0, 88.0, ALU.max, ALU.min))
                    do(dve.tensor_scalar(n, c, LOG2E, ROUND, ALU.mult, ALU.add))
                    do(dve.tensor_scalar(n, n, ROUND, None, ALU.subtract))
                    do(dve.scalar_tensor_tensor(r, n, -LN2_HI, c, ALU.mult, ALU.add))
                    do(dve.scalar_tensor_tensor(r, n, -LN2_LO, r, ALU.mult, ALU.add))
                    do(dve.tensor_scalar(p, r, 1 / 5040, 1 / 720, ALU.mult, ALU.add))
                    for k in (1 / 120, 1 / 24, 1 / 6, 0.5, 1.0, 1.0):
                        do(dve.tensor_tensor(p, p, r, ALU.mult))
                        do(dve.tensor_scalar(p, p, k, None, ALU.add))
                    do(dve.tensor_scalar(tint[:], n, 127.0, float(1 << 23), ALU.add, ALU.mult))
                    do(dve.tensor_tensor(out, p, tint[:].bitcast(F32), ALU.mult))

                def cmul(outr, outi, ar, ai, br, bi, t0, t1):
                    do(dve.tensor_tensor(t0, ar, br, ALU.mult))
                    do(dve.tensor_tensor(t1, ai, bi, ALU.mult))
                    do(dve.tensor_tensor(outr, t0, t1, ALU.subtract))
                    do(dve.tensor_tensor(t0, ar, bi, ALU.mult))
                    do(dve.tensor_tensor(t1, ai, br, ALU.mult))
                    do(dve.tensor_tensor(outi, t0, t1, ALU.add))

                dve.wait_ge(loaded, 16 * 8)
                exp(dt[:], logdt[:])
                a, b = tmp[6][:], tmp[7][:]
                do(dve.tensor_tensor(a, dt[:], are[:], ALU.mult))
                dve.tensor_tensor(b, dt[:], aim[:], ALU.mult).then_inc(asked, 1)
                dve.wait_ge(asked, 1)
                exp(ea[:], a)
                n, r = tmp[0][:], bhalf[:]
                do(dve.tensor_scalar(b, b, 0.5, None, ALU.mult))
                do(dve.tensor_scalar(n, b, INV_2PI, ROUND, ALU.mult, ALU.add))
                do(dve.tensor_scalar(n, n, ROUND, None, ALU.subtract))
                do(dve.scalar_tensor_tensor(r, n, -PI2_A, b, ALU.mult, ALU.add))
                do(dve.scalar_tensor_tensor(r, n, -PI2_B, r, ALU.mult, ALU.add))
                do(dve.scalar_tensor_tensor(r, n, -PI2_C, r, ALU.mult, ALU.add))
                dve.tensor_scalar(r, r, 3.1415925, -3.1415925, ALU.min, ALU.max).then_inc(asked, 1)
                dve.wait_ge(given, 3)
                do(dve.scalar_tensor_tensor(em1[:], ea[:], 1.0, em1[:], ALU.add, ALU.mult))
                sh, sq_, cm1, cosb, sinb, er, ei, den = (t[:] for t in tmp)
                do(dve.tensor_tensor(sq_, s_quart[:], s_quart[:], ALU.mult))
                do(dve.tensor_scalar(sh, sq_, -2.0, 1.0, ALU.mult, ALU.add))
                do(dve.scalar_tensor_tensor(sinb, s_half[:], 2.0, sh, ALU.mult, ALU.mult))
                do(dve.scalar_tensor_tensor(cm1, s_half[:], -2.0, s_half[:], ALU.mult, ALU.mult))
                do(dve.tensor_scalar(cosb, cm1, 1.0, None, ALU.add))
                do(dve.tensor_tensor(zr[:, 1, :], ea[:], cosb, ALU.mult))
                do(dve.tensor_tensor(zi[:, 1, :], ea[:], sinb, ALU.mult))
                do(dve.tensor_tensor(er, em1[:], cosb, ALU.mult))
                do(dve.tensor_tensor(er, er, cm1, ALU.add))
                do(dve.tensor_tensor(den, are[:], are[:], ALU.mult))
                do(dve.tensor_tensor(sh, aim[:], aim[:], ALU.mult))
                do(dve.tensor_tensor(den, den, sh, ALU.add))
                do(dve.reciprocal(den, den))
                do(dve.tensor_tensor(sh, er, are[:], ALU.mult))
                do(dve.tensor_tensor(sq_, zi[:, 1, :], aim[:], ALU.mult))
                do(dve.tensor_tensor(sh, sh, sq_, ALU.add))
                do(dve.tensor_tensor(ei, zi[:, 1, :], are[:], ALU.mult))
                do(dve.tensor_tensor(sq_, er, aim[:], ALU.mult))
                do(dve.tensor_tensor(ei, ei, sq_, ALU.subtract))
                do(dve.tensor_tensor(er, sh, den, ALU.mult))
                do(dve.tensor_tensor(ei, ei, den, ALU.mult))
                cmul(dcr[:], dci[:], cre[:], cim[:], er, ei, sh, sq_)

                def powers(tr, ti, count, base):
                    br, bi = base
                    have, cur = 1, 0
                    while have < count:
                        s = sq[cur]
                        if have == 1:
                            do(dve.tensor_copy(tr[:, 1, :], br))
                            do(dve.tensor_copy(ti[:, 1, :], bi))
                            br, bi = tr[:, 1, :], ti[:, 1, :]
                        else:
                            wide = [P, have, HD]
                            cmul(tr[:, have:2 * have, :], ti[:, have:2 * have, :],
                                 tr[:, 0:have, :], ti[:, 0:have, :],
                                 br.unsqueeze(1).to_broadcast(wide),
                                 bi.unsqueeze(1).to_broadcast(wide),
                                 part[0][:, 0:have, :], part[1][:, 0:have, :])
                        have *= 2
                        cmul(s[:, 0, :], s[:, 1, :], br, bi, br, bi, sh, sq_)
                        br, bi = s[:, 0, :], s[:, 1, :]
                        cur = 1 - cur
                    return br, bi

                for t in (zr, wr):
                    do(dve.memset(t[:, 0, :], 1.0))
                for t in (zi, wi):
                    do(dve.memset(t[:, 0, :], 0.0))
                do(dve.tensor_copy(cosb, zr[:, 1, :]))
                do(dve.tensor_copy(sinb, zi[:, 1, :]))
                z8 = powers(zr, zi, NCP, (cosb, sinb))
                wide = [P, NCP, HD]
                t0, t1 = part[0][:, 0:NCP, :], part[1][:, 0:NCP, :]
                cr, ci = (t[:].unsqueeze(1).to_broadcast(wide) for t in (dcr, dci))
                cmul(gr[:], gi[:], zr[:], zi[:], cr, ci, t0, t1)
                do(dve.tensor_scalar(gi[:], gi[:], -1.0, None, ALU.mult))
                do(dve.tensor_copy(cosb, z8[0]))
                do(dve.tensor_copy(sinb, z8[1]))
                powers(wr, wi, NA, (cosb, sinb))
                dve.tensor_copy(sh, sq_).then_inc(tables, 1)
                dve.wait_ge(kdone, 1)
                for h in range(2):
                    do(dve.tensor_copy(ksb[:, h * HD:(h + 1) * HD, :],
                                       pk[:, h, :].rearrange("a (d c) -> a d c", c=NCP)))
                k0 = ksb[0:1, :, 0]
                dve.scalar_tensor_tensor(k0, dskip[:], 0.5, k0, ALU.mult, ALU.add
                                         ).then_inc(kevac, 1)
                dve.wait_ge(fdone, 1)
                do(dve.tensor_copy(kr[:].rearrange("p k d -> p (k d)"), pf[:, 0, :]))
                do(dve.tensor_copy(ki[:].rearrange("p k d -> p (k d)"), pf[:, 1, :]))

            @block.tensor
            def _(pe):
                pe.wait_ge(tables, 1)
                for d in range(HD):
                    for h in range(2):
                        q = slice(64 * h, 64 * h + 64)
                        o = pk[:, h, d * NCP:(d + 1) * NCP]
                        pe.matmul(o, wr[q, :, d], gr[q, :, d], start=True, stop=False)
                        last = pe.matmul(o, wi[q, :, d], gi[q, :, d], start=False, stop=True)
                last.then_inc(kdone, 1)
                pe.wait_ge(kevac, 1)
                for comp in range(2):
                    for kc in range(2):
                        for c in range(NCP):
                            last = pe.matmul(pf[:, comp, kc * D:(kc + 1) * D],
                                             kdft[:, c, comp, kc * P:(kc + 1) * P], ksb[:, :, c],
                                             start=(c == 0), stop=(c == NCP - 1))
                last.then_inc(fdone, 1)


def first_attention(core, ctx, kr, ki):
    nc, dram = core.nc, core.dram
    with ExitStack() as own:
        def sb(name, shape, dt=F32):
            return core.sb(own, "a_" + name, shape, dt)

        wq = sb("wq", [P, DC, P])
        wk = sb("wk", [CP, 2, P])
        wv = sb("wv", [CP, 2, D])
        film = [sb("film_in", [P, DC, 2 * D]), sb("film_out", [P, DC, 2 * D])]
        film_b = [sb("film_in_b", [P, 2 * D]), sb("film_out_b", [P, 2 * D])]
        gate = sb("mod_gate", [P, 1])
        g_in, b_in = sb("g_in", [P, D]), sb("b_in", [P, D])
        g_out, b_out = sb("g_out", [P, D]), sb("b_out", [P, D])
        g_ffn, b_ffn = sb("g_ffn", [P, DC]), sb("b_ffn", [P, DC])
        w1, b1 = sb("w1", [P, DC, HID]), sb("b1", [P, HC])
        w2, b2 = sb("w2", [P, HC, D]), sb("b2", [P, D])
        dft, idft = sb("dft", [P, ST, 2, S]), sb("idft", [P, 2, 2, S])
        vmask8, vmask = sb("vmask8", [P, B * S], U8), sb("vmask", [P, B * S], BF16)
        tmask8, tmask = sb("tmask8", [P, NT], U8), sb("tmask", [P, NT])
        xw, ctxw = sb("x", [P, ST, D]), sb("ctx", [CP, 2, S])
        maskw = sb("mask", [P, S], BF16)
        st, mv = sb("stats", [P, ST, 6]), sb("mean_var", [P, 4, ST, 2])
        rstd = sb("rstd", [P, 4, ST])
        xn, xnT = sb("xn", [P, ST, D]), sb("xnT", [P, DC, S])
        u = sb("u", [P, ST, D])
        qk = sb("qk", [P, 2, S])
        v = sb("v", [P, ST, D])
        score = sb("score", [P, H0 * ST, S])
        rest = sb("rest", [P, H0 * ST, S])
        top = sb("top", [P, H0 * ST, TOPK])
        nmax = sb("nmax", [P, H0 * ST])
        prob, prob_rest = sb("prob", [P, H0 * ST, S]), sb("prob_rest", [P, H0 * ST, S])
        etop, esum = sb("etop", [P, TOPK]), sb("esum", [P, H0 * ST])
        diag = sb("diag", [P, H0 * ST, P])
        attnT, ctT = sb("attnT", [P, ST, S]), sb("ctT", [P, DC, S])
        f_in, f_out = sb("f_in", [P, ST, 2 * D]), sb("f_out", [P, ST, 2 * D])
        x1 = sb("x1", [P, ST, D])
        spec = sb("spec", [P, 2, 2 * S])
        prod = sb("prod", [P, 4, 2 * S])
        yspec = sb("yspec", [P, 2, 2 * S])
        xt = sb("xt", [P, ST, D])
        hT = sb("hT", [P, DC, S])
        act1 = sb("act1", [P, HC, S])
        pS = core.ps(own, "a_scores", [P, H0, ST, S])
        pT = core.ps(own, "a_psT", [P, DC, S])
        pA = core.ps(own, "a_psA", [P, 2, S])
        pB = core.ps(own, "a_psB", [P, 2 * D])
        pC = core.ps(own, "a_psC", [P, 2 * D])

        loaded = core.sem("a_loaded")
        ready = core.sem("a_ready")
        sig = core.flag
        x_in, ctx_in = sig("a_x_in"), sig("a_ctx_in", 2)
        var, rs = sig("a_var", 4), sig("a_rstd", 4)
        norm, u_ready = sig("a_norm"), sig("a_u")
        t_ps, t_sb = sig("a_T_ps", 2), sig("a_T_sb", 2)
        proj_ps, proj_sb = sig("a_proj_ps", 2), sig("a_proj_sb", 2)
        scores = sig("a_scores_ready")
        score_sb = sig("a_scores_sb")
        first8, taken = sig("a_max_ready"), sig("a_taken")
        exps, exps_rest, sums = sig("a_exps"), sig("a_exps_rest"), sig("a_sums")
        weights, diags, probs = sig("a_weights"), sig("a_diags"), sig("a_probs")
        at_ps, at_sb = sig("a_at_ps"), sig("a_at_sb")
        ct_ps, ct_sb = sig("a_ct_ps"), sig("a_ct_sb")
        film_ps, film_sb = sig("a_film_ps", 4), sig("a_film_sb", 4)
        x1_ready = sig("a_x1")
        spec_ps, spec_sb = sig("a_spec_ps"), sig("a_spec_sb")
        yi_ready, yr_ready = sig("a_yi"), sig("a_yr")
        y_ps, xt_pre, xt_ready = sig("a_y_ps"), sig("a_xt_pre"), sig("a_xt")
        h_norm, resid = sig("a_h_norm"), sig("a_resid")
        u_ps, u_act = sig("a_up_ps", HC), sig("a_up_act", HC)
        dn_ps, done = sig("a_down_ps"), sig("a_done")
        dchain, pchain = core.sem("a_dve"), core.sem("a_pool")
        DVE_STEPS, POOL_STEPS = 73, 8
        N_LOADS = 22

        with nc.Block() as block:
            @block.sync
            def _(sp):
                def load(out, in_):
                    sp.dma_start(out, in_).then_inc(loaded, 16)

                def split(name, p=P):
                    return dram["L0_xattn_" + name].rearrange("(c p) n -> p c n", p=p)

                def spread(name, n=P):
                    return dram["L0_xattn_" + name].partition_broadcast(n)

                load(wq[:], split("Wq"))
                load(wk[:], split("Wk", CP))
                load(wv[:], split("Wv", CP))
                load(vmask8[:], dram["mask_BxS2_bf1"].rearrange("b s -> (b s)")
                     .partition_broadcast(P))
                load(tmask8[:], dram["mask_BxS_bf1"])
                load(gate[:], spread("mod_gate"))
                for n, name in enumerate(("W_film_in", "W_film_out")):
                    load(film[n][:], split(name))
                for n, name in enumerate(("b_film_in", "b_film_out")):
                    load(film_b[n][:], spread(name))
                for t, name in ((g_in, "g_norm_in"), (b_in, "b_norm_in"), (g_out, "g_norm_out"),
                                (b_out, "b_norm_out"), (b2, "b2")):
                    load(t[:], spread(name))
                load(dft[:], dram["dft"])
                load(idft[:], dram["idft"])
                for t, name in ((g_ffn, "g_ffn"), (b_ffn, "b_ffn"), (b1, "b1")):
                    load(t[:], dram["L0_xattn_" + name])
                load(w1[:], split("W1"))
                load(w2[:], split("W2"))

            @block.gpsimd
            def _(pool):
                pool.wait_ge(core.setup, 7)
                pool.wait_ge(core.loads[1], 32)
                pool.wait_ge(ready, 6)
                pool.wait_ge(loaded, 16 * (N_LOADS))
                with pool.Fori(0, B) as i:
                    do = Chain(pool, pchain, i, POOL_STEPS)
                    released(pool, proj_ps, i)
                    released(pool, scores, i)
                    pool.tensor_copy(maskw[:], vmask[:, bass.ds(i * S, S)]).then_inc(ctx_in.s, 1)
                    pool.tensor_copy(ctxw[:], core.ctxT[:, :, bass.ds(i * S, S)]
                                     ).then_inc(ctx_in.s, 1)
                    for n in range(2):
                        reached_apart(pool, var, i, n + 1)
                        rstd_of(pool, do, rstd[:, n, :], mv[:, n, :, 1], core.minus_half[:]
                                ).then_inc(rs.s, 1)
                    reached(pool, norm, i)
                    wide = [P, ST, D]
                    do(pool.tensor_tensor(u[:], u[:], g_in[:].unsqueeze(1).to_broadcast(wide),
                                          ALU.mult))
                    pool.tensor_tensor(u[:], u[:], b_in[:].unsqueeze(1).to_broadcast(wide),
                                       ALU.add).then_inc(u_ready.s, 1)
                    reached(pool, exps, i)
                    reached(pool, exps_rest, i)
                    pool.tensor_tensor(prob[:], prob[:], prob_rest[:], ALU.subtract
                                       ).then_inc(probs.s, 1)
                    reached(pool, weights, i)
                    wide = [P, H0 * ST, P]
                    pool.tensor_tensor(diag[:], core.ident[:].unsqueeze(1).to_broadcast(wide),
                                       esum[:].unsqueeze(2).to_broadcast(wide), ALU.mult
                                       ).then_inc(diags.s, 1)
                    reached(pool, spec_sb, i)
                    k_re = kr[:].rearrange("p k d -> p (k d)")
                    k_im = ki[:].rearrange("p k d -> p (k d)")
                    do(pool.tensor_tensor(prod[:, 2, :], spec[:, 0, :], k_im, ALU.mult))
                    do(pool.tensor_tensor(prod[:, 3, :], spec[:, 1, :], k_re, ALU.mult))
                    released(pool, y_ps, i)
                    pool.tensor_tensor(yspec[:, 1, :], prod[:, 2, :], prod[:, 3, :], ALU.add
                                       ).then_inc(yi_ready.s, 1)
                    reached(pool, film_sb, i)
                    pool.tensor_tensor(f_out[:, :, D:2 * D], f_out[:, :, D:2 * D], xn[:], ALU.add
                                       ).then_inc(xt_pre.s, 1)
                    reached_apart(pool, var, i, 3)
                    rstd_of(pool, do, rstd[:, 2, :], mv[:, 2, :, 1], core.minus_half[:]
                            ).then_inc(rs.s, 1)
                    reached(pool, xt_ready, i)
                    reached(pool, x1_ready, i)
                    do(pool.tensor_tensor(u[:], xt[:], b2[:].unsqueeze(1).to_broadcast([P, ST, D]),
                                          ALU.add))
                    pool.tensor_tensor(xw[:], xw[:], b_out[:].unsqueeze(1).to_broadcast([P, ST, D]),
                                       ALU.add).then_inc(resid.s, 1)
                    reached_apart(pool, var, i, 4)
                    rstd_of(pool, do, rstd[:, 3, :], mv[:, 3, :, 1], core.minus_half[:]
                            ).then_inc(rs.s, 1)
                    do.end()

            @block.scalar
            def _(act):
                act.wait_ge(core.loads[0], 16)
                act.wait_ge(loaded, 16 * (N_LOADS))
                with act.Fori(0, B) as i:
                    released(act, done, i)
                    act.activation(xw[:], core.x[:, bass.ds(i * ST, ST), :], ACT.Copy
                                   ).then_inc(x_in.s, 1)
                    reached(act, t_ps, i, 1)
                    act.activation(xnT[:], pT[:], ACT.Copy).then_inc(t_sb.s, 1)
                    reached(act, proj_ps, i, 1)
                    act.activation(qk[:], pA[:], ACT.Copy).then_inc(proj_sb.s, 1)
                    reached(act, proj_ps, i, 2)
                    act.activation(v[:].rearrange("p g d -> p (g d)"), pB[:], ACT.Copy
                                   ).then_inc(proj_sb.s, 1)
                    reached(act, scores, i)
                    act.activation(score[:].rearrange("p (h t) s -> p h t s", h=H0), pS[:],
                                   ACT.Copy).then_inc(score_sb.s, 1)
                    reached(act, first8, i)
                    scale = float(DH0) ** -0.5
                    for j in range(H0 * ST):
                        last = act.activation(prob[:, j, :], score[:, j, :], ACT.Exp,
                                              bias=nmax[:, j:j + 1], scale=scale)
                    last.then_inc(exps.s, 1)
                    reached(act, taken, i)
                    for j in range(H0 * ST):
                        last = act.activation(prob_rest[:, j, :], rest[:, j, :], ACT.Exp,
                                              bias=nmax[:, j:j + 1], scale=scale)
                    last.then_inc(exps_rest.s, 1)
                    for j in range(H0 * ST):
                        last = act.activation(act1[:, 0, TOPK * j:TOPK * (j + 1)], top[:, j, :], ACT.Exp,
                                              bias=nmax[:, j:j + 1], scale=scale,
                                              accum_out=esum[:, j:j + 1])
                    last.then_inc(sums.s, 1)
                    reached(act, at_ps, i)
                    act.activation(attnT[:].rearrange("p g t -> p (g t)"), pC[:], ACT.Copy
                                   ).then_inc(at_sb.s, 1)
                    reached(act, ct_ps, i)
                    act.activation(ctT[:], pT[:], ACT.Copy).then_inc(ct_sb.s, 1)
                    reached(act, spec_ps, i)
                    act.activation(spec[:, 0, :], pA[:].rearrange("p a b -> p (a b)"), ACT.Copy)
                    act.activation(spec[:, 1, :], pB[:], ACT.Copy).then_inc(spec_sb.s, 1)
                    reached(act, t_ps, i, 2)
                    for c in range(DC):
                        last = act.activation(hT[:, c, :], pT[:, c, :], ACT.Identity,
                                              bias=b_ffn[:, c:c + 1], scale=g_ffn[:, c:c + 1])
                    last.then_inc(t_sb.s, 1)
                    for c in range(HC):
                        reached(act, u_ps, i, c // 2 * 2 + 2)
                        act.activation(act1[:, c, :], pS[:, c // 2, c % 2, :], ACT.Gelu,
                                       bias=b1[:, c:c + 1]).then_inc(u_act.s, 1)

            @block.vector
            def _(dve):
                dve.wait_ge(loaded, 16 * (N_LOADS))
                n = Chain(dve, ready)
                n(dve.tensor_scalar(vmask[:], vmask8[:], -NEG_MASK, NEG_MASK, ALU.mult, ALU.add))
                n(dve.tensor_scalar(tmask[:], tmask8[:], 1.0 / H0, None, ALU.mult))
                for f in film_b:
                    n(dve.tensor_scalar(f[:, 0:D], f[:, 0:D], gate[:, 0:1], 1.0, ALU.mult, ALU.add))
                    n(dve.tensor_scalar(f[:, D:], f[:, D:], gate[:, 0:1], None, ALU.mult))
                with dve.Fori(0, B) as i:
                    do = Chain(dve, dchain, i, DVE_STEPS)

                    def stats(n, src):
                        for t in range(ST):
                            do.mark(dve.bn_stats(st[:, t, :], src[:, t, :]))
                        do.wait_apart()
                        for t in range(ST):
                            last = dve.bn_aggr(mv[:, n, t, :], st[:, t, :])
                        last.then_inc(var.s, 1)

                    def normal(n, dst, src):
                        reached(dve, var, i, n + 1)
                        reached(dve, rs, i, n + 1)
                        for t in range(ST):
                            last = dve.tensor_scalar(dst[:, t, :], src[:, t, :],
                                                     mv[:, n, t, 0:1], rstd[:, n, t:t + 1],
                                                     ALU.subtract, ALU.mult)
                        return last

                    reached(dve, x_in, i)
                    stats(0, xw)
                    released(dve, t_ps, i)
                    do(normal(0, xn, xw))
                    stats(1, xn)
                    normal(1, u, xn).then_inc(norm.s, 1)
                    reached_apart(dve, score_sb, i)
                    R = H0 * ST
                    for r in range(TOPK // 8):
                        for j in range(R):
                            src = score[:, j, :] if r == 0 else rest[:, j, :]
                            do.mark(dve.max(top[:, j, 8 * r:8 * r + 8], src))
                        do.wait_apart()
                        if r == 0:
                            dve.tensor_scalar(nmax[:], top[:, :, 0], -float(DH0) ** -0.5, None,
                                              ALU.mult).then_inc(first8.s, 1)
                        for j in range(R):
                            src = score[:, j, :] if r == 0 else rest[:, j, :]
                            last = dve.match_replace(rest[:, j, :], top[:, j, 8 * r:8 * r + 8], src,
                                                     NEG_TAKEN)
                            if r < TOPK // 8 - 1:
                                do.mark(last)
                        if r < TOPK // 8 - 1:
                            do.wait_apart()
                    last.then_inc(taken.s, 1)
                    reached(dve, sums, i)
                    do(dve.reciprocal(esum[:], esum[:]))
                    tm = tmask[:, bass.ds(i * ST, ST)].unsqueeze(1).to_broadcast([P, H0, ST])
                    e3 = esum[:].rearrange("p (h t) -> p h t", h=H0)
                    dve.tensor_tensor(e3, e3, tm, ALU.mult).then_inc(weights.s, 1)
                    for n, (f, fb) in enumerate(((f_in, film_b[0]), (f_out, film_b[1]))):
                        for t in range(ST):
                            reached(dve, film_ps, i, ST * n + t + 1)
                            dve.scalar_tensor_tensor(f[:, t, :], pB[:] if t % 2 == 0 else pC[:],
                                                     gate[:, 0:1], fb[:], ALU.mult, ALU.add
                                                     ).then_inc(film_sb.s, 1)
                    reached(dve, u_ready, i)
                    reached(dve, film_sb, i)
                    do(dve.tensor_tensor(x1[:], u[:], f_in[:, :, 0:D], ALU.mult))
                    dve.tensor_tensor(x1[:], x1[:], f_in[:, :, D:2 * D], ALU.add
                                      ).then_inc(x1_ready.s, 1)
                    reached(dve, spec_sb, i)
                    k_re = kr[:].rearrange("p k d -> p (k d)")
                    k_im = ki[:].rearrange("p k d -> p (k d)")
                    do.mark(dve.tensor_tensor(prod[:, 0, :], spec[:, 0, :], k_re, ALU.mult))
                    do(dve.tensor_tensor(prod[:, 1, :], spec[:, 1, :], k_im, ALU.mult))
                    dve.tensor_tensor(yspec[:, 0, :], prod[:, 0, :], prod[:, 1, :], ALU.subtract
                                      ).then_inc(yr_ready.s, 1)
                    reached(dve, y_ps, i)
                    reached(dve, xt_pre, i)
                    do(dve.tensor_tensor(xt[:], pA[:], f_out[:, :, 0:D], ALU.mult))
                    dve.tensor_tensor(xt[:], xt[:], f_out[:, :, D:2 * D], ALU.add
                                      ).then_inc(xt_ready.s, 1)
                    reached(dve, xt_ready, i)
                    stats(2, xt)
                    normal(2, x1, xt).then_inc(h_norm.s, 1)
                    reached(dve, dn_ps, i)
                    reached(dve, resid, i)
                    do(dve.tensor_tensor(u[:].rearrange("p t d -> p (t d)"),
                                         u[:].rearrange("p t d -> p (t d)"), pB[:], ALU.add))
                    stats(3, u)
                    do(normal(3, u, u))
                    do(dve.tensor_tensor(u[:], u[:], g_out[:].unsqueeze(1).to_broadcast([P, ST, D]),
                                         ALU.mult))
                    dve.tensor_tensor(core.x[:, bass.ds(i * ST, ST), :], u[:], xw[:], ALU.add
                                      ).then_inc(done.s, 1)
                    do.end()

            @block.tensor
            def _(pe):
                pe.wait_ge(loaded, 16 * (N_LOADS))
                pe.wait_ge(ready, 6)

                def transposes(dst, src):
                    for t in range(ST):
                        for c in range(DC):
                            last = pe.transpose(dst[:, c, t * P:(t + 1) * P],
                                                src[:, t, c * P:(c + 1) * P], core.ident[:])
                    return last

                with pe.Fori(0, B) as i:
                    reached(pe, norm, i)
                    released(pe, t_sb, i)
                    transposes(pT, xn).then_inc(t_ps.s, 1)
                    reached(pe, t_sb, i, 1)
                    reached(pe, ctx_in, i)
                    released(pe, xt_ready, i)
                    for c in range(DC):
                        pe.matmul(pA[:, 0, :], wq[:, c, :], xnT[:, c, :], start=(c == 0),
                                  stop=(c == DC - 1))
                    for c in range(2):
                        last = pe.matmul(pA[:, 1, :], wk[:, c, :], ctxw[:, c, :], start=(c == 0),
                                         stop=(c == 1))
                    last.then_inc(proj_ps.s, 1)
                    released(pe, done, i)
                    for g in range(ST):
                        for c in range(2):
                            last = pe.matmul(pB[:, g * D:(g + 1) * D], ctxw[:, c, g * P:(g + 1) * P],
                                             wv[:, c, :], start=(c == 0), stop=(c == 1))
                    last.then_inc(proj_ps.s, 1)
                    reached(pe, proj_sb, i, 1)
                    released(pe, u_act, i)
                    for t in range(ST):
                        for h in range(H0):
                            r = slice(DH0 * h, DH0 * (h + 1))
                            q = slice(DH0 * h, DH0 * h + 1)
                            pe.matmul(pS[:, h, t, :], core.ones_bf[q, :], maskw[q, :],
                                      start=True, stop=False)
                            last = pe.matmul(pS[:, h, t, :], qk[r, 0, t * P:(t + 1) * P],
                                             qk[r, 1, :], start=False, stop=True)
                    last.then_inc(scores.s, 1)
                    reached(pe, probs, i)
                    reached(pe, diags, i)
                    for g in range(ST):
                        for t in range(ST):
                            for h in range(H0):
                                j = ST * h + t
                                last = pe.matmul(pC[:, g * S + t * P:g * S + (t + 1) * P],
                                                 prob[:, j, g * P:(g + 1) * P], diag[:, j, :],
                                                 start=(h == 0), stop=(h == H0 - 1))
                    last.then_inc(at_ps.s, 1)
                    reached(pe, at_sb, i)
                    reached(pe, proj_sb, i, 2)
                    for c in range(DC):
                        for g in range(ST):
                            last = pe.matmul(pT[:, c, :], v[:, g, c * P:(c + 1) * P],
                                             attnT[:, g, :], start=(g == 0), stop=(g == ST - 1))
                    last.then_inc(ct_ps.s, 1)
                    reached(pe, ct_sb, i)
                    for n in range(2):
                        for t in range(ST):
                            if n:
                                reached(pe, film_sb, i, t + 1)
                            out = pB[:] if t % 2 == 0 else pC[:]
                            for c in range(DC):
                                last = pe.matmul(out, ctT[:, c, t * P:(t + 1) * P],
                                                 film[n][:, c, :], start=(c == 0),
                                                 stop=(c == DC - 1))
                            last.then_inc(film_ps.s, 1)
                    reached(pe, x1_ready, i)
                    for part in range(2):
                        for k in range(2):
                            out = pA[:, k, :] if part == 0 else pB[:, k * D:(k + 1) * D]
                            for t in range(ST):
                                last = pe.matmul(out, dft[:, t, part, k * P:(k + 1) * P],
                                                 x1[:, t, :], start=(t == 0), stop=(t == ST - 1))
                    last.then_inc(spec_ps.s, 1)
                    reached(pe, yr_ready, i)
                    reached(pe, yi_ready, i)
                    for t in range(ST):
                        for part in range(2):
                            for k in range(2):
                                last = pe.matmul(pA[:, t, :], idft[:, k, part, t * P:(t + 1) * P],
                                                 yspec[:, part, k * D:(k + 1) * D],
                                                 start=(part == 0 and k == 0),
                                                 stop=(part == 1 and k == 1))
                    last.then_inc(y_ps.s, 1)
                    reached(pe, h_norm, i)
                    transposes(pT, x1).then_inc(t_ps.s, 1)
                    reached(pe, t_sb, i, 2)
                    for c in range(HC):
                        for k in range(DC):
                            last = pe.matmul(pS[:, c // 2, c % 2, :], w1[:, k, c * P:(c + 1) * P],
                                             hT[:, k, :], start=(k == 0), stop=(k == DC - 1))
                        last.then_inc(u_ps.s, 1)
                    for t in range(ST):
                        for c in range(HC):
                            if t == 0:
                                reached(pe, u_act, i, c + 1)
                            last = pe.matmul(pB[:, t * D:(t + 1) * D], act1[:, c, t * P:(t + 1) * P],
                                             w2[:, c, :], start=(c == 0), stop=(c == HC - 1))
                    last.then_inc(dn_ps.s, 1)


def leaf_masks(dve, do, bits, m, keep_groups):
    do(dve.memset(m[0][:, :, 0:1], 1.0))
    for level in range(DEPTH):
        n = 1 << level
        here = m[level % 2][:, :, 0:n]
        if n == NG:
            keep_groups(here)
        kids = m[1 - level % 2][:, :, 0:2 * n].rearrange("p j (n c) -> p j n c", c=2)
        do(dve.tensor_tensor(kids[:, :, :, 1], here, bits[:, :, n - 1:2 * n - 1], ALU.mult))
        do(dve.tensor_tensor(kids[:, :, :, 0], here, kids[:, :, :, 1], ALU.subtract))
    return m[DEPTH % 2]


def place_tokens(core, name, group_all, nf, first, slot_i, tile_group_i):
    nc = core.nc
    W = nf * NG
    with ExitStack() as own:
        def sb(n, shape, dt=F32):
            return core.sb(own, f"{name}_{n}", shape, dt)

        tri, ones = sb("tri", [P, P], BF16), sb("ones", [P, P], BF16)
        cst = sb("cst", [P, NT + TILES + NG * NG])
        trif = sb("trif", [P, P])
        total = sb("total", [P, NT, W])
        before = sb("before", [P, NT + 1, W])
        pre = sb("pre", [P, NT, W])
        cmp = sb("cmp", [P, W, max(NG, NT)])
        used, start, end = sb("used", [P, W]), sb("start", [P, W]), sb("end", [P, W])
        slot = sb("slot", [P, NT, nf])
        cmp2 = sb("cmp2", [P, nf, TILES, NG])
        tg = sb("tile_group", [P, nf, TILES])
        psP = core.ps(own, f"{name}_psP", [P, 2, 512])
        psT = core.ps(own, f"{name}_psT", [P, 2, 512])
        loaded, ready = core.sem(name + "_loaded"), core.sem(name + "_ready")
        counted, chain = core.sem(name + "_counted"), core.sem(name + "_steps")
        half = NT // 2 * W
        with nc.Block() as block:
            @block.sync
            def _(sp):
                sp.dma_start(trif[:], core.dram["tri"]).then_inc(loaded, 16)
                sp.dma_start(cst[:], core.dram["counts"].partition_broadcast(P)
                             ).then_inc(loaded, 16)

            @block.tensor
            def _(pe):
                pe.wait_ge(ready, 2)
                for h in range(2):
                    g = group_all[:, h * half:(h + 1) * half]
                    pe.matmul(psP[:, h, 0:half], tri[:], g, start=True, stop=True)
                    last = pe.matmul(psT[:, h, 0:half], ones[:], g, start=True, stop=True)
                last.then_inc(counted, 1)

            @block.vector
            def _(dve):
                do = Chain(dve, chain)
                dve.wait_ge(loaded, 32)
                dve.tensor_copy(tri[:], trif[:]).then_inc(ready, 1)
                dve.memset(ones[:], 1.0).then_inc(ready, 1)
                do.mark(dve.memset(before[:, 0, :], 0.0))
                dve.wait_ge(counted, 1)
                for h in range(2):
                    do(dve.tensor_copy(total[:, h * NT // 2:(h + 1) * NT // 2, :]
                                       .rearrange("p t w -> p (t w)"), psT[:, h, 0:half]))
                for t in range(NT):
                    do(dve.tensor_tensor(before[:, t + 1, :], before[:, t, :], total[:, t, :],
                                         ALU.add))
                count = before[:, NT, :]
                wide = [P, W, NT]
                do(dve.tensor_tensor(cmp[:, :, 0:NT], count.unsqueeze(2).to_broadcast(wide),
                                     cst[:, 0:NT].unsqueeze(1).to_broadcast(wide), ALU.is_gt))
                do(dve.tensor_reduce(used[:], cmp[:, :, 0:NT], AX_X, ALU.add))
                below = cst[:, NT + TILES:].rearrange("p (a b) -> p a b", b=NG)
                for f in range(nf):
                    u = used[:, f * NG:(f + 1) * NG]
                    do(dve.tensor_tensor(cmp[:, f * NG:(f + 1) * NG, 0:NG],
                                         u.unsqueeze(1).to_broadcast([P, NG, NG]), below,
                                         ALU.mult))
                do(dve.tensor_reduce(start[:], cmp[:, :, 0:NG], AX_X, ALU.add))
                do(dve.tensor_tensor(end[:], start[:], used[:], ALU.add))
                do(dve.tensor_scalar(start[:], start[:], float(P), None, ALU.mult))
                for h in range(2):
                    do(dve.tensor_tensor(pre[:, h * NT // 2:(h + 1) * NT // 2, :]
                                         .rearrange("p t w -> p (t w)"), psP[:, h, 0:half],
                                         before[:, h * NT // 2:(h + 1) * NT // 2, :]
                                         .rearrange("p t w -> p (t w)"), ALU.add))
                do(dve.tensor_tensor(pre[:], pre[:], start[:].unsqueeze(1).to_broadcast([P, NT, W]),
                                     ALU.add))
                do(dve.tensor_tensor(pre[:].rearrange("p t w -> p (t w)"),
                                     pre[:].rearrange("p t w -> p (t w)"), group_all, ALU.mult))
                do(dve.tensor_reduce(slot[:], pre[:].rearrange("p t (f s) -> p t f s", f=nf),
                                     AX_X, ALU.add))
                do(dve.tensor_copy(slot_i[:], slot[:]))
                for f in range(nf):
                    wide = [P, TILES, NG]
                    do(dve.tensor_tensor(cmp2[:, f, :, :],
                                         end[:, f * NG:(f + 1) * NG].unsqueeze(1)
                                         .to_broadcast(wide),
                                         cst[:, NT:NT + TILES].unsqueeze(2).to_broadcast(wide),
                                         ALU.is_le))
                    do(dve.tensor_reduce(tg[:, f, :], cmp2[:, f, :, :], AX_X, ALU.add))
                for f in range(nf):
                    do(dve.tensor_scalar(tg[:, f, :], tg[:, f, :], float(NG - 1),
                                         float((first + f) * NG), ALU.min, ALU.add))
                do(dve.tensor_copy(tile_group_i[:], tg[:]))




def group_products(core, name, nf, rows, slot_i, tile_group_i, sorted_x, sorted_y, results,
                   gelu=False):
    nc, dram = core.nc, core.dram
    NB = 4
    TURNS = nf * TILES // NB
    with ExitStack() as own:
        def sb(n, shape, dt=F32):
            return core.sb(own, f"{name}_{n}", shape, dt)

        hold = sb("hold", [GL, GH])
        spread = sb("leaf_units", [GL, GH], BF16)
        xs = [sb(f"x{n}", [P, XW]) for n in range(NB)]
        w1 = [sb(f"w1_{n}", [P, W1COLS]) for n in range(NB)]
        w2 = [sb(f"w2_{n}", [P, GH // P, D]) for n in range(NB)]
        b2 = [sb(f"b2_{n}", [GL, D]) for n in range(NB)]
        xT = [sb(f"xT{n}", [P, DC, P]) for n in range(2)]
        leafT = [sb(f"leafT{n}", [GL, P]) for n in range(2)]
        leafB = [sb(f"leafB{n}", [GL, P], BF16) for n in range(2)]
        act_h = [sb(f"act{n}", [P, GH // P, P]) for n in range(2)]
        hT = [sb(f"hT{n}", [P, GH // P, P]) for n in range(2)]
        ys = [sb(f"y{n}", [P, D]) for n in range(2)]
        psX = [core.ps(own, f"{name}_psX{n}", [P, 4, P]) for n in range(2)]
        psH = [core.ps(own, f"{name}_psH{n}", [P, 4, P]) for n in range(2)]
        psM = [core.ps(own, f"{name}_psM{n}", [P, 4, P]) for n in range(2)]
        psY = [core.ps(own, f"{name}_psY{n}", [P, 2 * D]) for n in range(2)]
        loaded, ready = core.sem(name + "_loaded"), core.sem(name + "_ready")
        placed = [core.sem(f"{name}_placed{f}") for f in range(nf)]
        fetched = core.sem(name + "_fetched")
        tile_in = [core.sem(f"{name}_tile_in{n}") for n in range(NB)]
        worked = [core.sem(f"{name}_worked{n}") for n in range(NB)]
        stored = [core.sem(f"{name}_stored{n}") for n in range(2)]
        x_ps, xT_sb, leaf_sb, h_ps, h_act, h_sb, y_sb = (
            core.sem(f"{name}_{n}") for n in ("x_ps", "xT_sb", "leaf_sb", "h_ps", "h_act", "h_sb",
                                              "y_sb"))

        def two_back(eng, i, n):
            eng.wait_ge(worked[(n + 2) % NB], i + 1 if n >= 2 else i)

        with nc.Block() as block:
            @block.gpsimd
            def _(pool):
                pool.wait_ge(core.zeroed, 16 * ZERO_FILLS)
                for f in range(nf):
                    for t in range(NT):
                        pool.indirect_dma_start(
                            sorted_x[f], bass.IndirectOffsetOnAxis(slot_i[:, t, f:f + 1], 0),
                            rows[:, f, t, :], None).then_inc(placed[f], 16)
                for f in range(nf):
                    for n in range(2):
                        pool.wait_ge(stored[n], 16 * (f + 1) * TILES // 2)
                    for t in range(NT):
                        pool.indirect_dma_start(
                            results[:, f, t, :], None, sorted_y[f],
                            bass.IndirectOffsetOnAxis(slot_i[:, t, f:f + 1], 0)
                            ).then_inc(fetched, 16)
                pool.wait_ge(fetched, 16 * NT * nf)

            @block.sync
            def _(sp):
                sp.dma_start(hold[:], dram["leaf_units"]).then_inc(loaded, 16)
                for f in range(nf):
                    sp.wait_ge(placed[f], 16 * NT)
                    with sp.Fori(f * TILES // NB, (f + 1) * TILES // NB) as i:
                        for n in range(NB):
                            tile = i * NB + n
                            g = sp.value_load(tile_group_i[0:1, bass.ds(tile, 1)], min_val=0,
                                              max_val=4 * NG - 1)
                            sp.wait_ge(worked[n], i)
                            for out, in_ in (
                                    (xs[n][:], sorted_x[f][bass.ds((tile - f * TILES) * P, P), :]),
                                    (w1[n][:], dram["group_w1"][bass.ds(g * P, P), :]),
                                    (w2[n][:].rearrange("p c d -> p (c d)"),
                                     dram["group_w2"][bass.ds(g * P, P), :]),
                                    (b2[n][:], dram["group_b2"][bass.ds(g * GL, GL), :])):
                                sp.dma_start(out, in_).then_inc(tile_in[n], 16)

            @block.scalar
            def _(act):
                for f in range(nf):
                    with act.Fori(f * TILES // NB, (f + 1) * TILES // NB) as i:
                        for n in range(NB):
                            tile, k = i * NB + n, n % 2
                            act.wait_ge(x_ps, tile + 1)
                            two_back(act, i, n)
                            act.wait_ge(xT_sb, tile + 1)
                            act.activation(leafT[k][:], psX[k][0:GL, DC, :], ACT.Copy
                                           ).then_inc(leaf_sb, 1)
                            act.wait_ge(h_ps, tile + 1)
                            two_back(act, i, n)
                            for c in range(GH // P):
                                b1 = w1[n][:, DC * GH + c:DC * GH + c + 1]
                                last = act.activation(act_h[k][:, c, :], psH[k][:, c, :],
                                                      ACT.Gelu if gelu else ACT.Relu, bias=b1)
                            last.then_inc(h_act, 1)
                            act.wait_ge(worked[n], i + 1)
                            act.wait_ge(stored[k], i * 32 + (16 if n >= 2 else 0))
                            act.activation(ys[k][:], psY[k][:, 0:D], ACT.Copy).then_inc(y_sb, 1)
                            act.wait_ge(y_sb, tile + 1)
                            act.dma_start(sorted_y[f][bass.ds((tile - f * TILES) * P, P), :], ys[k][:]
                                          ).then_inc(stored[k], 16)

            @block.vector
            def _(dve):
                dve.wait_ge(loaded, 16)
                dve.tensor_copy(spread[:], hold[:]).then_inc(ready, 1)
                with dve.Fori(0, TURNS) as i:
                    for n in range(NB):
                        tile, k = i * NB + n, n % 2
                        dve.wait_ge(x_ps, tile + 1)
                        two_back(dve, i, n)
                        dve.tensor_copy(leafB[k][:], psX[k][0:GL, DC, :])
                        dve.tensor_copy(xT[k][:], psX[k][:, 0:DC, :]).then_inc(xT_sb, 1)
                        dve.wait_ge(h_act, tile + 1)
                        dve.tensor_tensor(hT[k][:], act_h[k][:], psM[k][:, 0:GH // P, :], ALU.mult
                                          ).then_inc(h_sb, 1)

            @block.tensor
            def _(pe):
                pe.wait_ge(ready, 1)

                def turn_over(i, n, j):
                    return i + (n + j) // NB, (n + j) % NB

                def transposes(i, n, first=False):
                    tile, k = i * NB + n, n % 2
                    pe.wait_ge(tile_in[n], 64 * i + 64)
                    if not first:
                        pe.wait_ge(leaf_sb, tile - 1)
                    for c in range(DC):
                        pe.transpose(psX[k][:, c, :], xs[n][:, c * P:(c + 1) * P], core.ident[:])
                    pe.transpose(psX[k][0:GL, DC, :], xs[n][:, D:XW], core.ident[:]
                                 ).then_inc(x_ps, 1)

                def hidden(i, n, first=False):
                    tile, k = i * NB + n, n % 2
                    pe.wait_ge(xT_sb, tile + 1)
                    if not first:
                        pe.wait_ge(h_sb, tile - 1)
                    for c in range(GH // P):
                        for d in range(DC):
                            w = w1[n][:, d * GH + c * P:d * GH + (c + 1) * P]
                            pe.matmul(psH[k][:, c, :], w, xT[k][:, d, :], start=(d == 0),
                                      stop=(d == DC - 1))
                    for c in range(GH // P):
                        last = pe.matmul(psM[k][:, c, :], spread[:, c * P:(c + 1) * P],
                                         leafB[k][:], start=True, stop=True)
                    last.then_inc(h_ps, 1)

                def output(i, n):
                    tile, k = i * NB + n, n % 2
                    pe.wait_ge(leaf_sb, tile + 1)
                    if n >= 2:
                        pe.wait_ge(y_sb, tile - 1)
                    else:
                        pe.wait_ge(y_sb, i * NB + n)
                    pe.matmul(psY[k][:, 0:D], leafT[k][:], b2[n][:], start=True, stop=False)
                    pe.wait_ge(h_sb, tile + 1)
                    for c in range(GH // P):
                        last = pe.matmul(psY[k][:, 0:D], hT[k][:, c, :], w2[n][:, c, :],
                                         start=False, stop=(c == GH // P - 1))
                    last.then_inc(worked[n], 1)

                def turn(i, ahead=(True,) * NB):
                    for n in range(NB):
                        if ahead[n]:
                            hidden(*turn_over(i, n, 1))
                        if n + 2 < NB or ahead[n] and ahead[-1]:
                            transposes(*turn_over(i, n, 2))
                        output(i, n)

                transposes(0, 0, first=True)
                transposes(0, 1, first=True)
                hidden(0, 0, first=True)
                with pe.Fori(0, TURNS - 1) as i:
                    turn(i)
                turn(TURNS - 1, (True,) * (NB - 1) + (False,))


def standard_rows(pool, steps, out, var, plus_half, minus_half):
    steps(pool.tensor_scalar(out, var, D / (D - 1), None, ALU.mult))
    steps.mark(pool.tensor_tensor(out, out, plus_half, ALU.pow))
    steps.wait_apart()
    return rstd_of(pool, steps, out, out, minus_half)


def route_qkv(core, ctx, rows, xn_keep, group_all):
    nc, dram = core.nc, core.dram
    NF = 3
    with ExitStack() as own:
        def sb(n, shape, dt=F32):
            return core.sb(own, "r_" + n, shape, dt)

        nw, nb = sb("nw", [P, NF, DC, NN]), sb("nb", [P, NF, NN])
        st, mv = sb("stats", [P, ST, 6]), sb("mean_var", [P, 2, ST, 2])
        rstd = sb("rstd", [P, 2, ST])
        xl, xn, xnT = sb("xl", [P, ST, D]), sb("xn", [P, ST, D]), sb("xnT", [P, DC, S])
        bits = sb("bits", [P, NF * ST, NN])
        m = [sb(f"mask{n}", [P, NF * ST, NL]) for n in range(2)]
        psT = core.ps(own, "r_psT", [P, DC, S])
        psL = core.ps(own, "r_psL", [P, NF, ST, S])
        loaded, ready = core.sem("r_loaded"), core.sem("r_ready")
        sig = core.flag
        var, rs, norm, kept = sig("r_var", 2), sig("r_rstd", 2), sig("r_norm"), sig("r_kept")
        t_ps, t_sb, logits, bits_sb = (sig("r_" + n) for n in ("T_ps", "T_sb", "logits", "bits"))
        rows_in = sig("r_rows")
        dchain, pchain = core.sem("r_dve"), core.sem("r_pool")
        DVE_STEPS, POOL_STEPS = 25, 4
        with nc.Block() as block:
            @block.sync
            def _(sp):
                for n, f in enumerate("qkv"):
                    sp.dma_start(nw[:, n, :, :], dram[f"L0_ffn_{f}_nwT"]
                                 .rearrange("(c p) n -> p c n", p=P)).then_inc(loaded, 16)
                    sp.dma_start(nb[:, n, :], dram[f"L0_ffn_{f}_nb"].partition_broadcast(P)
                                 ).then_inc(loaded, 16)

            @block.gpsimd
            def _(pool):
                with pool.Fori(0, B) as i:
                    do = Chain(pool, pchain, i, POOL_STEPS)
                    reached_apart(pool, var, i, 1)
                    rstd_of(pool, do, rstd[:, 0, :], mv[:, 0, :, 1], core.minus_half[:]
                            ).then_inc(rs.s, 1)
                    reached_apart(pool, var, i, 2)
                    standard_rows(pool, do, rstd[:, 1, :], mv[:, 1, :, 1], core.plus_half[:],
                                  core.minus_half[:]).then_inc(rs.s, 1)
                    reached(pool, norm, i)
                    pool.tensor_copy(xn_keep[:, bass.ds(i * ST, ST), :], xn[:]).then_inc(kept.s, 1)
                    do.end()

            @block.scalar
            def _(act):
                with act.Fori(0, B) as i:
                    reached(act, t_ps, i)
                    act.activation(xnT[:], psT[:], ACT.Copy).then_inc(t_sb.s, 1)
                    for f in range(NF):
                        last = act.activation(rows[:, f, bass.ds(i * ST, ST), 0:D], xn[:],
                                              ACT.Copy)
                    last.then_inc(rows_in.s, 1)

            @block.vector
            def _(dve):
                dve.wait_ge(loaded, 16 * 2 * NF)
                dve.tensor_scalar(nb[:], nb[:], -1.0, None, ALU.mult).then_inc(ready, 1)
                dve.wait_ge(ready, 1)
                with dve.Fori(0, B) as i:
                    do = Chain(dve, dchain, i, DVE_STEPS)

                    def stats(n, src):
                        for t in range(ST):
                            do.mark(dve.bn_stats(st[:, t, :], src(t)))
                        do.wait_apart()
                        for t in range(ST):
                            last = dve.bn_aggr(mv[:, n, t, :], st[:, t, :])
                        last.then_inc(var.s, 1)

                    def normal(n, dst, src):
                        reached(dve, var, i, n + 1)
                        reached(dve, rs, i, n + 1)
                        for t in range(ST):
                            last = dve.tensor_scalar(dst[:, t, :], src(t), mv[:, n, t, 0:1],
                                                     rstd[:, n, t:t + 1], ALU.subtract, ALU.mult)
                        return last

                    def xt(t):
                        return core.x[:, bass.ds(i * ST + t, 1), :].rearrange("p a d -> p (a d)")

                    stats(0, xt)
                    do(normal(0, xl, xt))
                    stats(1, lambda t: xl[:, t, :])
                    released(dve, t_ps, i)
                    released(dve, kept, i)
                    released(dve, rows_in, i)
                    normal(1, xn, lambda t: xl[:, t, :]).then_inc(norm.s, 1)
                    reached(dve, logits, i)
                    nbw = nb[:].unsqueeze(2).to_broadcast([P, NF, ST, NN])
                    dve.tensor_tensor(bits[:].rearrange("p (f t) n -> p f t n", f=NF),
                                      psL[:, :, :, 0:NN], nbw, ALU.is_gt).then_inc(bits_sb.s, 1)
                    reached(dve, bits_sb, i)

                    def keep_groups(here):
                        out = group_all[:, bass.ds(i * ST, ST), :, :]
                        dve.tensor_copy(out.rearrange("p t f s -> p f t s"),
                                        here.rearrange("p (f t) s -> p f t s", f=NF))

                    leaves = leaf_masks(dve, do, bits, m, keep_groups)
                    for f in range(NF):
                        by_leaf = leaves[:, f * ST:(f + 1) * ST, :].rearrange(
                            "p t (g l) -> p t l g", l=GL)
                        do.mark(dve.tensor_reduce(rows[:, f, bass.ds(i * ST, ST), D:XW], by_leaf,
                                                  AX_X, ALU.add))
                    do.end()

            @block.tensor
            def _(pe):
                pe.wait_ge(loaded, 16 * 2 * NF)
                with pe.Fori(0, B) as i:
                    reached(pe, norm, i)
                    released(pe, t_sb, i)
                    for t in range(ST):
                        for c in range(DC):
                            last = pe.transpose(psT[:, c, t * P:(t + 1) * P],
                                                xn[:, t, c * P:(c + 1) * P], core.ident[:])
                    last.then_inc(t_ps.s, 1)
                    reached(pe, t_sb, i)
                    released(pe, bits_sb, i)
                    for f in range(NF):
                        for t in range(ST):
                            for c in range(DC):
                                last = pe.matmul(psL[:, f, t, 0:NN], xnT[:, c, t * P:(t + 1) * P],
                                                 nw[:, f, c, :], start=(c == 0),
                                                 stop=(c == DC - 1))
                    last.then_inc(logits.s, 1)


class Norms:

    def __init__(self, core, ctx, name, kinds, tiles=ST):
        self.core, self.kinds, self.tiles = core, kinds, tiles
        self.st = core.sb(ctx, name + "_stats", [P, tiles, 6])
        self.mv = core.sb(ctx, name + "_mean_var", [P, kinds, tiles, 2])
        self.rstd = core.sb(ctx, name + "_rstd", [P, kinds, tiles])
        self.half = core.sb(ctx, name + "_minus_half", [P, tiles])
        self.var = core.flag(name + "_var", kinds)
        self.rs = core.flag(name + "_rs", kinds)

    def stats(self, dve, do, n, src):
        for t in range(self.tiles):
            do.mark(dve.bn_stats(self.st[:, t, :], src[:, t, :]))
        do.wait_apart()
        for t in range(self.tiles):
            last = dve.bn_aggr(self.mv[:, n, t, :], self.st[:, t, :])
        last.then_inc(self.var.s, 1)

    def root(self, pool, do, i, n):
        reached_apart(pool, self.var, i, n + 1)
        rstd_of(pool, do, self.rstd[:, n, :], self.mv[:, n, :, 1], self.half[:]
                ).then_inc(self.rs.s, 1)

    def normal(self, dve, i, n, dst, src):
        reached(dve, self.var, i, n + 1)
        reached(dve, self.rs, i, n + 1)
        for t in range(self.tiles):
            last = dve.tensor_scalar(dst[:, t, :], src[:, t, :], self.mv[:, n, t, 0:1],
                                     self.rstd[:, n, t:t + 1], ALU.subtract, ALU.mult)
        return last


def token_attention(core, results, xn_keep, rows, group_all):
    nc, dram = core.nc, core.dram
    with ExitStack() as own:
        def sb(n, shape, dt=F32):
            return core.sb(own, "t_" + n, shape, dt)

        nw, nb = sb("nw", [P, DC, NN]), sb("nb", [P, NN])
        qk = sb("qk", [P, 2, ST, D])
        qkT = sb("qkT", [P, 2, DC, S])
        mx, nmx, total = sb("max", [P, ST]), sb("minus_max", [P, ST]), sb("total", [P, ST])
        p, pT = sb("p", [P, ST, S]), sb("pT", [P, ST, S])
        y, yT = sb("y", [P, ST, D]), sb("yT", [P, DC, S])
        bits = sb("bits", [P, ST, NN])
        m = [sb(f"mask{n}", [P, ST, NL]) for n in range(2)]
        psQ = core.ps(own, "t_psQ", [P, 2, DC, S])
        psS, psP = core.ps(own, "t_psS", [P, ST, S]), core.ps(own, "t_psP", [P, ST, S])
        psO, psY = core.ps(own, "t_psO", [P, ST, D]), core.ps(own, "t_psY", [P, DC, S])
        psL = core.ps(own, "t_psL", [P, ST, S])
        loaded, ready = core.sem("t_loaded"), core.sem("t_ready")
        sig = core.flag
        (qk_in, q_ps, q_sb, s_ps, m_sb, p_sb, pT_ps, pT_sb, o_ps, y_sb, y_kept, yT_ps, yT_sb,
         l_ps, bits_sb, row_in) = (
            sig("t_" + n) for n in ("qk_in", "q_ps", "q_sb", "s_ps", "m_sb", "p_sb", "pT_ps",
                                    "pT_sb", "o_ps", "y_sb", "y_kept", "yT_ps", "yT_sb", "l_ps",
                                    "bits", "row_in"))
        dchain = core.sem("t_dve")
        DVE_STEPS = 20
        with nc.Block() as block:
            @block.sync
            def _(sp):
                sp.dma_start(nw[:], dram["L0_ffn_f_nwT"].rearrange("(c p) n -> p c n", p=P)
                             ).then_inc(loaded, 16)
                sp.dma_start(nb[:], dram["L0_ffn_f_nb"].partition_broadcast(P)
                             ).then_inc(loaded, 16)

            @block.gpsimd
            def _(pool):
                with pool.Fori(0, B) as i:
                    reached(pool, y_sb, i)
                    xs = core.x[:, bass.ds(i * ST, ST), :]
                    pool.tensor_tensor(xs, xs, y[:], ALU.add).then_inc(y_kept.s, 1)

            @block.scalar
            def _(act):
                with act.Fori(0, B) as i:
                    released(act, q_ps, i)
                    for n in range(2):
                        last = act.activation(qk[:, n, :, :], results[:, n, bass.ds(i * ST, ST), :],
                                              ACT.Copy)
                    last.then_inc(qk_in.s, 1)
                    reached(act, q_ps, i)
                    act.activation(qkT[:], psQ[:], ACT.Copy).then_inc(q_sb.s, 1)
                    reached(act, m_sb, i)
                    for t in range(ST):
                        last = act.activation(p[:, t, :], psS[:, t, :], ACT.Exp,
                                              bias=nmx[:, t:t + 1], scale=float(D) ** -0.5,
                                              accum_out=total[:, t:t + 1])
                    last.then_inc(p_sb.s, 1)
                    reached(act, pT_ps, i)
                    act.activation(pT[:], psP[:], ACT.Copy).then_inc(pT_sb.s, 1)
                    reached(act, y_sb, i)
                    act.activation(rows[:, 0, bass.ds(i * ST, ST), 0:D], y[:], ACT.Copy
                                   ).then_inc(row_in.s, 1)
                    reached(act, yT_ps, i)
                    act.activation(yT[:], psY[:], ACT.Copy).then_inc(yT_sb.s, 1)

            @block.vector
            def _(dve):
                dve.wait_ge(loaded, 32)
                dve.tensor_scalar(nb[:], nb[:], -1.0, None, ALU.mult).then_inc(ready, 1)
                dve.wait_ge(ready, 1)
                with dve.Fori(0, B) as i:
                    do = Chain(dve, dchain, i, DVE_STEPS)
                    reached(dve, s_ps, i)
                    do(dve.tensor_reduce(mx[:], psS[:], AX_X, ALU.max))
                    dve.tensor_scalar(nmx[:], mx[:], -float(D) ** -0.5, None, ALU.mult
                                      ).then_inc(m_sb.s, 1)
                    reached(dve, p_sb, i)
                    do(dve.reciprocal(total[:], total[:]))
                    reached(dve, o_ps, i)
                    released(dve, y_kept, i)
                    released(dve, row_in, i)
                    for t in range(ST):
                        xn = xn_keep[:, bass.ds(i * ST + t, 1), :].rearrange("p a d -> p (a d)")
                        last = dve.scalar_tensor_tensor(y[:, t, :], psO[:, t, :],
                                                        total[:, t:t + 1], xn, ALU.mult, ALU.add)
                    last.then_inc(y_sb.s, 1)
                    reached(dve, l_ps, i)
                    dve.tensor_tensor(bits[:], psL[:, :, 0:NN],
                                      nb[:].unsqueeze(1).to_broadcast([P, ST, NN]), ALU.is_gt
                                      ).then_inc(bits_sb.s, 1)
                    reached(dve, bits_sb, i)

                    def keep_groups(here):
                        dve.tensor_copy(group_all[:, bass.ds(i * ST, ST), :], here)

                    leaves = leaf_masks(dve, do, bits, m, keep_groups)
                    do.mark(dve.tensor_reduce(rows[:, 0, bass.ds(i * ST, ST), D:XW],
                                              leaves.rearrange("p t (g l) -> p t l g", l=GL),
                                              AX_X, ALU.add))
                    do.end()

            @block.tensor
            def _(pe):
                pe.wait_ge(loaded, 32)

                def transposes(dst, src):
                    for t in range(ST):
                        for c in range(DC):
                            last = pe.transpose(dst[:, c, t * P:(t + 1) * P],
                                                src[:, t, c * P:(c + 1) * P], core.ident[:])
                    return last

                with pe.Fori(0, B) as i:
                    reached(pe, qk_in, i)
                    released(pe, q_sb, i)
                    transposes(psQ[:, 0, :, :], qk[:, 0, :, :])
                    transposes(psQ[:, 1, :, :], qk[:, 1, :, :]).then_inc(q_ps.s, 1)
                    reached(pe, q_sb, i)
                    released(pe, p_sb, i)
                    for t in range(ST):
                        for c in range(DC):
                            last = pe.matmul(psS[:, t, :], qkT[:, 0, c, t * P:(t + 1) * P],
                                             qkT[:, 1, c, :], start=(c == 0), stop=(c == DC - 1))
                    last.then_inc(s_ps.s, 1)
                    reached(pe, p_sb, i)
                    released(pe, pT_sb, i)
                    transposes(psP, p).then_inc(pT_ps.s, 1)
                    reached(pe, pT_sb, i)
                    released(pe, y_sb, i)
                    for t in range(ST):
                        for c in range(ST):
                            v = results[:, 2, bass.ds(i * ST + c, 1), :]
                            last = pe.matmul(psO[:, t, :], pT[:, c, t * P:(t + 1) * P],
                                             v.rearrange("p a d -> p (a d)"),
                                             start=(c == 0), stop=(c == ST - 1))
                    last.then_inc(o_ps.s, 1)
                    reached(pe, y_sb, i)
                    released(pe, yT_sb, i)
                    transposes(psY, y).then_inc(yT_ps.s, 1)
                    reached(pe, yT_sb, i)
                    released(pe, bits_sb, i)
                    for t in range(ST):
                        for c in range(DC):
                            last = pe.matmul(psL[:, t, 0:NN], yT[:, c, t * P:(t + 1) * P],
                                             nw[:, c, :], start=(c == 0), stop=(c == DC - 1))
                    last.then_inc(l_ps.s, 1)


QC = H1 // 4


def second_attention(core, results):
    nc, dram = core.nc, core.dram
    with ExitStack() as own:
        def sb(n, shape, dt=F32):
            return core.sb(own, "c_" + n, shape, dt)

        wq, wk = sb("wq", [P, DC, QC * P]), sb("wk", [CP, 2, QC * P])
        wv, wo = sb("wv", [CP, 2, D]), sb("wo", [P, DC, D])
        bq, bk = sb("bq", [P, QC]), sb("bk", [P, QC])
        bv, bo = sb("bv", [P, D]), sb("bo", [P, D])
        selh, sel = sb("sel32", [P, QC, P]), sb("sel", [P, QC, P], BF16)
        identb = sb("ident_bf16", [P, P], BF16)
        xw, ctxw = sb("x", [P, ST, D]), sb("ctx", [CP, 2, S])
        xn, xnT = sb("xn", [P, ST, D]), sb("xnT", [P, DC, S])
        qT, kT = sb("qT", [P, QC, S]), sb("kT", [P, QC, S])
        v = sb("v", [P, ST, H1, DH1 + 1])
        top = sb("max", [P, QC, 4, ST])
        shift = sb("shift", [P, ST, 4, 32], BF16)
        shiftT = sb("shiftT", [P, S], BF16)
        prob = [sb(f"prob{n}", [P, 4, ST, S]) for n in range(2)]
        rec = sb("rec", [P, ST, H1])
        att, attT = sb("att", [P, ST, D]), sb("attT", [P, DC, S])
        norms = Norms(core, own, "c", 1)
        psS = core.ps(own, "c_psS", [P, 4, 2, S])
        psO = core.ps(own, "c_psO", [P, ST, 512])
        psA = core.ps(own, "c_psA", [P, DC, S])
        psB = core.ps(own, "c_psB", [P, ST, D])
        psA_bf = psA[:, 0, 0:S // 2].bitcast(BF16)
        loaded, ready = core.sem("c_loaded"), core.sem("c_ready")
        sig = core.flag
        (x_in, ctx_in, norm, t_ps, t_sb, q_ps, q_sb, k_sb, v_ps, v_sb, sh_sb, sh_ps, shT_sb,
         att_sb, aT_ps, aT_sb, f_ps, xb, done) = (
            sig("c_" + n) for n in ("x_in", "ctx_in", "norm", "t_ps", "t_sb", "q_ps", "q_sb",
                                    "k_sb", "v_ps", "v_sb", "sh_sb", "sh_ps", "shT_sb",
                                    "att_sb", "aT_ps", "aT_sb", "f_ps", "xb", "done"))
        m_ps, m_sb, s_ps, p_sb, pv = (sig("c_" + n, QC) for n in ("m_ps", "m_sb", "s_ps", "p_sb",
                                                                   "pv"))
        dchain, pchain = core.sem("c_dve"), core.sem("c_pool")
        DVE_STEPS, POOL_STEPS = 8, 1
        N_LOADS = 9
        with nc.Block() as block:
            @block.sync
            def _(sp):
                def load(out, in_):
                    sp.dma_start(out, in_).then_inc(loaded, 16)

                load(wq[:], dram["c_wq"].rearrange("(c p) n -> p c n", p=P))
                load(wk[:], dram["c_wk"].rearrange("(c p) n -> p c n", p=CP))
                load(wv[:], dram["L1_xattn_wv"].rearrange("(c p) n -> p c n", p=CP))
                load(wo[:], dram["L1_xattn_wo"].rearrange("(c p) n -> p c n", p=P))
                load(bq[:], dram["c_bq"])
                load(bk[:], dram["c_bk"])
                load(bv[:], dram["L1_xattn_bv"].partition_broadcast(P))
                load(bo[:], dram["L1_xattn_bo"].partition_broadcast(P))
                load(selh[:], dram["c_sel"])

            @block.gpsimd
            def _(pool):
                pool.memset(norms.half[:], -0.5).then_inc(ready, 1)
                pool.memset(shift[:], 0.0).then_inc(ready, 1)
                pool.memset(v[:], 1.0).then_inc(ready, 1)
                pool.wait_ge(loaded, 16 * N_LOADS)
                pool.tensor_copy(sel[:], selh[:]).then_inc(ready, 1)
                pool.tensor_copy(identb[:], core.ident[:]).then_inc(ready, 1)
                pool.wait_ge(ready, 5)
                with pool.Fori(0, B) as i:
                    do = Chain(pool, pchain, i, POOL_STEPS)
                    released(pool, v_ps, i)
                    pool.tensor_copy(ctxw[:], core.ctxT[:, :, bass.ds(i * S, S)]
                                     ).then_inc(ctx_in.s, 1)
                    norms.root(pool, do, i, 0)
                    reached(pool, norm, i)
                    pool.tensor_tensor(xw[:], xw[:], bo[:].unsqueeze(1).to_broadcast([P, ST, D]),
                                       ALU.add).then_inc(xb.s, 1)
                    do.end()

            @block.scalar
            def _(act):
                act.wait_ge(loaded, 16 * N_LOADS)
                with act.Fori(0, B) as i:
                    reached(act, t_ps, i)
                    act.activation(xnT[:], psA[:], ACT.Copy).then_inc(t_sb.s, 1)
                    reached(act, q_ps, i)
                    for c in range(QC):
                        last = act.activation(qT[:, c, :], psS[:, c // 2, c % 2, :], ACT.Identity,
                                              bias=bq[:, c:c + 1])
                    last.then_inc(q_sb.s, 1)
                    reached(act, sh_ps, i)
                    act.activation(shiftT[:], psA_bf[:], ACT.Copy).then_inc(shT_sb.s, 1)
                    for c in range(QC):
                        reached(act, s_ps, i, c + 1)
                        if c >= 2:
                            reached(act, pv, i, c - 1)
                        else:
                            released(act, pv, i)
                        act.activation(prob[c % 2][:], psS[:], ACT.Exp, scale=float(DH1) ** -0.5
                                       ).then_inc(p_sb.s, 1)
                    reached(act, aT_ps, i)
                    act.activation(attT[:], psA[:], ACT.Copy).then_inc(aT_sb.s, 1)

            @block.vector
            def _(dve):
                dve.wait_ge(loaded, 16 * N_LOADS)
                dve.wait_ge(ready, 5)
                with dve.Fori(0, B) as i:
                    do = Chain(dve, dchain, i, DVE_STEPS)
                    released(dve, done, i)
                    tiles = bass.ds(i * ST, ST)
                    do(dve.tensor_tensor(xw[:], core.x[:, tiles, :], results[:, 0, tiles, :],
                                         ALU.add))
                    norms.stats(dve, do, 0, xw)
                    norms.normal(dve, i, 0, xn, xw).then_inc(norm.s, 1)
                    reached(dve, q_ps, i)
                    for c in range(QC):
                        last = dve.tensor_scalar(kT[:, c, :], psS[:, 2 + c // 2, c % 2, :],
                                                 bk[:, c:c + 1], None, ALU.add)
                    last.then_inc(k_sb.s, 1)
                    reached(dve, v_ps, i)
                    released(dve, pv, i)
                    dve.tensor_tensor(v[:, :, :, 0:DH1],
                                      psB[:].rearrange("p t (h d) -> p t h d", h=H1),
                                      bv[:].rearrange("p (h d) -> p h d", h=H1).unsqueeze(1)
                                      .to_broadcast([P, ST, H1, DH1]), ALU.add).then_inc(v_sb.s, 1)
                    for c in range(QC):
                        reached(dve, m_ps, i, c + 1)
                        dve.tensor_reduce(top[:, c, :, :], psS[:], AX_X, ALU.max
                                          ).then_inc(m_sb.s, 1)
                    reached(dve, m_sb, i)
                    t4 = top[:].rearrange("p c r t -> p t r c")
                    do(dve.tensor_scalar(shift[:, :, :, 0:QC], t4, -1.0, None, ALU.mult))
                    for t in range(ST):
                        do(dve.tensor_tensor(rec[:, t, :].rearrange("p (r c) -> p r c", r=4),
                                             t4[:, t, :, :], shift[:, t, :, 0:QC], ALU.add))
                        do.mark(dve.tensor_scalar(shift[:, t, :, QC:2 * QC],
                                                  rec[:, t, :].rearrange("p (r c) -> p r c", r=4),
                                                  -1.0, None, ALU.mult)) if t == 0 else (
                            dve.tensor_scalar(shift[:, t, :, QC:2 * QC],
                                              rec[:, t, :].rearrange("p (r c) -> p r c", r=4),
                                              -1.0, None, ALU.mult).then_inc(sh_sb.s, 1))
                    reached(dve, pv, i)
                    po = psO[:, :, 0:H1 * (DH1 + 1)].rearrange("p t (h d) -> p t h d", h=H1)
                    do(dve.reciprocal(rec[:], po[:, :, :, DH1]))
                    dve.tensor_tensor(att[:].rearrange("p t (h d) -> p t h d", h=H1),
                                      po[:, :, :, 0:DH1],
                                      rec[:].unsqueeze(3).to_broadcast([P, ST, H1, DH1]),
                                      ALU.mult).then_inc(att_sb.s, 1)
                    reached(dve, f_ps, i)
                    reached(dve, xb, i)
                    dve.tensor_tensor(core.x[:, tiles, :], psB[:], xw[:], ALU.add
                                      ).then_inc(done.s, 1)
                    do.end()

            @block.tensor
            def _(pe):
                pe.wait_ge(loaded, 16 * N_LOADS)
                pe.wait_ge(ready, 5)

                def transposes(dst, src):
                    for t in range(ST):
                        for c in range(DC):
                            last = pe.transpose(dst[:, c, t * P:(t + 1) * P],
                                                src[:, t, c * P:(c + 1) * P], core.ident[:])
                    return last

                with pe.Fori(0, B) as i:
                    reached(pe, norm, i)
                    released(pe, aT_sb, i)
                    transposes(psA, xn).then_inc(t_ps.s, 1)
                    reached(pe, t_sb, i)
                    reached(pe, ctx_in, i)
                    released(pe, p_sb, i)
                    for c in range(QC):
                        for k in range(DC):
                            pe.matmul(psS[:, c // 2, c % 2, :], wq[:, k, c * P:(c + 1) * P],
                                      xnT[:, k, :], start=(k == 0), stop=(k == DC - 1))
                        for k in range(2):
                            last = pe.matmul(psS[:, 2 + c // 2, c % 2, :],
                                             wk[:, k, c * P:(c + 1) * P], ctxw[:, k, :],
                                             start=(k == 0), stop=(k == 1))
                    last.then_inc(q_ps.s, 1)
                    released(pe, done, i)
                    for g in range(ST):
                        for k in range(2):
                            last = pe.matmul(psB[:, g, :], ctxw[:, k, g * P:(g + 1) * P],
                                             wv[:, k, :], start=(k == 0), stop=(k == 1))
                    last.then_inc(v_ps.s, 1)
                    reached(pe, q_sb, i)
                    reached(pe, k_sb, i)
                    for c in range(QC):
                        if c:
                            reached(pe, m_sb, i, c)
                        for t in range(ST):
                            for r in range(4):
                                q = slice(32 * r, 32 * r + DH1)
                                last = pe.matmul(psS[:, r, t, :], qT[q, c, t * P:(t + 1) * P],
                                                 kT[q, c, :], start=True, stop=True)
                        last.then_inc(m_ps.s, 1)
                    reached(pe, sh_sb, i)
                    for t in range(ST):
                        last = pe.transpose(psA_bf[:, t * P:(t + 1) * P],
                                            shift[:, t, :, :].rearrange("p r c -> p (r c)"),
                                            identb[:])
                    last.then_inc(sh_ps.s, 1)
                    reached(pe, shT_sb, i)
                    def by_key(c):
                        if c:
                            reached(pe, p_sb, i, c)
                        for g in range(ST):
                            for r in range(4):
                                q, w = slice(32 * r, 32 * r + DH1), slice(32 * r, 32 * r + 2 * QC)
                                pe.matmul(psS[:, r, g, :], sel[w, c, :], shiftT[w, :],
                                          start=True, stop=False)
                                last = pe.matmul(psS[:, r, g, :], kT[q, c, g * P:(g + 1) * P],
                                                 qT[q, c, :], start=False, stop=True)
                        last.then_inc(s_ps.s, 1)

                    def times_v(c):
                        reached(pe, p_sb, i, c + 1)
                        if c == 0:
                            reached(pe, v_sb, i)
                            released(pe, att_sb, i)
                        for t in range(ST):
                            for r in range(4):
                                h = 4 * c + r
                                for g in range(ST):
                                    o = psO[:, t, h * (DH1 + 1):(h + 1) * (DH1 + 1)]
                                    last = pe.matmul(o, prob[c % 2][:, r, g, t * P:(t + 1) * P],
                                                     v[:, g, h, :], start=(g == 0),
                                                     stop=(g == ST - 1))
                        last.then_inc(pv.s, 1)
                        return last

                    by_key(0)
                    for c in range(1, QC):
                        by_key(c)
                        times_v(c - 1)
                    times_v(QC - 1)
                    reached(pe, att_sb, i)
                    transposes(psA, att).then_inc(aT_ps.s, 1)
                    reached(pe, aT_sb, i)
                    for t in range(ST):
                        for k in range(DC):
                            last = pe.matmul(psB[:, t, :], attT[:, k, t * P:(t + 1) * P],
                                             wo[:, k, :], start=(k == 0), stop=(k == DC - 1))
                    last.then_inc(f_ps.s, 1)


MT = 4
MS = MT * P
NU = NE + SI // P


def moe(core):
    nc, dram = core.nc, core.dram
    TURNS = B * S // MS
    with ExitStack() as own:
        def sb(n, shape, dt=F32):
            return core.sb(own, "m_" + n, shape, dt)

        gate, up = sb("gate", [P, NU, DC, P]), sb("up", [P, NU, DC, P])
        down = sb("down", [P, NU, D])
        router = sb("router", [P, DC, NE])
        bias = sb("router_bias", [P, 1])
        lower = sb("lower", [P, NE, NE])
        xw, xn, xnT = sb("x", [P, MT, D]), sb("xn", [P, MT, D]), sb("xnT", [P, DC, MS])
        top = sb("max", [P, MT])
        score, corr, wt = (sb(n, [P, MT, NE]) for n in ("score", "corrected", "weight"))
        total = sb("total", [P, MT])
        above, equal = sb("above", [P, MT, NE, NE]), sb("equal", [P, MT, NE, NE])
        silu = [sb(f"silu{n}", [P, MS]) for n in range(2)]
        act_u = [sb(f"act{n}", [P, MS]) for n in range(2)]
        acc = sb("acc", [P, MT, D])
        norms = Norms(core, own, "m", 1, MT)
        psG = [core.ps(own, f"m_psG{n}", [P, MS]) for n in range(2)]
        psU = [core.ps(own, f"m_psU{n}", [P, MS]) for n in range(2)]
        psD = core.ps(own, "m_psD", [P, MT, D])
        psX = core.ps(own, "m_psX", [P, MT, D])
        loaded, ready = core.sem("m_loaded"), core.sem("m_ready")
        sig = core.flag
        norm, t_ps, t_sb, r_ps, cen, exps, weights, out_sb = (
            sig("m_" + n) for n in ("norm", "t_ps", "t_sb", "r_ps", "centred", "exps", "weights",
                                    "out_sb"))
        g_ps, g_sb, a_sb = (sig("m_" + n, NU) for n in ("g_ps", "g_sb", "a_sb"))
        d_ps, d_sb, s_ps = sig("m_d_ps", NE), sig("m_d_sb", NE), sig("m_s_ps", NU - NE)
        stored = core.sem("m_stored")
        dchain, pchain = core.sem("m_dve"), core.sem("m_pool")
        DVE_STEPS, POOL_STEPS = 27, 1
        N_LOADS = 13
        out = dram["out"].rearrange("b (t p) d -> p (b t) d", p=P)
        with nc.Block() as block:
            @block.sync
            def _(sp):
                def load(out, in_):
                    sp.dma_start(out, in_).then_inc(loaded, 16)

                def split(name):
                    return dram["L1_ffn_" + name].rearrange("(c p) n -> p c n", p=P)

                load(router[:], split("router_w"))
                load(bias[:], dram["L1_ffn_router_bias"].partition_broadcast(P))
                load(lower[:].rearrange("p a b -> p (a b)"), dram["lower"].partition_broadcast(P))
                for t, name in ((gate, "gate_w"), (up, "up_w")):
                    for c in range(DC):
                        load(t[:, 0:NE, c, :], dram["L1_ffn_" + name][:, c * P:(c + 1) * P, :]
                             .rearrange("e p n -> p e n"))
                        load(t[:, NE:NU, c, :], dram["L1_ffn_s_" + name][c * P:(c + 1) * P, :]
                             .rearrange("p (u n) -> p u n", n=P))
                load(down[:, 0:NE, :], dram["L1_ffn_down_w"].rearrange("e p n -> p e n"))
                load(down[:, NE:NU, :], split("s_down_w"))
                with sp.Fori(0, TURNS) as i:
                    reached(sp, out_sb, i)
                    sp.dma_start(out[:, bass.ds(i * MT, MT), :], acc[:]).then_inc(stored, 16)
                sp.wait_ge(stored, 16 * TURNS)

            @block.gpsimd
            def _(pool):
                pool.memset(norms.half[:], -0.5).then_inc(ready, 1)
                pool.wait_ge(ready, 1)
                with pool.Fori(0, TURNS) as i:
                    do = Chain(pool, pchain, i, POOL_STEPS)
                    norms.root(pool, do, i, 0)
                    do.end()

            @block.scalar
            def _(act):
                with act.Fori(0, TURNS) as i:
                    reached(act, t_ps, i)
                    act.activation(xnT[:].rearrange("p c s -> p (c s)"),
                                   psX[:].rearrange("p t d -> p (t d)"), ACT.Copy
                                   ).then_inc(t_sb.s, 1)
                    reached(act, cen, i)
                    act.activation(score[:], score[:], ACT.Exp).then_inc(exps.s, 1)
                    for u in range(NU):
                        reached(act, g_ps, i, u + 1)
                        if u >= 2:
                            reached(act, a_sb, i, u - 1)
                        act.activation(silu[u % 2][:], psG[u % 2][:], ACT.Silu).then_inc(g_sb.s, 1)

            @block.vector
            def _(dve):
                dve.wait_ge(loaded, 16 * N_LOADS)
                with dve.Fori(0, TURNS) as i:
                    do = Chain(dve, dchain, i, DVE_STEPS)
                    do(dve.tensor_copy(xw[:], core.x[:, bass.ds(i * MT, MT), :]))
                    norms.stats(dve, do, 0, xw)
                    norms.normal(dve, i, 0, xn, xw).then_inc(norm.s, 1)
                    reached(dve, r_ps, i)
                    lg = psD[:, 0, 0:MT * NE].rearrange("p (t e) -> p t e", e=NE)
                    do(dve.tensor_reduce(top[:], lg, AX_X, ALU.max))
                    e8 = [P, MT, NE]
                    dve.tensor_tensor(score[:], lg, top[:].unsqueeze(2).to_broadcast(e8),
                                      ALU.subtract).then_inc(cen.s, 1)
                    reached(dve, exps, i)
                    do(dve.tensor_reduce(total[:], score[:], AX_X, ALU.add))
                    do(dve.reciprocal(total[:], total[:]))
                    do(dve.tensor_tensor(score[:], score[:],
                                         total[:].unsqueeze(2).to_broadcast(e8), ALU.mult))
                    do(dve.tensor_scalar(corr[:], score[:], bias[:, 0:1], None, ALU.add))
                    for t in range(MT):
                        mine = corr[:, t, :].unsqueeze(2).to_broadcast([P, NE, NE])
                        other = corr[:, t, :].unsqueeze(1).to_broadcast([P, NE, NE])
                        do.mark(dve.tensor_tensor(above[:, t, :, :], other, mine, ALU.is_gt))
                        do.mark(dve.tensor_tensor(equal[:, t, :, :], other, mine, ALU.is_equal))
                    do.wait()
                    do(dve.tensor_tensor(equal[:], equal[:],
                                         lower[:].unsqueeze(1).to_broadcast([P, MT, NE, NE]),
                                         ALU.mult))
                    do(dve.tensor_tensor(above[:], above[:], equal[:], ALU.add))
                    do(dve.tensor_reduce(wt[:], above[:], AX_X, ALU.add))
                    do(dve.tensor_scalar(wt[:], wt[:], TOPE - 0.5, None, ALU.is_lt))
                    do(dve.tensor_tensor(wt[:], wt[:], score[:], ALU.mult))
                    do(dve.tensor_reduce(total[:], wt[:], AX_X, ALU.add))
                    do(dve.tensor_scalar(total[:], total[:], 1e-20, None, ALU.add))
                    do(dve.reciprocal(total[:], total[:]))
                    do(dve.tensor_tensor(wt[:], wt[:], total[:].unsqueeze(2).to_broadcast(e8),
                                         ALU.mult))
                    dve.wait_ge(stored, 16 * i)
                    dve.tensor_copy(acc[:], xw[:]).then_inc(weights.s, 1)
                    reached(dve, weights, i)

                    def product(u):
                        reached(dve, g_sb, i, u + 1)
                        dve.tensor_tensor(act_u[u % 2][:], silu[u % 2][:], psU[u % 2][:], ALU.mult
                                          ).then_inc(a_sb.s, 1)

                    product(0)
                    for u in range(NU):
                        if u + 1 < NU:
                            if 1 <= u <= NE:
                                reached(dve, d_ps, i, u)
                            elif u > NE:
                                reached(dve, s_ps, i, u - NE)
                            product(u + 1)
                        if u < NE:
                            reached(dve, d_ps, i, u + 1)
                            for t in range(MT):
                                last = dve.scalar_tensor_tensor(
                                    acc[:, t, :], psD[:, t, :], wt[:, t, u:u + 1], acc[:, t, :],
                                    ALU.mult, ALU.add)
                            last.then_inc(d_sb.s, 1)
                            dve.wait_ge(d_sb.s, i * NE + u + 1)
                    reached(dve, s_ps, i)
                    dve.tensor_tensor(acc[:], acc[:], psX[:], ALU.add).then_inc(out_sb.s, 1)
                    do.end()

            @block.tensor
            def _(pe):
                pe.wait_ge(loaded, 16 * N_LOADS)
                with pe.Fori(0, TURNS) as i:
                    reached(pe, norm, i)
                    released(pe, out_sb, i)
                    px = psX[:].rearrange("p t d -> p (t d)")
                    for c in range(DC):
                        for t in range(MT):
                            last = pe.transpose(px[:, c * MS + t * P:c * MS + (t + 1) * P],
                                                xn[:, t, c * P:(c + 1) * P], core.ident[:])
                    last.then_inc(t_ps.s, 1)
                    reached(pe, t_sb, i)
                    released(pe, d_sb, i)
                    for t in range(MT):
                        for c in range(DC):
                            last = pe.matmul(psD[:, 0, t * NE:(t + 1) * NE],
                                             xnT[:, c, t * P:(t + 1) * P], router[:, c, :],
                                             start=(c == 0), stop=(c == DC - 1))
                    last.then_inc(r_ps.s, 1)

                    def gate_up(u):
                        if u >= 2:
                            reached(pe, a_sb, i, u - 1)
                        for w, o in ((gate, psG), (up, psU)):
                            for c in range(DC):
                                last = pe.matmul(o[u % 2][:], w[:, u, c, :], xnT[:, c, :],
                                                 start=(c == 0), stop=(c == DC - 1))
                        last.then_inc(g_ps.s, 1)

                    def down_product(u):
                        reached(pe, a_sb, i, u + 1)
                        if u < NE:
                            if u == 0:
                                reached(pe, weights, i)
                            else:
                                reached(pe, d_sb, i, u)
                        for t in range(MT):
                            if u < NE:
                                last = pe.matmul(psD[:, t, :], act_u[u % 2][:, t * P:(t + 1) * P],
                                                 down[:, u, :], start=True, stop=True)
                            else:
                                last = pe.matmul(psX[:, t, :], act_u[u % 2][:, t * P:(t + 1) * P],
                                                 down[:, u, :], start=(u == NE and t % 2 == 0),
                                                 stop=(u == NU - 1), skip_group_check=True)
                        last.then_inc(d_ps.s if u < NE else s_ps.s, 1)

                    gate_up(0)
                    for u in range(1, NU):
                        gate_up(u)
                        down_product(u - 1)
                    down_product(NU - 1)


def program(nc, dram):
    with ExitStack() as ctx:
        core = Core(nc, ctx, dram)
        with ExitStack() as first:
            kr = core.sb(first, "kernel_re", [P, 2, D])
            ki = core.sb(first, "kernel_im", [P, 2, D])
            core.phase(spectrum, first, kr, ki)
            core.phase(first_attention, first, kr, ki)
        with ExitStack() as ffn:
            xn_keep = core.sb(ffn, "xn_keep", [P, NT, D])
            with ExitStack() as qkv:
                slots = core.sb(qkv, "qkv_slots", [P, NT, 3], I32)
                tile_group = core.sb(qkv, "qkv_tile_group", [P, 3, TILES], I32)
                results = core.sb(qkv, "qkv_results", [P, 3, NT, D])
                with ExitStack() as placing:
                    rows = core.sb(placing, "qkv_rows", [P, 3, NT, XW])
                    groups = core.sb(placing, "qkv_groups", [P, NT, 3, NG], BF16)
                    core.phase(route_qkv, placing, rows, xn_keep, groups)
                    core.phase(place_tokens, "pq", groups[:].rearrange("p t f g -> p (t f g)"), 3, 0,
                                 slots, tile_group)
                    core.phase(group_products, "gq", 3, rows, slots,
                                   tile_group[:].rearrange("p f t -> p (f t)"),
                                   [core.sorted_x[f] for f in "qkv"],
                                   [core.sorted_y[f] for f in "qkv"], results)
                rows = core.sb(qkv, "f_rows", [P, 1, NT, XW])
                groups = core.sb(qkv, "f_groups", [P, NT, NG], BF16)
                core.phase(token_attention, results, xn_keep, rows, groups)
                core.phase(place_tokens, "pf", groups[:].rearrange("p t g -> p (t g)"), 1, 3,
                             slots[:, :, 0:1], tile_group[:, 0:1, :])
                core.phase(group_products, "gf", 1, rows, slots,
                               tile_group[:].rearrange("p f t -> p (f t)"),
                               [core.sorted_x["f"]], [core.sorted_y["f"]], results, gelu=True)
                core.phase(second_attention, results)
        core.phase(moe)


_OUT_SHAPE = (B, S, D)


def _layout(inputs):
    a = {k: np.ascontiguousarray(v) for k, v in inputs.items()}

    def halves(m):
        return np.ascontiguousarray(m.T.reshape(NSTATE, 2, D // 2).transpose(1, 0, 2)
                                    .reshape(P, D // 2))

    for n in ("A_re", "A_im", "C_re", "C_im"):
        a[n + "T"] = halves(a.pop("L0_xattn_" + n))
    a["ctxT"] = np.ascontiguousarray(a.pop("ctx_768").transpose(0, 2, 1))
    for f in "qkvf":
        a[f"L0_ffn_{f}_nwT"] = np.ascontiguousarray(a.pop(f"L0_ffn_{f}_nw").T)
    gw1, gw2, gb2 = [], [], []
    for f in "qkvf":
        w1 = a.pop(f"L0_ffn_{f}_w1").reshape(NG, GL, DC, P, LW).transpose(0, 3, 2, 1, 4)
        b1 = a.pop(f"L0_ffn_{f}_b1").reshape(NG, GH // P, P).transpose(0, 2, 1)
        gw1.append(np.concatenate([w1.reshape(NG * P, DC * GH), b1.reshape(NG * P, GH // P)], 1))
        gw2.append(a.pop(f"L0_ffn_{f}_w2").reshape(NG, GH // P, P, D).transpose(0, 2, 1, 3)
                   .reshape(NG * P, GH // P * D))
        gb2.append(a.pop(f"L0_ffn_{f}_b2"))
    a["group_w1"], a["group_w2"], a["group_b2"] = (np.concatenate(v) for v in (gw1, gw2, gb2))
    def columns(v):
        return np.ascontiguousarray(v.reshape(-1, P).T)

    for n in ("L0_xattn_g_ffn", "L0_xattn_b_ffn", "L0_xattn_b1", "mask_BxS_bf1"):
        a[n] = columns(a[n])
    def padded(w):
        out = np.zeros((w.shape[0], H1, 32), w.dtype)
        out[:, :, 0:DH1] = w.reshape(-1, H1, DH1)
        return out.reshape(-1, H1 * 32)

    for n in "qk":
        a["c_w" + n] = padded(a.pop("L1_xattn_w" + n))
        a["c_b" + n] = columns(padded(a.pop("L1_xattn_b" + n)[None, :]))
    for n in ("mask_BxS_bf1", "mask_BxS2_bf1"):
        a[n] = a[n].view(np.uint8)
    for n in ("L0_xattn_mod_gate", "L1_ffn_router_bias"):
        a[n] = a[n].reshape(1)
    return a


def _tables():
    w = 2 * np.pi * (np.arange(S) + 0.5) / (2 * S)
    t = np.arange(S)
    ang = w[:, None] * t[None, :]
    fwd = np.stack([np.cos(ang), -np.sin(ang)])
    dft = fwd.transpose(2, 0, 1).reshape(ST, P, 2, S).transpose(1, 0, 2, 3)
    kd = fwd.transpose(2, 0, 1).reshape(NA, NCP, 2, S) * (2.0 * 2.0 / (2 * S))
    idft = fwd.transpose(1, 0, 2).reshape(2, P, 2, S).transpose(1, 0, 2, 3)
    leaf_units = np.repeat(np.eye(GL), LW, axis=1)
    tri = np.triu(np.ones((P, P)), 1)
    counts = np.concatenate([P * np.arange(NT), np.arange(TILES),
                             np.tril(np.ones((NG, NG)), -1).ravel()])
    sel = np.zeros((4, 32, QC, P))
    for c in range(QC):
        sel[:, [c, QC + c], c, :] = 1
    lower = np.tril(np.ones((NE, NE)), -1).ravel()
    return {"lower": lower, "c_sel": sel.reshape(P, QC, P), "leaf_units": leaf_units, "tri": tri, "counts": counts, "dft": dft, "kernel_dft": kd, "idft": idft}


def kernel(**inputs):
    import concourse.bacc as _bacc
    from concourse import mybir as _mybir
    from concourse.bass_utils import run_bass_kernel_spmd as _run

    nc = _bacc.Bacc("TRN2", target_bir_lowering=False, num_devices=1)
    arrays = _layout(inputs)
    arrays.update({k: np.ascontiguousarray(v, dtype=np.float32) for k, v in _tables().items()})
    dram = {}
    feed = {}
    for name, a in arrays.items():
        feed[f"in_{name}"] = a
        dram[name] = nc.dram_tensor(f"in_{name}", a.shape, _mybir.dt.from_np(a.dtype),
                                    kind="ExternalInput").ap()
    dram["out"] = nc.dram_tensor("out_0", _OUT_SHAPE, F32, kind="ExternalOutput").ap()
    program(nc, dram)
    r = _run(nc, [feed], core_ids=[0])
    return r.results[0]["out_0"]
```

```python
from contextlib import ExitStack

import numpy as np

import concourse.bass as bass
from concourse import mybir

ALU = mybir.AluOpType
ACT = mybir.ActivationFunctionType
AX_X = mybir.AxisListType.X
F32 = mybir.dt.float32
BF16 = mybir.dt.bfloat16
I32 = mybir.dt.int32
U8 = mybir.dt.uint8

P = 128
B = 8
S = 256
D = 256
DCTX = 192
CP = DCTX // 2
ST = S // P
DC = D // P
NT = B * ST
H0, DH0, TOPK = 4, 32, 32
HID = 4 * D
HC = HID // P
NSTATE = 64
NA, NCP = 32, 8
NEG_MASK = -1e30
NEG_TAKEN = -3e38
EPS = 1e-5
NN, NL, LW, DEPTH = 255, 256, 16, 8
FH = NL * LW
FC = FH // P
H1, DH1 = 16, 16
NE, EI, TOPE = 8, 128, 4
SI = 512

LOG2E = 1.4426950408889634
LN2_HI, LN2_LO = 0.693145751953125, 1.42860682030941723e-6
ROUND = 12582912.0
INV_2PI = 0.15915494309189535
PI2_A, PI2_B = 6.28125, 0.0019340515136718750
PI2_C = 6.283185307179586 - PI2_A - PI2_B


class Signal:

    def __init__(self, handle, per=1):
        self.s = handle
        self.per = per


def reached(eng, signal, i, k=None):
    eng.wait_ge(signal.s, i * signal.per + (signal.per if k is None else k))


def reached_apart(eng, signal, i, k=None):
    wait_apart(eng, signal.s, i * signal.per + (signal.per if k is None else k))


def released(eng, signal, i):
    eng.wait_ge(signal.s, i * signal.per)


def wait_apart(eng, handle, value):
    eng.to_reg(value)
    eng.wait_ge(handle, 1)
    eng.wait_ge(handle, value)


def in_turns(eng, step):
    with eng.Fori(0, B - 1) as i:
        step(i, i + 1)
    step(B - 1, None)


class Chain:

    def __init__(self, eng, handle, turn=0, per=0):
        self.eng, self.s, self.base, self.per, self.n = eng, handle, turn * per, per, 0

    def mark(self, ins):
        self.n += 1
        ins.then_inc(self.s, 1)
        return self.n

    def wait(self, n=None):
        self.eng.wait_ge(self.s, self.base + (self.n if n is None else n))

    def __call__(self, ins):
        self.mark(ins)
        self.wait()

    def wait_apart(self):
        wait_apart(self.eng, self.s, self.base + self.n)

    def end(self):
        assert self.n == self.per, f"the turn has {self.n} steps"
GL = 16
NG = NL // GL
GH = GL * LW
TMAX = (B * S + NG * (P - 1)) // P
TILES = TMAX + -TMAX % 4
PLACES = TILES * P
W1COLS = DC * GH + GH // P
XW = D + GL
ZERO_FILLS = 4


class Core:

    def __init__(self, nc, ctx, dram):
        self.nc, self.ctx, self.dram, self.own = nc, ctx, dram, []
        self.x = self.sb(ctx, "x_tokens", [P, NT, D])
        self.ctxT = self.sb(ctx, "ctx_T", [CP, 2, B * S])
        self.ident = self.sb(ctx, "identity", [P, P])
        self.ones = self.sb(ctx, "ones_row", [P, P])
        self.ones_bf = self.sb(ctx, "ones_row_bf16", [P, P], BF16)
        self.minus_half = self.sb(ctx, "minus_half", [P, ST])
        self.plus_half = self.sb(ctx, "plus_half", [P, ST])
        self.loads = [self.sem("x_loaded"), self.sem("ctx_loaded")]
        self.setup = self.sem("constants_set")
        self.zeroed = self.sem("places_zeroed")
        self.sorted_x = {f: nc.dram_tensor(f"sorted_x_{f}", (PLACES, XW), F32, kind="Internal").ap()
                         for f in "qkvf"}
        self.sorted_y = {f: nc.dram_tensor(f"sorted_y_{f}", (PLACES, D), F32, kind="Internal").ap()
                         for f in "qkvf"}
        self.zero = self.sb(ctx, "zero_row", [P, XW])

    def sb(self, ctx, name, shape, dt=F32):
        return ctx.enter_context(self.nc.sbuf_tensor(name, shape, dt))

    def ps(self, ctx, name, shape, dt=F32):
        return ctx.enter_context(self.nc.psum_tensor(name, shape, dt))

    def sem(self, name):
        handle = self.nc.alloc_semaphore(name=name)
        self.own.append(handle)
        return handle

    def phase(self, stage, *args, **kwargs):
        self.own = []
        stage(self, *args, **kwargs)
        self.nc.clear_and_free_semaphores(self.own)
        self.nc.all_engine_barrier()

    def flag(self, name, per=1):
        return Signal(self.sem(name), per)


def row(ap):
    return ap.rearrange("(a n) -> a n", a=1)


def rstd_of(pool, steps, out, var, minus_half):
    steps(pool.tensor_scalar(out, var, EPS, None, ALU.add))
    return pool.tensor_tensor(out, out, minus_half, ALU.pow)


def spectrum(core, ctx, kr, ki):
    nc, dram = core.nc, core.dram
    with ExitStack() as own:
        HD = D // 2
        logdt = core.sb(own, "s4_logdt", [P, HD])
        are = core.sb(own, "s4_A_re", [P, HD])
        aim = core.sb(own, "s4_A_im", [P, HD])
        cre = core.sb(own, "s4_C_re", [P, HD])
        cim = core.sb(own, "s4_C_im", [P, HD])
        dskip = core.sb(own, "s4_D_skip", [1, D])
        kdft = core.sb(own, "s4_kernel_dft", [NA, NCP, 2, S])
        tmp = [core.sb(own, f"s4_t{n}", [P, HD]) for n in range(8)]
        tint = core.sb(own, "s4_int", [P, HD], I32)
        dt = core.sb(own, "s4_dt", [P, HD])
        ea = core.sb(own, "s4_exp_a", [P, HD])
        em1 = core.sb(own, "s4_expm1_a", [P, HD])
        s_half = core.sb(own, "s4_sin_half", [P, HD])
        s_quart = core.sb(own, "s4_sin_quarter", [P, HD])
        bhalf = core.sb(own, "s4_b_half", [P, HD])
        dcr = core.sb(own, "s4_dC_re", [P, HD])
        dci = core.sb(own, "s4_dC_im", [P, HD])
        zr = core.sb(own, "s4_Z_re", [P, NCP, HD])
        zi = core.sb(own, "s4_Z_im", [P, NCP, HD])
        gr = core.sb(own, "s4_G_re", [P, NCP, HD])
        gi = core.sb(own, "s4_minus_G_im", [P, NCP, HD])
        wr = core.sb(own, "s4_W_re", [P, NA, HD])
        wi = core.sb(own, "s4_W_im", [P, NA, HD])
        sq = [core.sb(own, f"s4_square{n}", [P, 2, HD]) for n in range(2)]
        part = [core.sb(own, f"s4_product{n}", [P, NA // 2, HD]) for n in range(2)]
        ksb = core.sb(own, "s4_K", [NA, D, NCP])
        pk = core.ps(own, "s4_K_ps", [NA, 2, HD * NCP])
        pf = core.ps(own, "s4_spectrum_ps", [P, 2, 2 * S])
        zero = core.zero
        loaded, chain = core.sem("s4_loaded"), core.sem("s4_steps")
        asked, given = core.sem("s4_act_asked"), core.sem("s4_act_given")
        tables, kdone, kevac, fdone = (core.sem(f"s4_{n}") for n in ("tables", "k", "k_evac", "f"))

        with nc.Block() as block:
            @block.sync
            def _(sp):
                for h in range(2):
                    sp.dma_start(logdt[64 * h:64 * h + 64, :],
                                 dram["L0_xattn_log_dt"][h * HD:(h + 1) * HD]
                                 .partition_broadcast(64)).then_inc(loaded, 16)
                for t, name in ((are, "A_reT"), (aim, "A_imT"), (cre, "C_reT"), (cim, "C_imT")):
                    sp.dma_start(t[:], dram[name]).then_inc(loaded, 16)
                sp.dma_start(dskip[:], row(dram["L0_xattn_D_skip"])).then_inc(loaded, 16)
                sp.dma_start(kdft[:], dram["kernel_dft"]).then_inc(loaded, 16)
                sp.dma_start(core.x[:], dram["x"].rearrange("b (t p) d -> p (b t) d", p=P)
                             ).then_inc(core.loads[0], 16)
                for c in range(2):
                    sp.dma_start(core.ctxT[:, c, :].rearrange("p (b s) -> p b s", b=B),
                                 dram["ctxT"][:, c * CP:(c + 1) * CP, :].rearrange("b p s -> p b s")
                                 ).then_inc(core.loads[1], 16)

                sp.wait_ge(core.setup, 6)
                for t in core.sorted_x.values():
                    sp.dma_start(t.rearrange("(p r) c -> p r c", p=P),
                                 zero[:].unsqueeze(1).to_broadcast([P, TILES, XW])
                                 ).then_inc(core.zeroed, 16)

            @block.gpsimd
            def _(pool):
                pool.memset(zero[:], 0.0).then_inc(core.setup, 1)
                pool.memset(core.ident[:], 0.0).then_inc(core.setup, 1)
                pool.memset(core.ones[:], 1.0).then_inc(core.setup, 1)
                pool.memset(core.ones_bf[:], 1.0).then_inc(core.setup, 1)
                pool.memset(core.minus_half[:], -0.5).then_inc(core.setup, 1)
                pool.memset(core.plus_half[:], 0.5).then_inc(core.setup, 1)
                pool.wait_ge(core.setup, 6)
                pool.affine_select(out=core.ident[:], in_=core.ident[:], compare_op=ALU.not_equal,
                                   fill=1.0, base=0, pattern=[[-1, P]], channel_multiplier=1
                                   ).then_inc(core.setup, 1)

            @block.scalar
            def _(act):
                act.wait_ge(asked, 1)
                act.activation(em1[:], tmp[6][:], ACT.Tanh, scale=0.5).then_inc(given, 1)
                act.wait_ge(asked, 2)
                act.activation(s_half[:], bhalf[:], ACT.Sin).then_inc(given, 1)
                act.activation(s_quart[:], bhalf[:], ACT.Sin, scale=0.5).then_inc(given, 1)

            @block.vector
            def _(dve):
                do = Chain(dve, chain)

                def exp(out, x):
                    c, n, r, p = (t[:] for t in tmp[:4])
                    do(dve.tensor_scalar(c, x, -87.0, 88.0, ALU.max, ALU.min))
                    do(dve.tensor_scalar(n, c, LOG2E, ROUND, ALU.mult, ALU.add))
                    do(dve.tensor_scalar(n, n, ROUND, None, ALU.subtract))
                    do(dve.scalar_tensor_tensor(r, n, -LN2_HI, c, ALU.mult, ALU.add))
                    do(dve.scalar_tensor_tensor(r, n, -LN2_LO, r, ALU.mult, ALU.add))
                    do(dve.tensor_scalar(p, r, 1 / 5040, 1 / 720, ALU.mult, ALU.add))
                    for k in (1 / 120, 1 / 24, 1 / 6, 0.5, 1.0, 1.0):
                        do(dve.tensor_tensor(p, p, r, ALU.mult))
                        do(dve.tensor_scalar(p, p, k, None, ALU.add))
                    do(dve.tensor_scalar(tint[:], n, 127.0, float(1 << 23), ALU.add, ALU.mult))
                    do(dve.tensor_tensor(out, p, tint[:].bitcast(F32), ALU.mult))

                def cmul(outr, outi, ar, ai, br, bi, t0, t1):
                    do(dve.tensor_tensor(t0, ar, br, ALU.mult))
                    do(dve.tensor_tensor(t1, ai, bi, ALU.mult))
                    do(dve.tensor_tensor(outr, t0, t1, ALU.subtract))
                    do(dve.tensor_tensor(t0, ar, bi, ALU.mult))
                    do(dve.tensor_tensor(t1, ai, br, ALU.mult))
                    do(dve.tensor_tensor(outi, t0, t1, ALU.add))

                dve.wait_ge(loaded, 16 * 8)
                exp(dt[:], logdt[:])
                a, b = tmp[6][:], tmp[7][:]
                do(dve.tensor_tensor(a, dt[:], are[:], ALU.mult))
                dve.tensor_tensor(b, dt[:], aim[:], ALU.mult).then_inc(asked, 1)
                dve.wait_ge(asked, 1)
                exp(ea[:], a)
                n, r = tmp[0][:], bhalf[:]
                do(dve.tensor_scalar(b, b, 0.5, None, ALU.mult))
                do(dve.tensor_scalar(n, b, INV_2PI, ROUND, ALU.mult, ALU.add))
                do(dve.tensor_scalar(n, n, ROUND, None, ALU.subtract))
                do(dve.scalar_tensor_tensor(r, n, -PI2_A, b, ALU.mult, ALU.add))
                do(dve.scalar_tensor_tensor(r, n, -PI2_B, r, ALU.mult, ALU.add))
                do(dve.scalar_tensor_tensor(r, n, -PI2_C, r, ALU.mult, ALU.add))
                dve.tensor_scalar(r, r, 3.1415925, -3.1415925, ALU.min, ALU.max).then_inc(asked, 1)
                dve.wait_ge(given, 3)
                do(dve.scalar_tensor_tensor(em1[:], ea[:], 1.0, em1[:], ALU.add, ALU.mult))
                sh, sq_, cm1, cosb, sinb, er, ei, den = (t[:] for t in tmp)
                do(dve.tensor_tensor(sq_, s_quart[:], s_quart[:], ALU.mult))
                do(dve.tensor_scalar(sh, sq_, -2.0, 1.0, ALU.mult, ALU.add))
                do(dve.scalar_tensor_tensor(sinb, s_half[:], 2.0, sh, ALU.mult, ALU.mult))
                do(dve.scalar_tensor_tensor(cm1, s_half[:], -2.0, s_half[:], ALU.mult, ALU.mult))
                do(dve.tensor_scalar(cosb, cm1, 1.0, None, ALU.add))
                do(dve.tensor_tensor(zr[:, 1, :], ea[:], cosb, ALU.mult))
                do(dve.tensor_tensor(zi[:, 1, :], ea[:], sinb, ALU.mult))
                do(dve.tensor_tensor(er, em1[:], cosb, ALU.mult))
                do(dve.tensor_tensor(er, er, cm1, ALU.add))
                do(dve.tensor_tensor(den, are[:], are[:], ALU.mult))
                do(dve.tensor_tensor(sh, aim[:], aim[:], ALU.mult))
                do(dve.tensor_tensor(den, den, sh, ALU.add))
                do(dve.reciprocal(den, den))
                do(dve.tensor_tensor(sh, er, are[:], ALU.mult))
                do(dve.tensor_tensor(sq_, zi[:, 1, :], aim[:], ALU.mult))
                do(dve.tensor_tensor(sh, sh, sq_, ALU.add))
                do(dve.tensor_tensor(ei, zi[:, 1, :], are[:], ALU.mult))
                do(dve.tensor_tensor(sq_, er, aim[:], ALU.mult))
                do(dve.tensor_tensor(ei, ei, sq_, ALU.subtract))
                do(dve.tensor_tensor(er, sh, den, ALU.mult))
                do(dve.tensor_tensor(ei, ei, den, ALU.mult))
                cmul(dcr[:], dci[:], cre[:], cim[:], er, ei, sh, sq_)

                def powers(tr, ti, count, base):
                    br, bi = base
                    have, cur = 1, 0
                    while have < count:
                        s = sq[cur]
                        if have == 1:
                            do(dve.tensor_copy(tr[:, 1, :], br))
                            do(dve.tensor_copy(ti[:, 1, :], bi))
                            br, bi = tr[:, 1, :], ti[:, 1, :]
                        else:
                            wide = [P, have, HD]
                            cmul(tr[:, have:2 * have, :], ti[:, have:2 * have, :],
                                 tr[:, 0:have, :], ti[:, 0:have, :],
                                 br.unsqueeze(1).to_broadcast(wide),
                                 bi.unsqueeze(1).to_broadcast(wide),
                                 part[0][:, 0:have, :], part[1][:, 0:have, :])
                        have *= 2
                        cmul(s[:, 0, :], s[:, 1, :], br, bi, br, bi, sh, sq_)
                        br, bi = s[:, 0, :], s[:, 1, :]
                        cur = 1 - cur
                    return br, bi

                for t in (zr, wr):
                    do(dve.memset(t[:, 0, :], 1.0))
                for t in (zi, wi):
                    do(dve.memset(t[:, 0, :], 0.0))
                do(dve.tensor_copy(cosb, zr[:, 1, :]))
                do(dve.tensor_copy(sinb, zi[:, 1, :]))
                z8 = powers(zr, zi, NCP, (cosb, sinb))
                wide = [P, NCP, HD]
                t0, t1 = part[0][:, 0:NCP, :], part[1][:, 0:NCP, :]
                cr, ci = (t[:].unsqueeze(1).to_broadcast(wide) for t in (dcr, dci))
                cmul(gr[:], gi[:], zr[:], zi[:], cr, ci, t0, t1)
                do(dve.tensor_scalar(gi[:], gi[:], -1.0, None, ALU.mult))
                do(dve.tensor_copy(cosb, z8[0]))
                do(dve.tensor_copy(sinb, z8[1]))
                powers(wr, wi, NA, (cosb, sinb))
                dve.tensor_copy(sh, sq_).then_inc(tables, 1)
                dve.wait_ge(kdone, 1)
                for h in range(2):
                    do(dve.tensor_copy(ksb[:, h * HD:(h + 1) * HD, :],
                                       pk[:, h, :].rearrange("a (d c) -> a d c", c=NCP)))
                k0 = ksb[0:1, :, 0]
                dve.scalar_tensor_tensor(k0, dskip[:], 0.5, k0, ALU.mult, ALU.add
                                         ).then_inc(kevac, 1)
                dve.wait_ge(fdone, 1)
                do(dve.tensor_copy(kr[:].rearrange("p k d -> p (k d)"), pf[:, 0, :]))
                do(dve.tensor_copy(ki[:].rearrange("p k d -> p (k d)"), pf[:, 1, :]))

            @block.tensor
            def _(pe):
                pe.wait_ge(tables, 1)
                for d in range(HD):
                    for h in range(2):
                        q = slice(64 * h, 64 * h + 64)
                        o = pk[:, h, d * NCP:(d + 1) * NCP]
                        pe.matmul(o, wr[q, :, d], gr[q, :, d], start=True, stop=False)
                        last = pe.matmul(o, wi[q, :, d], gi[q, :, d], start=False, stop=True)
                last.then_inc(kdone, 1)
                pe.wait_ge(kevac, 1)
                for comp in range(2):
                    for kc in range(2):
                        for c in range(NCP):
                            last = pe.matmul(pf[:, comp, kc * D:(kc + 1) * D],
                                             kdft[:, c, comp, kc * P:(kc + 1) * P], ksb[:, :, c],
                                             start=(c == 0), stop=(c == NCP - 1))
                last.then_inc(fdone, 1)


def first_attention(core, ctx, kr, ki):
    nc, dram = core.nc, core.dram
    with ExitStack() as own:
        def sb(name, shape, dt=F32):
            return core.sb(own, "a_" + name, shape, dt)

        wq = sb("wq", [P, DC, P])
        wk = sb("wk", [CP, 2, P])
        wv = sb("wv", [CP, 2, D])
        film = [sb("film_in", [P, DC, 2 * D]), sb("film_out", [P, DC, 2 * D])]
        film_b = [sb("film_in_b", [P, 2 * D]), sb("film_out_b", [P, 2 * D])]
        gate = sb("mod_gate", [P, 1])
        g_in, b_in = sb("g_in", [P, D]), sb("b_in", [P, D])
        g_out, b_out = sb("g_out", [P, D]), sb("b_out", [P, D])
        g_ffn, b_ffn = sb("g_ffn", [P, DC]), sb("b_ffn", [P, DC])
        w1, b1 = sb("w1", [P, DC, HID]), sb("b1", [P, HC])
        w2, b2 = sb("w2", [P, HC, D]), sb("b2", [P, D])
        dft, idft = sb("dft", [P, ST, 2, S]), sb("idft", [P, 2, 2, S])
        vmask8, vmask = sb("vmask8", [P, B * S], U8), sb("vmask", [P, B * S], BF16)
        tmask8, tmask = sb("tmask8", [P, NT], U8), sb("tmask", [P, NT])
        ctxw = sb("ctx", [CP, 2, S])
        maskw = sb("mask", [P, S], BF16)
        x_st, x_mv = sb("x_stats", [P, ST, 6]), sb("x_mean_var", [P, ST, 2])
        x_rstd, x_var2 = sb("x_rstd", [P, 2, ST]), sb("x_norm_var", [P, ST])
        st, mv = sb("stats", [P, ST, 6]), sb("mean_var", [P, 2, ST, 2])
        rstd = sb("rstd", [P, 2, ST])
        xn, xnT = sb("xn", [P, ST, D]), sb("xnT", [P, DC, S])
        u, xr = sb("u", [P, ST, D]), sb("residual", [P, ST, D])
        xn_back, u_back = sb("xn_back", [P, ST, D]), sb("u_back", [P, ST, D])
        qk = sb("qk", [P, 2, S])
        v = sb("v", [P, ST, D])
        score = sb("score", [P, H0 * ST, S])
        rest = sb("rest", [P, H0 * ST, S])
        top = sb("top", [P, H0 * ST, TOPK])
        nmax = sb("nmax", [P, H0 * ST])
        prob = sb("prob", [P, H0 * ST, S])
        etop, esum = sb("etop", [P, H0 * ST, TOPK]), sb("esum", [P, H0 * ST])
        mean = sb("mean", [P, ST, S])
        attnT, ctT = sb("attnT", [P, ST, S]), sb("ctT", [P, DC, S])
        f_in, f_out = sb("f_in", [P, ST, 2 * D]), sb("f_out", [P, ST, 2 * D])
        x1 = sb("x1", [P, ST, D])
        spec = sb("spec", [P, 2, 2 * S])
        prod = sb("prod", [P, 4, 2 * S])
        yspec = sb("yspec", [P, 2, 2 * S])
        xt = sb("xt", [P, ST, D])
        hT = sb("hT", [P, DC, S])
        act1 = sb("act1", [P, HC, S])
        pS = core.ps(own, "a_scores", [P, H0, ST, S])
        pT = core.ps(own, "a_psT", [P, DC, S])
        pA = core.ps(own, "a_psA", [P, 2, S])
        pB = core.ps(own, "a_psB", [P, 2 * D])
        pC = core.ps(own, "a_psC", [P, 2 * D])

        loaded, late = core.sem("a_loaded"), core.sem("a_late_loaded")
        ready = core.sem("a_ready")
        sig = core.flag
        x_var, x_rs = sig("a_x_var"), sig("a_x_rstd")
        ctx_in, norm, u_ready = sig("a_ctx_in", 2), sig("a_norm"), sig("a_u")
        xT_ps, xT_sb = sig("a_xT_ps"), sig("a_xT_sb")
        proj_ps, proj_sb = sig("a_proj_ps", 2), sig("a_proj_sb", 2)
        scores, score_sb = sig("a_scores_ready"), sig("a_scores_sb")
        first8, taken = sig("a_max_ready"), sig("a_taken")
        exps, sums, xn_kept, mean_sb = sig("a_exps"), sig("a_sums"), sig("a_xn_kept"), sig("a_mean")
        var_b, rs_b = sig("a_var_b", 2), sig("a_rstd_b", 2)
        at_ps, at_sb = sig("a_at_ps"), sig("a_at_sb")
        ct_ps, ct_sb = sig("a_ct_ps"), sig("a_ct_sb")
        film_ps, film_sb = sig("a_film_ps", 4), sig("a_film_sb", 4)
        x1_ready = sig("a_x1")
        spec_ps, spec_sb = sig("a_spec_ps"), sig("a_spec_sb")
        yi_ready, yr_ready = sig("a_yi"), sig("a_yr")
        y_ps, xt_pre, xt_ready = sig("a_y_ps"), sig("a_xt_pre"), sig("a_xt")
        h_norm, resid = sig("a_h_norm"), sig("a_resid")
        hT_ps, hT_sb = sig("a_hT_ps"), sig("a_hT_sb")
        u_ps, u_act = sig("a_up_ps", HC), sig("a_up_act", HC)
        dn_ps, dn_sb, done = sig("a_down_ps"), sig("a_down_sb"), sig("a_done")
        fchain, bchain, pfchain, pbchain = (core.sem("a_" + n) for n in (
            "dve_front", "dve_back", "pool_front", "pool_back"))
        TOP_STEPS = TOPK // 8 * H0 * ST + (TOPK // 8 - 1) * H0 * ST
        FRONT_STEPS, BACK_STEPS = TOP_STEPS + ST + 6, 2 * ST + 6
        POOL_FRONT, POOL_BACK = 7, 5
        N_LOADS, N_LATE = 16, 6

        with nc.Block() as block:
            @block.sync
            def _(sp):
                def load(out, in_, signal=loaded):
                    sp.dma_start(out, in_).then_inc(signal, 16)

                def split(name, p=P):
                    return dram["L0_xattn_" + name].rearrange("(c p) n -> p c n", p=p)

                def spread(name, n=P):
                    return dram["L0_xattn_" + name].partition_broadcast(n)

                load(wq[:], split("Wq"))
                load(wk[:], split("Wk", CP))
                load(wv[:], split("Wv", CP))
                load(vmask8[:], dram["mask_BxS2_bf1"].rearrange("b s -> (b s)")
                     .partition_broadcast(P))
                load(tmask8[:], dram["mask_BxS_bf1"])
                load(gate[:], spread("mod_gate"))
                for n, name in enumerate(("b_film_in", "b_film_out")):
                    load(film_b[n][:], spread(name))
                for t, name in ((g_in, "g_norm_in"), (b_in, "b_norm_in"), (g_out, "g_norm_out"),
                                (b_out, "b_norm_out"), (b2, "b2")):
                    load(t[:], spread(name))
                for t, name in ((g_ffn, "g_ffn"), (b_ffn, "b_ffn"), (b1, "b1")):
                    load(t[:], dram["L0_xattn_" + name])
                for n, name in enumerate(("W_film_in", "W_film_out")):
                    load(film[n][:], split(name), late)
                load(dft[:], dram["dft"], late)
                load(idft[:], dram["idft"], late)
                load(w1[:], split("W1"), late)
                load(w2[:], split("W2"), late)

            @block.gpsimd
            def _(pool):
                wide = [P, ST, D]

                def root(do, signal, signal_rs, b, n, k):
                    reached_apart(pool, signal, b, k)
                    rstd_of(pool, do, rstd[:, n, :], mv[:, n, :, 1], core.minus_half[:]
                            ).then_inc(signal_rs.s, 1)

                def front_factors(do, b):
                    reached_apart(pool, x_var, b)
                    r1, r2 = x_rstd[:, 0, :], x_rstd[:, 1, :]
                    do(rstd_of(pool, do, r1, x_mv[:, :, 1], core.minus_half[:]))
                    do(pool.tensor_tensor(x_var2[:], x_mv[:, :, 1], r1, ALU.mult))
                    do.mark(pool.tensor_tensor(x_var2[:], x_var2[:], r1, ALU.mult))
                    do.wait_apart()
                    do(rstd_of(pool, do, r2, x_var2[:], core.minus_half[:]))
                    pool.tensor_tensor(r2, r2, r1, ALU.mult).then_inc(x_rs.s, 1)

                def front_context(b):
                    released(pool, proj_ps, b)
                    released(pool, scores, b)
                    pool.tensor_copy(maskw[:], vmask[:, bass.ds(b * S, S)]).then_inc(ctx_in.s, 1)
                    pool.tensor_copy(ctxw[:], core.ctxT[:, :, bass.ds(b * S, S)]
                                     ).then_inc(ctx_in.s, 1)

                def front_kept(do, b):
                    reached(pool, norm, b)
                    released(pool, x1_ready, b)
                    released(pool, xt_pre, b)
                    do(pool.tensor_tensor(u_back[:], u[:], g_in[:].unsqueeze(1)
                                          .to_broadcast(wide), ALU.mult))
                    pool.tensor_tensor(u_back[:], u_back[:], b_in[:].unsqueeze(1)
                                       .to_broadcast(wide), ALU.add).then_inc(u_ready.s, 1)
                    pool.tensor_copy(xn_back[:], xn[:]).then_inc(xn_kept.s, 1)
                    do.end()


                def step(i, b):
                    do = Chain(pool, pbchain, i, POOL_BACK)
                    if b is not None:
                        front = Chain(pool, pfchain, b, POOL_FRONT)
                    if b is not None:
                        front_factors(front, b)
                        front_context(b)
                    reached(pool, film_sb, i)
                    reached(pool, xn_kept, i)
                    pool.tensor_tensor(f_out[:, :, D:2 * D], f_out[:, :, D:2 * D], xn_back[:],
                                       ALU.add).then_inc(xt_pre.s, 1)
                    if b is not None:
                        front_kept(front, b)
                    reached(pool, spec_sb, i)
                    k_re = kr[:].rearrange("p k d -> p (k d)")
                    k_im = ki[:].rearrange("p k d -> p (k d)")
                    do.mark(pool.tensor_tensor(prod[:, 2, :], spec[:, 0, :], k_im, ALU.mult))
                    do(pool.tensor_tensor(prod[:, 3, :], spec[:, 1, :], k_re, ALU.mult))
                    released(pool, y_ps, i)
                    pool.tensor_tensor(yspec[:, 1, :], prod[:, 2, :], prod[:, 3, :], ALU.add
                                       ).then_inc(yi_ready.s, 1)
                    root(do, var_b, rs_b, i, 0, 1)
                    reached(pool, xt_ready, i)
                    released(pool, done, i)
                    do(pool.tensor_tensor(xr[:], xt[:], b2[:].unsqueeze(1).to_broadcast(wide),
                                          ALU.add))
                    x_i = core.x[:, bass.ds(i * ST, ST), :]
                    pool.tensor_tensor(x_i, x_i, b_out[:].unsqueeze(1).to_broadcast(wide),
                                       ALU.add).then_inc(resid.s, 1)
                    root(do, var_b, rs_b, i, 1, 2)
                    do.end()

                pool.wait_ge(core.setup, 7)
                pool.wait_ge(core.loads[1], 32)
                pool.wait_ge(ready, 6)
                pool.wait_ge(loaded, 16 * (N_LOADS))
                front = Chain(pool, pfchain, 0, POOL_FRONT)
                front_factors(front, 0)
                front_context(0)
                front_kept(front, 0)
                in_turns(pool, step)

            @block.scalar
            def _(act):
                scale = float(DH0) ** -0.5

                def front_xT(b):
                    reached(act, xT_ps, b)
                    act.activation(xnT[:], pT[:], ACT.Copy).then_inc(xT_sb.s, 1)

                def front_proj(b):
                    reached(act, proj_ps, b, 1)
                    act.activation(qk[:], pA[:], ACT.Copy).then_inc(proj_sb.s, 1)
                    reached(act, proj_ps, b, 2)
                    act.activation(v[:].rearrange("p g d -> p (g d)"), pB[:], ACT.Copy
                                   ).then_inc(proj_sb.s, 1)

                def front_scores(b):
                    reached(act, scores, b)
                    released(act, taken, b)
                    act.activation(score[:].rearrange("p (h t) s -> p h t s", h=H0), pS[:],
                                   ACT.Copy).then_inc(score_sb.s, 1)

                def front_exps(b):
                    reached(act, first8, b)
                    released(act, mean_sb, b)
                    for j in range(H0 * ST):
                        last = act.activation(prob[:, j, :], score[:, j, :], ACT.Exp,
                                              bias=nmax[:, j:j + 1], scale=scale)
                    last.then_inc(exps.s, 1)

                def front_sums(b):
                    reached(act, taken, b)
                    released(act, mean_sb, b)
                    for j in range(H0 * ST):
                        last = act.activation(etop[:, j, :], top[:, j, :], ACT.Exp,
                                              bias=nmax[:, j:j + 1], scale=scale,
                                              accum_out=esum[:, j:j + 1])
                    last.then_inc(sums.s, 1)

                def step(i, b):
                    reached(act, at_ps, i)
                    act.activation(attnT[:].rearrange("p g t -> p (g t)"), pC[:], ACT.Copy
                                   ).then_inc(at_sb.s, 1)
                    reached(act, ct_ps, i)
                    act.activation(ctT[:], pT[:], ACT.Copy).then_inc(ct_sb.s, 1)
                    if b is not None:
                        front_xT(b)
                        front_proj(b)
                    reached(act, spec_ps, i)
                    act.activation(spec[:, 0, :], pA[:].rearrange("p a b -> p (a b)"), ACT.Copy)
                    act.activation(spec[:, 1, :], pC[:], ACT.Copy).then_inc(spec_sb.s, 1)
                    if b is not None:
                        front_scores(b)
                        front_exps(b)
                    reached(act, hT_ps, i)
                    for c in range(DC):
                        last = act.activation(hT[:, c, :], pT[:, c, :], ACT.Identity,
                                              bias=b_ffn[:, c:c + 1], scale=g_ffn[:, c:c + 1])
                    last.then_inc(hT_sb.s, 1)
                    for c in range(HC):
                        reached(act, u_ps, i, c // 2 * 2 + 2)
                        act.activation(act1[:, c, :], pS[:, c // 2, c % 2, :], ACT.Gelu,
                                       bias=b1[:, c:c + 1]).then_inc(u_act.s, 1)
                    if b is not None:
                        front_sums(b)

                act.wait_ge(core.loads[0], 16)
                act.wait_ge(loaded, 16 * (N_LOADS))
                front_xT(0)
                front_proj(0)
                front_scores(0)
                front_exps(0)
                front_sums(0)
                in_turns(act, step)

            @block.vector
            def _(dve):
                dve.wait_ge(loaded, 16 * (N_LOADS))
                n = Chain(dve, ready)
                n(dve.tensor_scalar(vmask[:], vmask8[:], -NEG_MASK, NEG_MASK, ALU.mult, ALU.add))
                n(dve.tensor_scalar(tmask[:], tmask8[:], 1.0 / H0, None, ALU.mult))
                for f in film_b:
                    n(dve.tensor_scalar(f[:, 0:D], f[:, 0:D], gate[:, 0:1], 1.0, ALU.mult, ALU.add))
                    n(dve.tensor_scalar(f[:, D:], f[:, D:], gate[:, 0:1], None, ALU.mult))

                def stats(do, n, signal, src):
                    for t in range(ST):
                        do.mark(dve.bn_stats(st[:, t, :], src(t)))
                    do.wait_apart()
                    for t in range(ST):
                        last = dve.bn_aggr(mv[:, n, t, :], st[:, t, :])
                    last.then_inc(signal.s, 1)

                def normal(n, dst, src):
                    for t in range(ST):
                        last = dve.tensor_scalar(dst[:, t, :], src(t), mv[:, n, t, 0:1],
                                                 rstd[:, n, t:t + 1], ALU.subtract, ALU.mult)
                    return last

                def tile_of(buffer):
                    return lambda t: buffer[:, t, :]

                def x_tile(b, t):
                    return core.x[:, bass.ds(b * ST + t, 1), :].rearrange("p a d -> p (a d)")

                def front_stats(do, b):
                    released(dve, norm, b)
                    for t in range(ST):
                        do.mark(dve.bn_stats(x_st[:, t, :], x_tile(b, t)))
                    do.wait_apart()
                    for t in range(ST):
                        last = dve.bn_aggr(x_mv[:, t, :], x_st[:, t, :])
                    last.then_inc(x_var.s, 1)

                def front_norms(b):
                    reached(dve, x_var, b)
                    reached(dve, x_rs, b)
                    released(dve, xn_kept, b)
                    released(dve, xT_ps, b)
                    for n, dst in enumerate((xn, u)):
                        for t in range(ST):
                            last = dve.tensor_scalar(dst[:, t, :], x_tile(b, t), x_mv[:, t, 0:1],
                                                     x_rstd[:, n, t:t + 1], ALU.subtract, ALU.mult)
                    last.then_inc(norm.s, 1)

                R = H0 * ST

                def row_in(r, j):
                    return score[:, j, :] if r == 0 else rest[:, j, :]

                def eight(do, b, r):
                    if r == 0:
                        reached_apart(dve, score_sb, b)
                        released(dve, sums, b)
                    else:
                        do.wait_apart()
                    for j in range(R):
                        do.mark(dve.max(top[:, j, 8 * r:8 * r + 8], row_in(r, j)))
                    if r == 0:
                        do.wait()
                        dve.tensor_scalar(nmax[:], top[:, :, 0], -float(DH0) ** -0.5, None,
                                          ALU.mult).then_inc(first8.s, 1)

                def take(do, r, rows=range(R)):
                    do.wait_apart()
                    for j in rows:
                        last = dve.match_replace(rest[:, j, :], top[:, j, 8 * r:8 * r + 8],
                                                 row_in(r, j), NEG_TAKEN)
                        if r < TOPK // 8 - 1:
                            do.mark(last)
                    if r == TOPK // 8 - 1:
                        last.then_inc(taken.s, 1)

                def front_taken(do, b):
                    reached(dve, exps, b)
                    reached(dve, taken, b)
                    do(dve.scalar_tensor_tensor(prob[:], rest[:], NEG_TAKEN, prob[:],
                                                ALU.is_equal, ALU.mult))

                def front_mean(do, b):
                    reached(dve, sums, b)
                    do(dve.reciprocal(esum[:], esum[:]))
                    tm = tmask[:, bass.ds(b * ST, ST)].unsqueeze(1).to_broadcast([P, H0, ST])
                    e3 = esum[:].rearrange("p (h t) -> p h t", h=H0)
                    do(dve.tensor_tensor(e3, e3, tm, ALU.mult))
                    released(dve, at_ps, b)
                    for h in range(H0):
                        for t in range(ST):
                            j = ST * h + t
                            if h == 0:
                                last = dve.tensor_scalar(mean[:, t, :], prob[:, j, :],
                                                         esum[:, j:j + 1], None, ALU.mult)
                            else:
                                last = dve.scalar_tensor_tensor(
                                    mean[:, t, :], prob[:, j, :], esum[:, j:j + 1], mean[:, t, :],
                                    ALU.mult, ALU.add)
                        if h < H0 - 1:
                            do(last)
                    last.then_inc(mean_sb.s, 1)
                    do.end()

                def step(i, b):
                    do = Chain(dve, bchain, i, BACK_STEPS)
                    if b is not None:
                        front = Chain(dve, fchain, b, FRONT_STEPS)
                    if b is not None:
                        front_stats(front, b)
                    for n, (f, fb) in enumerate(((f_in, film_b[0]), (f_out, film_b[1]))):
                        for t in range(ST):
                            if n == 0 and t == 1 and b is not None:
                                front_norms(b)
                            reached(dve, film_ps, i, ST * n + t + 1)
                            dve.scalar_tensor_tensor(f[:, t, :], pB[:] if t % 2 == 0 else pC[:],
                                                     gate[:, 0:1], fb[:], ALU.mult, ALU.add
                                                     ).then_inc(film_sb.s, 1)
                    reached(dve, u_ready, i)
                    reached(dve, film_sb, i, ST)
                    released(dve, hT_ps, i)
                    do(dve.tensor_tensor(x1[:], u_back[:], f_in[:, :, 0:D], ALU.mult))
                    dve.tensor_tensor(x1[:], x1[:], f_in[:, :, D:2 * D], ALU.add
                                      ).then_inc(x1_ready.s, 1)
                    reached(dve, spec_sb, i)
                    k_re = kr[:].rearrange("p k d -> p (k d)")
                    k_im = ki[:].rearrange("p k d -> p (k d)")
                    do.mark(dve.tensor_tensor(prod[:, 0, :], spec[:, 0, :], k_re, ALU.mult))
                    do(dve.tensor_tensor(prod[:, 1, :], spec[:, 1, :], k_im, ALU.mult))
                    dve.tensor_tensor(yspec[:, 0, :], prod[:, 0, :], prod[:, 1, :], ALU.subtract
                                      ).then_inc(yr_ready.s, 1)
                    if b is not None:
                        eight(front, b, 0)
                        take(front, 0)
                    reached(dve, y_ps, i)
                    reached(dve, xt_pre, i)
                    do(dve.tensor_tensor(xt[:], pA[:], f_out[:, :, 0:D], ALU.mult))
                    dve.tensor_tensor(xt[:], xt[:], f_out[:, :, D:2 * D], ALU.add
                                      ).then_inc(xt_ready.s, 1)
                    reached(dve, xt_ready, i)
                    stats(do, 0, var_b, tile_of(xt))
                    reached(dve, rs_b, i, 1)
                    normal(0, x1, tile_of(xt)).then_inc(h_norm.s, 1)
                    if b is not None:
                        for r in range(1, TOPK // 8):
                            eight(front, b, r)
                            take(front, r)
                        front_taken(front, b)
                    reached(dve, dn_ps, i)
                    reached(dve, resid, i)
                    dve.tensor_tensor(xr[:].rearrange("p t d -> p (t d)"),
                                      xr[:].rearrange("p t d -> p (t d)"), pB[:], ALU.add
                                      ).then_inc(dn_sb.s, 1)
                    reached(dve, dn_sb, i)
                    stats(do, 1, var_b, tile_of(xr))
                    if b is not None:
                        front_mean(front, b)
                    reached(dve, rs_b, i, 2)
                    do(normal(1, xr, tile_of(xr)))
                    do(dve.tensor_tensor(xr[:], xr[:], g_out[:].unsqueeze(1)
                                         .to_broadcast([P, ST, D]), ALU.mult))
                    x_i = core.x[:, bass.ds(i * ST, ST), :]
                    dve.tensor_tensor(x_i, xr[:], x_i, ALU.add).then_inc(done.s, 1)
                    do.end()

                dve.wait_ge(core.loads[0], 16)
                front = Chain(dve, fchain, 0, FRONT_STEPS)
                front_stats(front, 0)
                front_norms(0)
                for r in range(TOPK // 8):
                    eight(front, 0, r)
                    take(front, r)
                front_taken(front, 0)
                front_mean(front, 0)
                in_turns(dve, step)

            @block.tensor
            def _(pe):
                def transposes(dst, src):
                    for t in range(ST):
                        for c in range(DC):
                            last = pe.transpose(dst[:, c, t * P:(t + 1) * P],
                                                src[:, t, c * P:(c + 1) * P], core.ident[:])
                    return last

                def front_xT(b):
                    reached(pe, norm, b)
                    transposes(pT, xn).then_inc(xT_ps.s, 1)

                def front_proj(b):
                    reached(pe, xT_sb, b)
                    reached(pe, ctx_in, b)
                    for c in range(DC):
                        pe.matmul(pA[:, 0, :], wq[:, c, :], xnT[:, c, :], start=(c == 0),
                                  stop=(c == DC - 1))
                    for c in range(2):
                        last = pe.matmul(pA[:, 1, :], wk[:, c, :], ctxw[:, c, :], start=(c == 0),
                                         stop=(c == 1))
                    last.then_inc(proj_ps.s, 1)
                    for g in range(ST):
                        for c in range(2):
                            last = pe.matmul(pB[:, g * D:(g + 1) * D], ctxw[:, c, g * P:(g + 1) * P],
                                             wv[:, c, :], start=(c == 0), stop=(c == 1))
                    last.then_inc(proj_ps.s, 1)

                def front_scores(b):
                    reached(pe, proj_sb, b, 1)
                    for t in range(ST):
                        for h in range(H0):
                            r = slice(DH0 * h, DH0 * (h + 1))
                            q = slice(DH0 * h, DH0 * h + 1)
                            pe.matmul(pS[:, h, t, :], core.ones_bf[q, :], maskw[q, :],
                                      start=True, stop=False)
                            last = pe.matmul(pS[:, h, t, :], qk[r, 0, t * P:(t + 1) * P],
                                             qk[r, 1, :], start=False, stop=True)
                    last.then_inc(scores.s, 1)

                def step(i, b):
                    reached(pe, mean_sb, i)
                    released(pe, spec_sb, i)
                    for t in range(ST):
                        for g in range(ST):
                            last = pe.transpose(pC[:, g * S + t * P:g * S + (t + 1) * P],
                                                mean[:, t, g * P:(g + 1) * P], core.ident[:])
                    last.then_inc(at_ps.s, 1)
                    released(pe, hT_sb, i)
                    reached(pe, at_sb, i)
                    reached(pe, proj_sb, i, 2)
                    for c in range(DC):
                        for g in range(ST):
                            last = pe.matmul(pT[:, c, :], v[:, g, c * P:(c + 1) * P],
                                             attnT[:, g, :], start=(g == 0), stop=(g == ST - 1))
                    last.then_inc(ct_ps.s, 1)
                    released(pe, dn_sb, i)
                    reached(pe, ct_sb, i)
                    for n in range(2):
                        for t in range(ST):
                            if n:
                                reached(pe, film_sb, i, t + 1)
                            out = pB[:] if t % 2 == 0 else pC[:]
                            for c in range(DC):
                                last = pe.matmul(out, ctT[:, c, t * P:(t + 1) * P],
                                                 film[n][:, c, :], start=(c == 0),
                                                 stop=(c == DC - 1))
                            last.then_inc(film_ps.s, 1)
                        if n == 0 and b is not None:
                            front_xT(b)
                    released(pe, xt_ready, i)
                    reached(pe, film_sb, i)
                    if b is not None:
                        front_proj(b)
                        reached(pe, proj_sb, b, 1)
                    reached(pe, x1_ready, i)
                    for part in range(2):
                        for k in range(2):
                            out = pA[:, k, :] if part == 0 else pC[:, k * D:(k + 1) * D]
                            for t in range(ST):
                                last = pe.matmul(out, dft[:, t, part, k * P:(k + 1) * P],
                                                 x1[:, t, :], start=(t == 0), stop=(t == ST - 1))
                    last.then_inc(spec_ps.s, 1)
                    if b is not None:
                        front_scores(b)
                    reached(pe, spec_sb, i)
                    reached(pe, yr_ready, i)
                    reached(pe, yi_ready, i)
                    for t in range(ST):
                        for part in range(2):
                            for k in range(2):
                                last = pe.matmul(pA[:, t, :], idft[:, k, part, t * P:(t + 1) * P],
                                                 yspec[:, part, k * D:(k + 1) * D],
                                                 start=(part == 0 and k == 0),
                                                 stop=(part == 1 and k == 1))
                    last.then_inc(y_ps.s, 1)
                    reached(pe, h_norm, i)
                    transposes(pT, x1).then_inc(hT_ps.s, 1)
                    reached(pe, hT_sb, i)
                    if b is not None:
                        reached(pe, score_sb, b)
                        reached(pe, proj_sb, b, 2)
                    for c in range(HC):
                        for k in range(DC):
                            last = pe.matmul(pS[:, c // 2, c % 2, :], w1[:, k, c * P:(c + 1) * P],
                                             hT[:, k, :], start=(k == 0), stop=(k == DC - 1))
                        last.then_inc(u_ps.s, 1)
                    for t in range(ST):
                        for c in range(HC):
                            if t == 0:
                                reached(pe, u_act, i, c + 1)
                            last = pe.matmul(pB[:, t * D:(t + 1) * D], act1[:, c, t * P:(t + 1) * P],
                                             w2[:, c, :], start=(c == 0), stop=(c == HC - 1))
                    last.then_inc(dn_ps.s, 1)

                pe.wait_ge(loaded, 16 * (N_LOADS))
                pe.wait_ge(ready, 6)
                front_xT(0)
                front_proj(0)
                front_scores(0)
                pe.wait_ge(late, 16 * N_LATE)
                in_turns(pe, step)


def leaf_masks(dve, do, bits, m, keep_groups):
    do(dve.memset(m[0][:, :, 0:1], 1.0))
    for level in range(DEPTH):
        n = 1 << level
        here = m[level % 2][:, :, 0:n]
        if n == NG:
            keep_groups(here)
        kids = m[1 - level % 2][:, :, 0:2 * n].rearrange("p j (n c) -> p j n c", c=2)
        do(dve.tensor_tensor(kids[:, :, :, 1], here, bits[:, :, n - 1:2 * n - 1], ALU.mult))
        do(dve.tensor_tensor(kids[:, :, :, 0], here, kids[:, :, :, 1], ALU.subtract))
    return m[DEPTH % 2]


def place_tokens(core, name, group_all, nf, first, slot_i, tile_group_i):
    nc = core.nc
    W = nf * NG
    with ExitStack() as own:
        def sb(n, shape, dt=F32):
            return core.sb(own, f"{name}_{n}", shape, dt)

        tri, ones = sb("tri", [P, P], BF16), sb("ones", [P, P], BF16)
        cst = sb("cst", [P, NT + TILES + NG * NG])
        trif = sb("trif", [P, P])
        total = sb("total", [P, NT, W])
        before = sb("before", [P, NT + 1, W])
        pre = sb("pre", [P, NT, W])
        cmp = sb("cmp", [P, W, max(NG, NT)])
        used, start, end = sb("used", [P, W]), sb("start", [P, W]), sb("end", [P, W])
        slot = sb("slot", [P, NT, nf])
        cmp2 = sb("cmp2", [P, nf, TILES, NG])
        tg = sb("tile_group", [P, nf, TILES])
        psP = core.ps(own, f"{name}_psP", [P, 2, 512])
        psT = core.ps(own, f"{name}_psT", [P, 2, 512])
        loaded, ready = core.sem(name + "_loaded"), core.sem(name + "_ready")
        counted, chain = core.sem(name + "_counted"), core.sem(name + "_steps")
        half = NT // 2 * W
        with nc.Block() as block:
            @block.sync
            def _(sp):
                sp.dma_start(trif[:], core.dram["tri"]).then_inc(loaded, 16)
                sp.dma_start(cst[:], core.dram["counts"].partition_broadcast(P)
                             ).then_inc(loaded, 16)

            @block.tensor
            def _(pe):
                pe.wait_ge(ready, 2)
                for h in range(2):
                    g = group_all[:, h * half:(h + 1) * half]
                    pe.matmul(psP[:, h, 0:half], tri[:], g, start=True, stop=True)
                    last = pe.matmul(psT[:, h, 0:half], ones[:], g, start=True, stop=True)
                last.then_inc(counted, 1)

            @block.vector
            def _(dve):
                do = Chain(dve, chain)
                dve.wait_ge(loaded, 32)
                dve.tensor_copy(tri[:], trif[:]).then_inc(ready, 1)
                dve.memset(ones[:], 1.0).then_inc(ready, 1)
                do.mark(dve.memset(before[:, 0, :], 0.0))
                dve.wait_ge(counted, 1)
                for h in range(2):
                    do(dve.tensor_copy(total[:, h * NT // 2:(h + 1) * NT // 2, :]
                                       .rearrange("p t w -> p (t w)"), psT[:, h, 0:half]))
                for t in range(NT):
                    do(dve.tensor_tensor(before[:, t + 1, :], before[:, t, :], total[:, t, :],
                                         ALU.add))
                count = before[:, NT, :]
                wide = [P, W, NT]
                do(dve.tensor_tensor(cmp[:, :, 0:NT], count.unsqueeze(2).to_broadcast(wide),
                                     cst[:, 0:NT].unsqueeze(1).to_broadcast(wide), ALU.is_gt))
                do(dve.tensor_reduce(used[:], cmp[:, :, 0:NT], AX_X, ALU.add))
                below = cst[:, NT + TILES:].rearrange("p (a b) -> p a b", b=NG)
                for f in range(nf):
                    u = used[:, f * NG:(f + 1) * NG]
                    do(dve.tensor_tensor(cmp[:, f * NG:(f + 1) * NG, 0:NG],
                                         u.unsqueeze(1).to_broadcast([P, NG, NG]), below,
                                         ALU.mult))
                do(dve.tensor_reduce(start[:], cmp[:, :, 0:NG], AX_X, ALU.add))
                do(dve.tensor_tensor(end[:], start[:], used[:], ALU.add))
                do(dve.tensor_scalar(start[:], start[:], float(P), None, ALU.mult))
                for h in range(2):
                    do(dve.tensor_tensor(pre[:, h * NT // 2:(h + 1) * NT // 2, :]
                                         .rearrange("p t w -> p (t w)"), psP[:, h, 0:half],
                                         before[:, h * NT // 2:(h + 1) * NT // 2, :]
                                         .rearrange("p t w -> p (t w)"), ALU.add))
                do(dve.tensor_tensor(pre[:], pre[:], start[:].unsqueeze(1).to_broadcast([P, NT, W]),
                                     ALU.add))
                do(dve.tensor_tensor(pre[:].rearrange("p t w -> p (t w)"),
                                     pre[:].rearrange("p t w -> p (t w)"), group_all, ALU.mult))
                do(dve.tensor_reduce(slot[:], pre[:].rearrange("p t (f s) -> p t f s", f=nf),
                                     AX_X, ALU.add))
                do(dve.tensor_copy(slot_i[:], slot[:]))
                for f in range(nf):
                    wide = [P, TILES, NG]
                    do(dve.tensor_tensor(cmp2[:, f, :, :],
                                         end[:, f * NG:(f + 1) * NG].unsqueeze(1)
                                         .to_broadcast(wide),
                                         cst[:, NT:NT + TILES].unsqueeze(2).to_broadcast(wide),
                                         ALU.is_le))
                    do(dve.tensor_reduce(tg[:, f, :], cmp2[:, f, :, :], AX_X, ALU.add))
                for f in range(nf):
                    do(dve.tensor_scalar(tg[:, f, :], tg[:, f, :], float(NG - 1),
                                         float((first + f) * NG), ALU.min, ALU.add))
                do(dve.tensor_copy(tile_group_i[:], tg[:]))




def group_products(core, name, nf, rows, slot_i, tile_group_i, sorted_x, sorted_y, results,
                   gelu=False):
    nc, dram = core.nc, core.dram
    NB = 4
    TURNS = nf * TILES // NB
    with ExitStack() as own:
        def sb(n, shape, dt=F32):
            return core.sb(own, f"{name}_{n}", shape, dt)

        hold = sb("hold", [GL, GH])
        spread = sb("leaf_units", [GL, GH], BF16)
        xs = [sb(f"x{n}", [P, XW]) for n in range(NB)]
        w12 = [sb(f"w_{n}", [P, W1COLS + GH // P * D]) for n in range(NB)]
        w1 = [w[:, 0:W1COLS] for w in w12]
        w2 = [w[:, W1COLS:].rearrange("p (c d) -> p c d", d=D) for w in w12]
        b2 = [sb(f"b2_{n}", [GL, D]) for n in range(NB)]
        xT = [sb(f"xT{n}", [P, DC, P]) for n in range(NB)]
        leafT = [sb(f"leafT{n}", [GL, P]) for n in range(NB)]
        leafB = [sb(f"leafB{n}", [GL, P], BF16) for n in range(NB)]
        act_h = [sb(f"act{n}", [P, GH // P, P]) for n in range(2)]
        hT = [sb(f"hT{n}", [P, GH // P, P]) for n in range(2)]
        ys = [sb(f"y{n}", [P, D]) for n in range(2)]
        psX = [core.ps(own, f"{name}_psX{n}", [P, 4, P]) for n in range(2)]
        psH = [core.ps(own, f"{name}_psH{n}", [P, 4, P]) for n in range(2)]
        psM = [core.ps(own, f"{name}_psM{n}", [P, 4, P]) for n in range(2)]
        psY = [core.ps(own, f"{name}_psY{n}", [P, 2 * D]) for n in range(2)]
        loaded, ready = core.sem(name + "_loaded"), core.sem(name + "_ready")
        placed = [core.sem(f"{name}_placed{f}") for f in range(nf)]
        fetched = core.sem(name + "_fetched")
        tile_in = [core.sem(f"{name}_tile_in{n}") for n in range(NB)]
        worked = [core.sem(f"{name}_worked{n}") for n in range(NB)]
        stored = [core.sem(f"{name}_stored{n}") for n in range(2)]
        x_ps, xT_sb, h_ps, h_act, h_sb, y_sb = (
            core.sem(f"{name}_{n}") for n in ("x_ps", "xT_sb", "h_ps", "h_act", "h_sb", "y_sb"))

        def on(i, n, j):
            return i + (n + j) // NB, (n + j) % NB

        def turns(eng, step):
            with eng.Fori(0, TURNS - 1) as i:
                for n in range(NB):
                    step(i, n, False)
            for n in range(NB):
                step(TURNS - 1, n, True)

        with nc.Block() as block:
            @block.gpsimd
            def _(pool):
                pool.wait_ge(core.zeroed, 16 * ZERO_FILLS)
                for f in range(nf):
                    for t in range(NT):
                        pool.indirect_dma_start(
                            sorted_x[f], bass.IndirectOffsetOnAxis(slot_i[:, t, f:f + 1], 0),
                            rows[:, f, t, :], None).then_inc(placed[f], 16)
                for f in range(nf):
                    for n in range(2):
                        pool.wait_ge(stored[n], 16 * (f + 1) * TILES // 2)
                    for t in range(NT):
                        pool.indirect_dma_start(
                            results[:, f, t, :], None, sorted_y[f],
                            bass.IndirectOffsetOnAxis(slot_i[:, t, f:f + 1], 0)
                            ).then_inc(fetched, 16)
                pool.wait_ge(fetched, 16 * NT * nf)

            @block.sync
            def _(sp):
                sp.dma_start(hold[:], dram["leaf_units"]).then_inc(loaded, 16)
                for f in range(nf):
                    sp.wait_ge(placed[f], 16 * NT)
                    with sp.Fori(f * TILES // NB, (f + 1) * TILES // NB) as i:
                        for n in range(NB):
                            tile = i * NB + n
                            g = sp.value_load(tile_group_i[0:1, bass.ds(tile, 1)], min_val=0,
                                              max_val=4 * NG - 1)
                            sp.wait_ge(worked[n], i)
                            for out, in_ in (
                                    (xs[n][:], sorted_x[f][bass.ds((tile - f * TILES) * P, P), :]),
                                    (w12[n][:], dram["group_w"][bass.ds(g * P, P), :]),
                                    (b2[n][:], dram["group_b2"][bass.ds(g * GL, GL), :])):
                                sp.dma_start(out, in_).then_inc(tile_in[n], 16)

            @block.scalar
            def _(act):
                def activate(i, n):
                    tile, k = i * NB + n, n % 2
                    act.wait_ge(h_ps, tile + 1)
                    for c in range(GH // P):
                        b1 = w1[n][:, DC * GH + c:DC * GH + c + 1]
                        last = act.activation(act_h[k][:, c, :], psH[k][:, c, :],
                                              ACT.Gelu if gelu else ACT.Relu, bias=b1)
                    last.then_inc(h_act, 1)

                def store(f, i, n):
                    tile, k = i * NB + n, n % 2
                    act.wait_ge(worked[n], i + 1)
                    act.wait_ge(stored[k], i * 32 + (16 if n >= 2 else 0))
                    act.activation(ys[k][:], psY[k][:, 0:D], ACT.Copy).then_inc(y_sb, 1)
                    act.wait_ge(y_sb, tile + 1)
                    act.dma_start(sorted_y[f][bass.ds((tile - f * TILES) * P, P), :], ys[k][:]
                                  ).then_inc(stored[k], 16)

                activate(0, 0)
                for f in range(nf):
                    first, end = f * TILES // NB, (f + 1) * TILES // NB
                    with act.Fori(first, end - (f == nf - 1)) as i:
                        for n in range(NB):
                            activate(*on(i, n, 1))
                            store(f, i, n)
                for n in range(NB):
                    if n < NB - 1:
                        activate(TURNS - 1, n + 1)
                    store(nf - 1, TURNS - 1, n)

            @block.vector
            def _(dve):
                dve.wait_ge(loaded, 16)
                dve.tensor_copy(spread[:], hold[:]).then_inc(ready, 1)

                def transposed(i, n):
                    dve.wait_ge(x_ps, i * NB + n + 1)
                    dve.tensor_copy(leafT[n][:], psX[n % 2][0:GL, DC, :])
                    dve.tensor_copy(leafB[n][:], psX[n % 2][0:GL, DC, :])
                    dve.tensor_copy(xT[n][:], psX[n % 2][:, 0:DC, :]).then_inc(xT_sb, 1)

                def leaf_only(i, n):
                    dve.wait_ge(h_act, i * NB + n + 1)
                    dve.tensor_tensor(hT[n % 2][:], act_h[n % 2][:], psM[n % 2][:, 0:GH // P, :],
                                      ALU.mult).then_inc(h_sb, 1)

                def step(i, n, last):
                    if not (last and n >= NB - 2):
                        transposed(*on(i, n, 2))
                    if not (last and n == NB - 1):
                        leaf_only(*on(i, n, 1))

                transposed(0, 0)
                transposed(0, 1)
                leaf_only(0, 0)
                turns(dve, step)

            @block.tensor
            def _(pe):
                pe.wait_ge(ready, 1)

                def transposes(i, n, first=False):
                    tile, k = i * NB + n, n % 2
                    pe.wait_ge(tile_in[n], 48 * i + 48)
                    if not first:
                        pe.wait_ge(xT_sb, tile - 1)
                    for c in range(DC):
                        pe.transpose(psX[k][:, c, :], xs[n][:, c * P:(c + 1) * P], core.ident[:])
                    pe.transpose(psX[k][0:GL, DC, :], xs[n][:, D:XW], core.ident[:]
                                 ).then_inc(x_ps, 1)

                def hidden(i, n, first=False):
                    tile, k = i * NB + n, n % 2
                    pe.wait_ge(xT_sb, tile + 1)
                    if not first:
                        pe.wait_ge(h_sb, tile - 1)
                    for c in range(GH // P):
                        for d in range(DC):
                            w = w1[n][:, d * GH + c * P:d * GH + (c + 1) * P]
                            pe.matmul(psH[k][:, c, :], w, xT[n][:, d, :], start=(d == 0),
                                      stop=(d == DC - 1))
                    for c in range(GH // P):
                        last = pe.matmul(psM[k][:, c, :], spread[:, c * P:(c + 1) * P],
                                         leafB[n][:], start=True, stop=True)
                    last.then_inc(h_ps, 1)

                def output(i, n):
                    tile, k = i * NB + n, n % 2
                    if n >= 2:
                        pe.wait_ge(y_sb, tile - 1)
                    else:
                        pe.wait_ge(y_sb, i * NB + n)
                    pe.matmul(psY[k][:, 0:D], leafT[n][:], b2[n][:], start=True, stop=False)
                    pe.wait_ge(h_sb, tile + 1)
                    for c in range(GH // P):
                        last = pe.matmul(psY[k][:, 0:D], hT[k][:, c, :], w2[n][:, c, :],
                                         start=False, stop=(c == GH // P - 1))
                    last.then_inc(worked[n], 1)

                def step(i, n, last):
                    if not (last and n == NB - 1):
                        hidden(*on(i, n, 1))
                    if not (last and n >= NB - 2):
                        transposes(*on(i, n, 2))
                    output(i, n)

                transposes(0, 0, first=True)
                transposes(0, 1, first=True)
                hidden(0, 0, first=True)
                turns(pe, step)


def standard_factors(core, pool, do, out, hold, var):
    do(rstd_of(pool, do, out, var, core.minus_half[:]))
    do(pool.tensor_tensor(hold, var, out, ALU.mult))
    do.mark(pool.tensor_tensor(hold, hold, out, ALU.mult))
    do.wait_apart()
    do(pool.tensor_scalar(hold, hold, D / (D - 1), None, ALU.mult))
    do.mark(pool.tensor_tensor(hold, hold, core.plus_half[:], ALU.pow))
    do.wait_apart()
    do(rstd_of(pool, do, hold, hold, core.minus_half[:]))
    return pool.tensor_tensor(out, out, hold, ALU.mult)


def route_qkv(core, ctx, rows, xn_keep, group_all):
    nc, dram = core.nc, core.dram
    NF = 3
    with ExitStack() as own:
        def sb(n, shape, dt=F32):
            return core.sb(own, "r_" + n, shape, dt)

        nw, nb = sb("nw", [P, NF, DC, NN]), sb("nb", [P, NF, NN])
        st, mv = sb("stats", [P, ST, 6]), sb("mean_var", [P, ST, 2])
        factor, hold = sb("factor", [P, ST]), sb("hold", [P, ST])
        xn, xnT = sb("xn", [P, ST, D]), sb("xnT", [P, DC, S])
        bits = sb("bits", [P, NF * ST, NN])
        m = [sb(f"mask{n}", [P, NF * ST, NL]) for n in range(2)]
        psT = core.ps(own, "r_psT", [P, DC, S])
        psL = core.ps(own, "r_psL", [P, NF, ST, S])
        loaded, ready = core.sem("r_loaded"), core.sem("r_ready")
        sig = core.flag
        var, rs, norm, kept = sig("r_var"), sig("r_factor"), sig("r_norm"), sig("r_kept")
        t_ps, t_sb, logits, bits_sb = (sig("r_" + n) for n in ("T_ps", "T_sb", "logits", "bits"))
        rows_in = sig("r_rows")
        nchain, dchain, pchain = core.sem("r_dve_norm"), core.sem("r_dve"), core.sem("r_pool")
        MASK_STEPS, POOL_STEPS = 20, 8
        with nc.Block() as block:
            @block.sync
            def _(sp):
                for n, f in enumerate("qkv"):
                    sp.dma_start(nw[:, n, :, :], dram[f"L0_ffn_{f}_nwT"]
                                 .rearrange("(c p) n -> p c n", p=P)).then_inc(loaded, 16)
                    sp.dma_start(nb[:, n, :], dram[f"L0_ffn_{f}_nb"].partition_broadcast(P)
                                 ).then_inc(loaded, 16)

            @block.gpsimd
            def _(pool):
                with pool.Fori(0, B) as i:
                    do = Chain(pool, pchain, i, POOL_STEPS)
                    reached_apart(pool, var, i)
                    standard_factors(core, pool, do, factor[:], hold[:], mv[:, :, 1]
                                     ).then_inc(rs.s, 1)
                    reached(pool, norm, i)
                    pool.tensor_copy(xn_keep[:, bass.ds(i * ST, ST), :], xn[:]).then_inc(kept.s, 1)
                    do.end()

            @block.scalar
            def _(act):
                with act.Fori(0, B) as i:
                    reached(act, t_ps, i)
                    act.activation(xnT[:], psT[:], ACT.Copy).then_inc(t_sb.s, 1)
                    for f in range(NF):
                        last = act.activation(rows[:, f, bass.ds(i * ST, ST), 0:D], xn[:],
                                              ACT.Copy)
                    last.then_inc(rows_in.s, 1)

            @block.vector
            def _(dve):
                dve.wait_ge(loaded, 16 * 2 * NF)
                dve.tensor_scalar(nb[:], nb[:], -1.0, None, ALU.mult).then_inc(ready, 1)
                dve.wait_ge(ready, 1)

                def x_tile(b, t):
                    return core.x[:, bass.ds(b * ST + t, 1), :].rearrange("p a d -> p (a d)")

                def stats(b):
                    do = Chain(dve, nchain, b, ST)
                    released(dve, norm, b)
                    for t in range(ST):
                        do.mark(dve.bn_stats(st[:, t, :], x_tile(b, t)))
                    do.wait_apart()
                    for t in range(ST):
                        last = dve.bn_aggr(mv[:, t, :], st[:, t, :])
                    last.then_inc(var.s, 1)
                    do.end()

                def normal(b):
                    reached(dve, var, b)
                    reached(dve, rs, b)
                    released(dve, t_ps, b)
                    released(dve, kept, b)
                    released(dve, rows_in, b)
                    for t in range(ST):
                        last = dve.tensor_scalar(xn[:, t, :], x_tile(b, t), mv[:, t, 0:1],
                                                 factor[:, t:t + 1], ALU.subtract, ALU.mult)
                    last.then_inc(norm.s, 1)

                def step(i, b):
                    do = Chain(dve, dchain, i, MASK_STEPS)
                    if b is not None:
                        stats(b)
                    reached(dve, logits, i)
                    nbw = nb[:].unsqueeze(2).to_broadcast([P, NF, ST, NN])
                    dve.tensor_tensor(bits[:].rearrange("p (f t) n -> p f t n", f=NF),
                                      psL[:, :, :, 0:NN], nbw, ALU.is_gt).then_inc(bits_sb.s, 1)
                    reached(dve, bits_sb, i)
                    if b is not None:
                        normal(b)

                    def keep_groups(here):
                        out = group_all[:, bass.ds(i * ST, ST), :, :]
                        dve.tensor_copy(out.rearrange("p t f s -> p f t s"),
                                        here.rearrange("p (f t) s -> p f t s", f=NF))

                    leaves = leaf_masks(dve, do, bits, m, keep_groups)
                    for f in range(NF):
                        by_leaf = leaves[:, f * ST:(f + 1) * ST, :].rearrange(
                            "p t (g l) -> p t l g", l=GL)
                        do.mark(dve.tensor_reduce(rows[:, f, bass.ds(i * ST, ST), D:XW], by_leaf,
                                                  AX_X, ALU.add))
                    do.end()

                stats(0)
                normal(0)
                in_turns(dve, step)

            @block.tensor
            def _(pe):
                pe.wait_ge(loaded, 16 * 2 * NF)
                with pe.Fori(0, B) as i:
                    reached(pe, norm, i)
                    released(pe, t_sb, i)
                    for t in range(ST):
                        for c in range(DC):
                            last = pe.transpose(psT[:, c, t * P:(t + 1) * P],
                                                xn[:, t, c * P:(c + 1) * P], core.ident[:])
                    last.then_inc(t_ps.s, 1)
                    reached(pe, t_sb, i)
                    released(pe, bits_sb, i)
                    for f in range(NF):
                        for t in range(ST):
                            for c in range(DC):
                                last = pe.matmul(psL[:, f, t, 0:NN], xnT[:, c, t * P:(t + 1) * P],
                                                 nw[:, f, c, :], start=(c == 0),
                                                 stop=(c == DC - 1))
                    last.then_inc(logits.s, 1)


class Norms:

    def __init__(self, core, ctx, name, kinds, tiles=ST):
        self.core, self.kinds, self.tiles = core, kinds, tiles
        self.st = core.sb(ctx, name + "_stats", [P, tiles, 6])
        self.mv = core.sb(ctx, name + "_mean_var", [P, kinds, tiles, 2])
        self.rstd = core.sb(ctx, name + "_rstd", [P, kinds, tiles])
        self.half = core.sb(ctx, name + "_minus_half", [P, tiles])
        self.var = core.flag(name + "_var", kinds)
        self.rs = core.flag(name + "_rs", kinds)

    def stats(self, dve, do, n, src):
        for t in range(self.tiles):
            do.mark(dve.bn_stats(self.st[:, t, :], src[:, t, :]))
        do.wait_apart()
        for t in range(self.tiles):
            last = dve.bn_aggr(self.mv[:, n, t, :], self.st[:, t, :])
        last.then_inc(self.var.s, 1)

    def root(self, pool, do, i, n):
        reached_apart(pool, self.var, i, n + 1)
        rstd_of(pool, do, self.rstd[:, n, :], self.mv[:, n, :, 1], self.half[:]
                ).then_inc(self.rs.s, 1)

    def normal(self, dve, i, n, dst, src):
        reached(dve, self.var, i, n + 1)
        reached(dve, self.rs, i, n + 1)
        for t in range(self.tiles):
            last = dve.tensor_scalar(dst[:, t, :], src[:, t, :], self.mv[:, n, t, 0:1],
                                     self.rstd[:, n, t:t + 1], ALU.subtract, ALU.mult)
        return last


def token_attention(core, results, xn_keep, rows, group_all):
    nc, dram = core.nc, core.dram
    with ExitStack() as own:
        def sb(n, shape, dt=F32):
            return core.sb(own, "t_" + n, shape, dt)

        nw, nb = sb("nw", [P, DC, NN]), sb("nb", [P, NN])
        qk = sb("qk", [P, 2, ST, D])
        qkT = sb("qkT", [P, 2, DC, S])
        mx, nmx, total = sb("max", [P, ST]), sb("minus_max", [P, ST]), sb("total", [P, ST])
        p, pT = sb("p", [P, ST, S]), sb("pT", [P, ST, S])
        y, yT = sb("y", [P, ST, D]), sb("yT", [P, DC, S])
        bits = sb("bits", [P, ST, NN])
        m = [sb(f"mask{n}", [P, ST, NL]) for n in range(2)]
        psQ = core.ps(own, "t_psQ", [P, 2, DC, S])
        psS, psP = core.ps(own, "t_psS", [P, ST, S]), core.ps(own, "t_psP", [P, ST, S])
        psO, psY = core.ps(own, "t_psO", [P, ST, D]), core.ps(own, "t_psY", [P, DC, S])
        psL = core.ps(own, "t_psL", [P, ST, S])
        loaded, ready = core.sem("t_loaded"), core.sem("t_ready")
        sig = core.flag
        (qk_in, q_ps, q_sb, s_ps, m_sb, p_sb, pT_ps, pT_sb, o_ps, y_sb, y_kept, yT_ps, yT_sb,
         l_ps, bits_sb, row_in) = (
            sig("t_" + n) for n in ("qk_in", "q_ps", "q_sb", "s_ps", "m_sb", "p_sb", "pT_ps",
                                    "pT_sb", "o_ps", "y_sb", "y_kept", "yT_ps", "yT_sb", "l_ps",
                                    "bits", "row_in"))
        dchain, mchain = core.sem("t_dve"), core.sem("t_dve_max")
        DVE_STEPS = 19
        with nc.Block() as block:
            @block.sync
            def _(sp):
                sp.dma_start(nw[:], dram["L0_ffn_f_nwT"].rearrange("(c p) n -> p c n", p=P)
                             ).then_inc(loaded, 16)
                sp.dma_start(nb[:], dram["L0_ffn_f_nb"].partition_broadcast(P)
                             ).then_inc(loaded, 16)

            @block.gpsimd
            def _(pool):
                def front_in(b):
                    released(pool, q_ps, b)
                    for n in range(2):
                        last = pool.tensor_copy(qk[:, n, :, :], results[:, n, bass.ds(b * ST, ST), :])
                    last.then_inc(qk_in.s, 1)

                def step(i, b):
                    if b is not None:
                        front_in(b)
                    reached(pool, y_sb, i)
                    xs = core.x[:, bass.ds(i * ST, ST), :]
                    pool.tensor_tensor(xs, xs, y[:], ALU.add).then_inc(y_kept.s, 1)

                front_in(0)
                in_turns(pool, step)

            @block.scalar
            def _(act):
                def front_transposed(b):
                    reached(act, q_ps, b)
                    act.activation(qkT[:], psQ[:], ACT.Copy).then_inc(q_sb.s, 1)

                def front_probs(b):
                    reached(act, m_sb, b)
                    for t in range(ST):
                        last = act.activation(p[:, t, :], psS[:, t, :], ACT.Exp,
                                              bias=nmx[:, t:t + 1], scale=float(D) ** -0.5,
                                              accum_out=total[:, t:t + 1])
                    last.then_inc(p_sb.s, 1)

                def step(i, b):
                    reached(act, pT_ps, i)
                    act.activation(pT[:], psP[:], ACT.Copy).then_inc(pT_sb.s, 1)
                    if b is not None:
                        front_transposed(b)
                        front_probs(b)
                    reached(act, yT_ps, i)
                    act.activation(yT[:], psY[:], ACT.Copy).then_inc(yT_sb.s, 1)
                    reached(act, y_sb, i)
                    act.activation(rows[:, 0, bass.ds(i * ST, ST), 0:D], y[:], ACT.Copy
                                   ).then_inc(row_in.s, 1)

                front_transposed(0)
                front_probs(0)
                in_turns(act, step)

            @block.vector
            def _(dve):
                dve.wait_ge(loaded, 32)
                dve.tensor_scalar(nb[:], nb[:], -1.0, None, ALU.mult).then_inc(ready, 1)
                dve.wait_ge(ready, 1)

                def front_max(b):
                    do = Chain(dve, mchain, b, 1)
                    reached(dve, s_ps, b)
                    do(dve.tensor_reduce(mx[:], psS[:], AX_X, ALU.max))
                    dve.tensor_scalar(nmx[:], mx[:], -float(D) ** -0.5, None, ALU.mult
                                      ).then_inc(m_sb.s, 1)
                    do.end()

                def step(i, b):
                    do = Chain(dve, dchain, i, DVE_STEPS)
                    reached(dve, p_sb, i)
                    do(dve.reciprocal(total[:], total[:]))
                    reached(dve, o_ps, i)
                    released(dve, y_kept, i)
                    released(dve, row_in, i)
                    for t in range(ST):
                        xn = xn_keep[:, bass.ds(i * ST + t, 1), :].rearrange("p a d -> p (a d)")
                        last = dve.scalar_tensor_tensor(y[:, t, :], psO[:, t, :],
                                                        total[:, t:t + 1], xn, ALU.mult, ALU.add)
                    last.then_inc(y_sb.s, 1)
                    if b is not None:
                        front_max(b)
                    reached(dve, l_ps, i)
                    dve.tensor_tensor(bits[:], psL[:, :, 0:NN],
                                      nb[:].unsqueeze(1).to_broadcast([P, ST, NN]), ALU.is_gt
                                      ).then_inc(bits_sb.s, 1)
                    reached(dve, bits_sb, i)

                    def keep_groups(here):
                        dve.tensor_copy(group_all[:, bass.ds(i * ST, ST), :], here)

                    leaves = leaf_masks(dve, do, bits, m, keep_groups)
                    do.mark(dve.tensor_reduce(rows[:, 0, bass.ds(i * ST, ST), D:XW],
                                              leaves.rearrange("p t (g l) -> p t l g", l=GL),
                                              AX_X, ALU.add))
                    do.end()

                front_max(0)
                in_turns(dve, step)

            @block.tensor
            def _(pe):
                def transposes(dst, src):
                    for t in range(ST):
                        for c in range(DC):
                            last = pe.transpose(dst[:, c, t * P:(t + 1) * P],
                                                src(t)[:, c * P:(c + 1) * P], core.ident[:])
                    return last

                def value(b, t):
                    return results[:, 2, bass.ds(b * ST + t, 1), :].rearrange("p a d -> p (a d)")

                def front_transposes(b):
                    reached(pe, qk_in, b)
                    released(pe, q_sb, b)
                    for n in range(2):
                        last = transposes(psQ[:, n, :, :], lambda t: qk[:, n, t, :])
                    last.then_inc(q_ps.s, 1)

                def front_scores(b):
                    reached(pe, q_sb, b)
                    released(pe, p_sb, b)
                    for t in range(ST):
                        for c in range(DC):
                            last = pe.matmul(psS[:, t, :], qkT[:, 0, c, t * P:(t + 1) * P],
                                             qkT[:, 1, c, :], start=(c == 0), stop=(c == DC - 1))
                    last.then_inc(s_ps.s, 1)

                def step(i, b):
                    reached(pe, p_sb, i)
                    released(pe, pT_sb, i)
                    transposes(psP, lambda t: p[:, t, :]).then_inc(pT_ps.s, 1)
                    if b is not None:
                        front_transposes(b)
                    reached(pe, pT_sb, i)
                    released(pe, y_sb, i)
                    for t in range(ST):
                        for c in range(ST):
                            last = pe.matmul(psO[:, t, :], pT[:, c, t * P:(t + 1) * P],
                                             value(i, c), start=(c == 0), stop=(c == ST - 1))
                    last.then_inc(o_ps.s, 1)
                    if b is not None:
                        front_scores(b)
                    reached(pe, y_sb, i)
                    released(pe, yT_sb, i)
                    transposes(psY, lambda t: y[:, t, :]).then_inc(yT_ps.s, 1)
                    reached(pe, yT_sb, i)
                    released(pe, bits_sb, i)
                    for t in range(ST):
                        for c in range(DC):
                            last = pe.matmul(psL[:, t, 0:NN], yT[:, c, t * P:(t + 1) * P],
                                             nw[:, c, :], start=(c == 0), stop=(c == DC - 1))
                    last.then_inc(l_ps.s, 1)

                front_transposes(0)
                front_scores(0)
                pe.wait_ge(loaded, 32)
                in_turns(pe, step)


QC = H1 // 4
PAIRS = H1 // 2


def second_attention(core, results):
    nc, dram = core.nc, core.dram
    with ExitStack() as own:
        def sb(n, shape, dt=F32):
            return core.sb(own, "c_" + n, shape, dt)

        wq, wk = sb("wq", [P, DC, QC * P]), sb("wk", [CP, 2, QC * P])
        wv, wo = sb("wv", [CP, 2, D]), sb("wo", [P, QC, D])
        bq, bk = sb("bq", [P, QC]), sb("bk", [P, QC])
        bv, bo = sb("bv", [P, D]), sb("bo", [P, D])
        ctxw = sb("ctx", [CP, 2, S])
        xn, xnT = sb("xn", [P, ST, D]), sb("xnT", [P, DC, S])
        qT, kT = sb("qT", [P, QC, S]), sb("kT", [P, QC, S])
        v = sb("v", [P, ST, H1, 32])
        top, shift = (sb(n, [P, 2, 2, ST]) for n in ("max", "minus_max"))
        prob, probT = ([sb(f"{w}{n}", [P, 2, ST, S]) for n in range(2)]
                       for w in ("prob", "probT"))
        total = sb("total", [P, 2, 2, ST])
        attT = sb("attT", [P, QC, S])
        norms = Norms(core, own, "c", 1)
        psS = [core.ps(own, f"c_psS{n}", [P, 2, ST, S]) for n in range(2)]
        psP = [core.ps(own, f"c_psP{n}", [P, ST, S]) for n in range(2)]
        psO = core.ps(own, "c_psO", [P, QC, S])
        loaded, ready = core.sem("c_loaded"), core.sem("c_ready")
        sig = core.flag
        (x_in, ctx_in, norm, xT_ps, xT_sb, q_ps, k_ps, q_sb, k_sb, v_ps, v_sb, heads,
         aT_sb, f_ps, bias_in, done) = (
            sig("c_" + n) for n in ("x_in", "ctx_in", "norm", "xT_ps", "xT_sb", "q_ps", "k_ps",
                                    "q_sb", "k_sb", "v_ps", "v_sb", "heads", "aT_sb",
                                    "f_ps", "bias_in", "done"))
        scores, shifts, probs, sums, shares, pT_ps, pT_sb = (
            sig("c_" + n, PAIRS) for n in ("scores", "shifts", "probs", "sums", "shares", "probT_ps",
                                           "probT_sb"))
        nchain, dchain, pchain = (core.sem("c_" + n) for n in ("dve_norm", "dve", "pool"))
        NORM_STEPS, DVE_STEPS, POOL_STEPS = 2, PAIRS, 1
        N_LOADS = 8

        with nc.Block() as block:
            @block.sync
            def _(sp):
                def load(out, in_):
                    sp.dma_start(out, in_).then_inc(loaded, 16)

                load(wq[:], dram["c_wq"].rearrange("(c p) n -> p c n", p=P))
                load(wk[:], dram["c_wk"].rearrange("(c p) n -> p c n", p=CP))
                load(wv[:], dram["L1_xattn_wv"].rearrange("(c p) n -> p c n", p=CP))
                load(wo[:], dram["c_wo"].rearrange("(c p) n -> p c n", p=P))
                load(bq[:], dram["c_bq"])
                load(bk[:], dram["c_bk"])
                load(bv[:], dram["L1_xattn_bv"].partition_broadcast(P))
                load(bo[:], dram["L1_xattn_bo"].partition_broadcast(P))

            @block.gpsimd
            def _(pool):
                pool.memset(norms.half[:], -0.5).then_inc(ready, 1)
                pool.memset(v[:], 0.0).then_inc(ready, 1)
                pool.wait_ge(ready, 2)
                pool.wait_ge(loaded, 16 * N_LOADS)

                def tiles(b):
                    return core.x[:, bass.ds(b * ST, ST), :]

                def front(b):
                    pool.tensor_tensor(tiles(b), tiles(b), results[:, 0, bass.ds(b * ST, ST), :],
                                       ALU.add).then_inc(x_in.s, 1)
                    released(pool, k_ps, b)
                    pool.tensor_copy(ctxw[:], core.ctxT[:, :, bass.ds(b * S, S)]
                                     ).then_inc(ctx_in.s, 1)

                def front_root(b):
                    do = Chain(pool, pchain, b, POOL_STEPS)
                    norms.root(pool, do, b, 0)
                    do.end()

                def front_bias(b):
                    reached_apart(pool, norm, b)
                    pool.tensor_tensor(tiles(b), tiles(b),
                                       bo[:].unsqueeze(1).to_broadcast([P, ST, D]),
                                       ALU.add).then_inc(bias_in.s, 1)

                def step(i, b):
                    for p in range(PAIRS):
                        reached(pool, sums, i, p + 1)
                        pr = prob[p % 2][:]
                        pool.tensor_tensor(pr, pr, total[:, p % 2, :, :].unsqueeze(3)
                                           .to_broadcast([P, 2, ST, S]), ALU.mult
                                           ).then_inc(shares.s, 1)
                        if b is not None:
                            if p == 1:
                                front(b)
                            if p == 3:
                                front_root(b)
                            if p == 6:
                                front_bias(b)

                front(0)
                front_root(0)
                front_bias(0)
                in_turns(pool, step)

            @block.scalar
            def _(act):
                def project(b):
                    reached(act, xT_ps, b)
                    act.activation(xnT[:], psP[0][:], ACT.Copy).then_inc(xT_sb.s, 1)

                def queries(b):
                    reached(act, q_ps, b)
                    for c in range(QC):
                        last = act.activation(qT[:, c, :], psS[0][:, c // 2, c % 2, :],
                                              ACT.Identity, bias=bq[:, c:c + 1])
                    last.then_inc(q_sb.s, 1)

                def step(i, ahead):
                    for p in range(PAIRS):
                        reached(act, shifts, i, p + 1)
                        for r in range(2):
                            for t in range(ST):
                                last = act.activation(
                                    prob[p % 2][:, r, t, :], psS[p % 2][:, r, t, :], ACT.Exp,
                                    bias=shift[:, p % 2, r, t:t + 1], scale=float(DH1) ** -0.5,
                                    accum_out=total[:, p % 2, r, t:t + 1])
                        last.then_inc(probs.s, 1)
                    if ahead is not None:
                        project(ahead)
                    reached(act, heads, i)
                    act.activation(attT[:], psO[:], ACT.Copy).then_inc(aT_sb.s, 1)
                    if ahead is not None:
                        queries(ahead)

                act.wait_ge(loaded, 16 * N_LOADS)
                project(0)
                queries(0)
                in_turns(act, step)

            @block.vector
            def _(dve):
                def rows_of(b):
                    class Tiles:
                        def __getitem__(self, at):
                            return core.x[:, bass.ds(b * ST + at[1], 1), :].rearrange(
                                "p a d -> p (a d)")
                    return Tiles()

                def statistics(b):
                    reached(dve, x_in, b)
                    do = Chain(dve, nchain, b, NORM_STEPS)
                    norms.stats(dve, do, 0, rows_of(b))
                    do.end()

                def normalise(b):
                    released(dve, xT_ps, b)
                    norms.normal(dve, b, 0, xn, rows_of(b)).then_inc(norm.s, 1)

                def values(b):
                    reached(dve, v_ps, b)
                    heads_of = [t.rearrange("p t (h d) -> p t h d", h=H1) for t in (
                        psP[1][:], bv[:].unsqueeze(1).to_broadcast([P, ST, D]))]
                    dve.tensor_tensor(v[:, :, :, 0:DH1], *heads_of, ALU.add).then_inc(v_sb.s, 1)

                def keys(b):
                    reached(dve, k_ps, b)
                    dve.tensor_tensor(kT[:], psS[1][:].rearrange("p a b s -> p (a b) s"),
                                      bk[:].unsqueeze(2).to_broadcast([P, QC, S]), ALU.add
                                      ).then_inc(k_sb.s, 1)

                def transposed(i, p):
                    reached(dve, pT_ps, i, p + 1)
                    for r in range(2):
                        last = dve.tensor_copy(probT[p % 2][:, r, :, :], psP[r][:])
                    last.then_inc(pT_sb.s, 1)

                def step(i, ahead):
                    do = Chain(dve, dchain, i, DVE_STEPS)
                    for p in range(PAIRS):
                        reached(dve, scores, i, p + 1)
                        do(dve.tensor_reduce(top[:, p % 2, :, :], psS[p % 2][:], AX_X, ALU.max))
                        dve.tensor_scalar(shift[:, p % 2, :, :], top[:, p % 2, :, :],
                                          -float(DH1) ** -0.5, None, ALU.mult
                                          ).then_inc(shifts.s, 1)
                        reached(dve, probs, i, p + 1)
                        of_pair = total[:, p % 2, :, :]
                        dve.reciprocal(of_pair, of_pair).then_inc(sums.s, 1)
                        if p:
                            transposed(i, p - 1)
                        if ahead is not None and p == 2:
                            statistics(ahead)
                        if ahead is not None and p == 4:
                            normalise(ahead)
                    transposed(i, PAIRS - 1)
                    if ahead is not None:
                        values(ahead)
                        keys(ahead)
                    reached(dve, f_ps, i)
                    reached(dve, bias_in, i)
                    x_i = core.x[:, bass.ds(i * ST, ST), :]
                    dve.tensor_tensor(x_i, psP[0][:], x_i, ALU.add).then_inc(done.s, 1)
                    do.end()

                dve.wait_ge(loaded, 16 * N_LOADS)
                dve.wait_ge(ready, 2)
                statistics(0)
                normalise(0)
                values(0)
                keys(0)
                in_turns(dve, step)

            @block.tensor
            def _(pe):
                def transposes(dst, src):
                    for t in range(ST):
                        for c in range(DC):
                            last = pe.transpose(dst[:, c, t * P:(t + 1) * P],
                                                src[:, t, c * P:(c + 1) * P], core.ident[:])
                    return last

                def x_transposed(b):
                    reached(pe, norm, b)
                    transposes(psP[0], xn).then_inc(xT_ps.s, 1)

                def value_product(b):
                    reached(pe, ctx_in, b)
                    for g in range(ST):
                        for k in range(2):
                            last = pe.matmul(psP[1][:, g, :], ctxw[:, k, g * P:(g + 1) * P],
                                             wv[:, k, :], start=(k == 0), stop=(k == 1))
                    last.then_inc(v_ps.s, 1)

                def head_product(out, w, src, ready_):
                    for c in range(QC):
                        for k in range(2):
                            last = pe.matmul(out[:, c // 2, c % 2, :], w[:, k, c * P:(c + 1) * P],
                                             src[:, k, :], start=(k == 0), stop=(k == 1))
                    last.then_inc(ready_.s, 1)

                def score_product(p):
                    c = p // 2
                    for r in range(2):
                        head = 32 * (2 * (p % 2) + r)
                        q = slice(head, head + DH1)
                        for t in range(ST):
                            last = pe.matmul(psS[p % 2][:, r, t, :], qT[q, c, t * P:(t + 1) * P],
                                             kT[q, c, :], start=True, stop=True)
                    last.then_inc(scores.s, 1)

                def value_sum(i, p):
                    reached(pe, pT_sb, i, p + 1)
                    for r in range(2):
                        h = 2 * p + r
                        out = psO[32 * (h % 4):32 * (h % 4) + 32, h // 4, :]
                        for g in range(ST):
                            last = pe.matmul(out, v[:, g, h, :], probT[p % 2][:, r, g, :],
                                             start=(g == 0), stop=(g == ST - 1))
                    return last

                def step(i, ahead):
                    reached(pe, q_sb, i)
                    reached(pe, k_sb, i)
                    score_product(0)
                    score_product(1)
                    released(pe, done, i)
                    reached(pe, v_sb, i)
                    for p in range(PAIRS):
                        reached(pe, shares, i, p + 1)
                        if p:
                            reached(pe, pT_sb, i, p)
                        else:
                            released(pe, pT_sb, i)
                        for r in range(2):
                            for t in range(ST):
                                for g in range(ST):
                                    last = pe.transpose(psP[r][:, g, t * P:(t + 1) * P],
                                                        prob[p % 2][:, r, t, g * P:(g + 1) * P],
                                                        core.ident[:])
                        last.then_inc(pT_ps.s, 1)
                        if p + 2 < PAIRS:
                            score_product(p + 2)
                        if p:
                            value_sum(i, p - 1)
                    reached(pe, pT_sb, i)
                    if ahead is not None:
                        x_transposed(ahead)
                    value_sum(i, PAIRS - 1).then_inc(heads.s, 1)
                    if ahead is not None:
                        value_product(ahead)
                        reached(pe, xT_sb, ahead)
                        head_product(psS[0], wq, xnT, q_ps)
                        head_product(psS[1], wk, ctxw, k_ps)
                    reached(pe, aT_sb, i)
                    for t in range(ST):
                        for c in range(QC):
                            last = pe.matmul(psP[0][:, t, :], attT[:, c, t * P:(t + 1) * P],
                                             wo[:, c, :], start=(c == 0), stop=(c == QC - 1))
                    last.then_inc(f_ps.s, 1)

                pe.wait_ge(loaded, 16 * N_LOADS)
                x_transposed(0)
                value_product(0)
                reached(pe, xT_sb, 0)
                head_product(psS[0], wq, xnT, q_ps)
                head_product(psS[1], wk, ctxw, k_ps)
                in_turns(pe, step)


MT = 4
MS = MT * P
NU = NE + SI // P


def moe(core):
    nc, dram = core.nc, core.dram
    TURNS = B * S // MS
    with ExitStack() as own:
        def sb(n, shape, dt=F32):
            return core.sb(own, "m_" + n, shape, dt)

        gate, up = sb("gate", [P, NU, DC, P]), sb("up", [P, NU, DC, P])
        down = sb("down", [P, NU, D])
        router = sb("router", [P, DC, NE])
        bias = sb("router_bias", [P, 1])
        lower = sb("lower", [P, NE, NE])
        xw, xn, xnT = sb("x", [P, MT, D]), sb("xn", [P, MT, D]), sb("xnT", [P, DC, MS])
        top = sb("max", [P, MT])
        score, corr, wt = (sb(n, [P, MT, NE]) for n in ("score", "corrected", "weight"))
        total = sb("total", [P, MT])
        above, equal = sb("above", [P, MT, NE, NE]), sb("equal", [P, MT, NE, NE])
        silu = [sb(f"silu{n}", [P, MS]) for n in range(2)]
        act_u = [sb(f"act{n}", [P, MS]) for n in range(2)]
        acc = sb("acc", [P, MT, D])
        norms = Norms(core, own, "m", 1, MT)
        psG = [core.ps(own, f"m_psG{n}", [P, MS]) for n in range(2)]
        psU = [core.ps(own, f"m_psU{n}", [P, MS]) for n in range(2)]
        psD = core.ps(own, "m_psD", [P, MT, D])
        psX = core.ps(own, "m_psX", [P, MT, D])
        loaded, ready = core.sem("m_loaded"), core.sem("m_ready")
        sig = core.flag
        norm, t_ps, t_sb, r_ps, cen, exps, weights, out_sb = (
            sig("m_" + n) for n in ("norm", "t_ps", "t_sb", "r_ps", "centred", "exps", "weights",
                                    "out_sb"))
        g_ps, g_sb, a_sb = (sig("m_" + n, NU) for n in ("g_ps", "g_sb", "a_sb"))
        d_ps, d_sb, s_ps = sig("m_d_ps", NE), sig("m_d_sb", NE), sig("m_s_ps", NU - NE)
        stored = core.sem("m_stored")
        dchain, pchain = core.sem("m_dve"), core.sem("m_pool")
        DVE_STEPS, POOL_STEPS = 27, 1
        N_LOADS = 13
        out = dram["out"].rearrange("b (t p) d -> p (b t) d", p=P)
        with nc.Block() as block:
            @block.sync
            def _(sp):
                def load(out, in_):
                    sp.dma_start(out, in_).then_inc(loaded, 16)

                def split(name):
                    return dram["L1_ffn_" + name].rearrange("(c p) n -> p c n", p=P)

                load(router[:], split("router_w"))
                load(bias[:], dram["L1_ffn_router_bias"].partition_broadcast(P))
                load(lower[:].rearrange("p a b -> p (a b)"), dram["lower"].partition_broadcast(P))
                for t, name in ((gate, "gate_w"), (up, "up_w")):
                    for c in range(DC):
                        load(t[:, 0:NE, c, :], dram["L1_ffn_" + name][:, c * P:(c + 1) * P, :]
                             .rearrange("e p n -> p e n"))
                        load(t[:, NE:NU, c, :], dram["L1_ffn_s_" + name][c * P:(c + 1) * P, :]
                             .rearrange("p (u n) -> p u n", n=P))
                load(down[:, 0:NE, :], dram["L1_ffn_down_w"].rearrange("e p n -> p e n"))
                load(down[:, NE:NU, :], split("s_down_w"))
                with sp.Fori(0, TURNS) as i:
                    reached(sp, out_sb, i)
                    sp.dma_start(out[:, bass.ds(i * MT, MT), :], acc[:]).then_inc(stored, 16)
                sp.wait_ge(stored, 16 * TURNS)

            @block.gpsimd
            def _(pool):
                pool.memset(norms.half[:], -0.5).then_inc(ready, 1)
                pool.wait_ge(ready, 1)
                with pool.Fori(0, TURNS) as i:
                    do = Chain(pool, pchain, i, POOL_STEPS)
                    norms.root(pool, do, i, 0)
                    do.end()

            @block.scalar
            def _(act):
                with act.Fori(0, TURNS) as i:
                    reached(act, t_ps, i)
                    act.activation(xnT[:].rearrange("p c s -> p (c s)"),
                                   psX[:].rearrange("p t d -> p (t d)"), ACT.Copy
                                   ).then_inc(t_sb.s, 1)
                    reached(act, cen, i)
                    act.activation(score[:], score[:], ACT.Exp).then_inc(exps.s, 1)
                    for u in range(NU):
                        reached(act, g_ps, i, u + 1)
                        if u >= 2:
                            reached(act, a_sb, i, u - 1)
                        act.activation(silu[u % 2][:], psG[u % 2][:], ACT.Silu).then_inc(g_sb.s, 1)

            @block.vector
            def _(dve):
                dve.wait_ge(loaded, 16 * N_LOADS)
                with dve.Fori(0, TURNS) as i:
                    do = Chain(dve, dchain, i, DVE_STEPS)
                    do(dve.tensor_copy(xw[:], core.x[:, bass.ds(i * MT, MT), :]))
                    norms.stats(dve, do, 0, xw)
                    norms.normal(dve, i, 0, xn, xw).then_inc(norm.s, 1)
                    reached(dve, r_ps, i)
                    lg = psD[:, 0, 0:MT * NE].rearrange("p (t e) -> p t e", e=NE)
                    do(dve.tensor_reduce(top[:], lg, AX_X, ALU.max))
                    e8 = [P, MT, NE]
                    dve.tensor_tensor(score[:], lg, top[:].unsqueeze(2).to_broadcast(e8),
                                      ALU.subtract).then_inc(cen.s, 1)
                    reached(dve, exps, i)
                    do(dve.tensor_reduce(total[:], score[:], AX_X, ALU.add))
                    do(dve.reciprocal(total[:], total[:]))
                    do(dve.tensor_tensor(score[:], score[:],
                                         total[:].unsqueeze(2).to_broadcast(e8), ALU.mult))
                    do(dve.tensor_scalar(corr[:], score[:], bias[:, 0:1], None, ALU.add))
                    for t in range(MT):
                        mine = corr[:, t, :].unsqueeze(2).to_broadcast([P, NE, NE])
                        other = corr[:, t, :].unsqueeze(1).to_broadcast([P, NE, NE])
                        do.mark(dve.tensor_tensor(above[:, t, :, :], other, mine, ALU.is_gt))
                        do.mark(dve.tensor_tensor(equal[:, t, :, :], other, mine, ALU.is_equal))
                    do.wait()
                    do(dve.tensor_tensor(equal[:], equal[:],
                                         lower[:].unsqueeze(1).to_broadcast([P, MT, NE, NE]),
                                         ALU.mult))
                    do(dve.tensor_tensor(above[:], above[:], equal[:], ALU.add))
                    do(dve.tensor_reduce(wt[:], above[:], AX_X, ALU.add))
                    do(dve.tensor_scalar(wt[:], wt[:], TOPE - 0.5, None, ALU.is_lt))
                    do(dve.tensor_tensor(wt[:], wt[:], score[:], ALU.mult))
                    do(dve.tensor_reduce(total[:], wt[:], AX_X, ALU.add))
                    do(dve.tensor_scalar(total[:], total[:], 1e-20, None, ALU.add))
                    do(dve.reciprocal(total[:], total[:]))
                    do(dve.tensor_tensor(wt[:], wt[:], total[:].unsqueeze(2).to_broadcast(e8),
                                         ALU.mult))
                    dve.wait_ge(stored, 16 * i)
                    dve.tensor_copy(acc[:], xw[:]).then_inc(weights.s, 1)
                    reached(dve, weights, i)

                    def product(u):
                        reached(dve, g_sb, i, u + 1)
                        dve.tensor_tensor(act_u[u % 2][:], silu[u % 2][:], psU[u % 2][:], ALU.mult
                                          ).then_inc(a_sb.s, 1)

                    product(0)
                    for u in range(NU):
                        if u + 1 < NU:
                            if 1 <= u <= NE:
                                reached(dve, d_ps, i, u)
                            elif u > NE:
                                reached(dve, s_ps, i, u - NE)
                            product(u + 1)
                        if u < NE:
                            reached(dve, d_ps, i, u + 1)
                            for t in range(MT):
                                last = dve.scalar_tensor_tensor(
                                    acc[:, t, :], psD[:, t, :], wt[:, t, u:u + 1], acc[:, t, :],
                                    ALU.mult, ALU.add)
                            last.then_inc(d_sb.s, 1)
                            dve.wait_ge(d_sb.s, i * NE + u + 1)
                    reached(dve, s_ps, i)
                    dve.tensor_tensor(acc[:], acc[:], psX[:], ALU.add).then_inc(out_sb.s, 1)
                    do.end()

            @block.tensor
            def _(pe):
                pe.wait_ge(loaded, 16 * N_LOADS)
                with pe.Fori(0, TURNS) as i:
                    reached(pe, norm, i)
                    released(pe, out_sb, i)
                    px = psX[:].rearrange("p t d -> p (t d)")
                    for c in range(DC):
                        for t in range(MT):
                            last = pe.transpose(px[:, c * MS + t * P:c * MS + (t + 1) * P],
                                                xn[:, t, c * P:(c + 1) * P], core.ident[:])
                    last.then_inc(t_ps.s, 1)
                    reached(pe, t_sb, i)
                    released(pe, d_sb, i)
                    for t in range(MT):
                        for c in range(DC):
                            last = pe.matmul(psD[:, 0, t * NE:(t + 1) * NE],
                                             xnT[:, c, t * P:(t + 1) * P], router[:, c, :],
                                             start=(c == 0), stop=(c == DC - 1))
                    last.then_inc(r_ps.s, 1)

                    def gate_up(u):
                        if u >= 2:
                            reached(pe, a_sb, i, u - 1)
                        for w, o in ((gate, psG), (up, psU)):
                            for c in range(DC):
                                last = pe.matmul(o[u % 2][:], w[:, u, c, :], xnT[:, c, :],
                                                 start=(c == 0), stop=(c == DC - 1))
                        last.then_inc(g_ps.s, 1)

                    def down_product(u):
                        reached(pe, a_sb, i, u + 1)
                        if u < NE:
                            if u == 0:
                                reached(pe, weights, i)
                            else:
                                reached(pe, d_sb, i, u)
                        for t in range(MT):
                            if u < NE:
                                last = pe.matmul(psD[:, t, :], act_u[u % 2][:, t * P:(t + 1) * P],
                                                 down[:, u, :], start=True, stop=True)
                            else:
                                last = pe.matmul(psX[:, t, :], act_u[u % 2][:, t * P:(t + 1) * P],
                                                 down[:, u, :], start=(u == NE and t % 2 == 0),
                                                 stop=(u == NU - 1), skip_group_check=True)
                        last.then_inc(d_ps.s if u < NE else s_ps.s, 1)

                    gate_up(0)
                    for u in range(1, NU):
                        gate_up(u)
                        down_product(u - 1)
                    down_product(NU - 1)


def program(nc, dram):
    with ExitStack() as ctx:
        core = Core(nc, ctx, dram)
        with ExitStack() as first:
            kr = core.sb(first, "kernel_re", [P, 2, D])
            ki = core.sb(first, "kernel_im", [P, 2, D])
            core.phase(spectrum, first, kr, ki)
            core.phase(first_attention, first, kr, ki)
        with ExitStack() as ffn:
            xn_keep = core.sb(ffn, "xn_keep", [P, NT, D])
            with ExitStack() as qkv:
                slots = core.sb(qkv, "qkv_slots", [P, NT, 3], I32)
                tile_group = core.sb(qkv, "qkv_tile_group", [P, 3, TILES], I32)
                results = core.sb(qkv, "qkv_results", [P, 3, NT, D])
                with ExitStack() as placing:
                    rows = core.sb(placing, "qkv_rows", [P, 3, NT, XW])
                    groups = core.sb(placing, "qkv_groups", [P, NT, 3, NG], BF16)
                    core.phase(route_qkv, placing, rows, xn_keep, groups)
                    core.phase(place_tokens, "pq", groups[:].rearrange("p t f g -> p (t f g)"), 3, 0,
                                 slots, tile_group)
                    core.phase(group_products, "gq", 3, rows, slots,
                                   tile_group[:].rearrange("p f t -> p (f t)"),
                                   [core.sorted_x[f] for f in "qkv"],
                                   [core.sorted_y[f] for f in "qkv"], results)
                rows = core.sb(qkv, "f_rows", [P, 1, NT, XW])
                groups = core.sb(qkv, "f_groups", [P, NT, NG], BF16)
                core.phase(token_attention, results, xn_keep, rows, groups)
                core.phase(place_tokens, "pf", groups[:].rearrange("p t g -> p (t g)"), 1, 3,
                             slots[:, :, 0:1], tile_group[:, 0:1, :])
                core.phase(group_products, "gf", 1, rows, slots,
                               tile_group[:].rearrange("p f t -> p (f t)"),
                               [core.sorted_x["f"]], [core.sorted_y["f"]], results, gelu=True)
                core.phase(second_attention, results)
        core.phase(moe)


_OUT_SHAPE = (B, S, D)


def _layout(inputs):
    a = {k: np.ascontiguousarray(v) for k, v in inputs.items()}

    def halves(m):
        return np.ascontiguousarray(m.T.reshape(NSTATE, 2, D // 2).transpose(1, 0, 2)
                                    .reshape(P, D // 2))

    for n in ("A_re", "A_im", "C_re", "C_im"):
        a[n + "T"] = halves(a.pop("L0_xattn_" + n))
    a["ctxT"] = np.ascontiguousarray(a.pop("ctx_768").transpose(0, 2, 1))
    for f in "qkvf":
        a[f"L0_ffn_{f}_nwT"] = np.ascontiguousarray(a.pop(f"L0_ffn_{f}_nw").T)
    gw, gb2 = [], []
    for f in "qkvf":
        w1 = a.pop(f"L0_ffn_{f}_w1").reshape(NG, GL, DC, P, LW).transpose(0, 3, 2, 1, 4)
        b1 = a.pop(f"L0_ffn_{f}_b1").reshape(NG, GH // P, P).transpose(0, 2, 1)
        w2 = a.pop(f"L0_ffn_{f}_w2").reshape(NG, GH // P, P, D).transpose(0, 2, 1, 3)
        gw.append(np.concatenate([w1.reshape(NG * P, DC * GH), b1.reshape(NG * P, GH // P),
                                  w2.reshape(NG * P, GH // P * D)], 1))
        gb2.append(a.pop(f"L0_ffn_{f}_b2"))
    a["group_w"], a["group_b2"] = np.concatenate(gw), np.concatenate(gb2)
    def columns(v):
        return np.ascontiguousarray(v.reshape(-1, P).T)

    for n in ("L0_xattn_g_ffn", "L0_xattn_b_ffn", "L0_xattn_b1", "mask_BxS_bf1"):
        a[n] = columns(a[n])
    def padded(w):
        out = np.zeros((w.shape[0], H1, 32), w.dtype)
        out[:, :, 0:DH1] = w.reshape(-1, H1, DH1)
        return out.reshape(-1, H1 * 32)

    for n in "qk":
        a["c_w" + n] = padded(a.pop("L1_xattn_w" + n))
        a["c_b" + n] = columns(padded(a.pop("L1_xattn_b" + n)[None, :]))
    a["c_wo"] = np.ascontiguousarray(padded(a.pop("L1_xattn_wo").T).T)
    for n in ("mask_BxS_bf1", "mask_BxS2_bf1"):
        a[n] = a[n].view(np.uint8)
    for n in ("L0_xattn_mod_gate", "L1_ffn_router_bias"):
        a[n] = a[n].reshape(1)
    return a


def _tables():
    w = 2 * np.pi * (np.arange(S) + 0.5) / (2 * S)
    t = np.arange(S)
    ang = w[:, None] * t[None, :]
    fwd = np.stack([np.cos(ang), -np.sin(ang)])
    dft = fwd.transpose(2, 0, 1).reshape(ST, P, 2, S).transpose(1, 0, 2, 3)
    kd = fwd.transpose(2, 0, 1).reshape(NA, NCP, 2, S) * (2.0 * 2.0 / (2 * S))
    idft = fwd.transpose(1, 0, 2).reshape(2, P, 2, S).transpose(1, 0, 2, 3)
    leaf_units = np.repeat(np.eye(GL), LW, axis=1)
    tri = np.triu(np.ones((P, P)), 1)
    counts = np.concatenate([P * np.arange(NT), np.arange(TILES),
                             np.tril(np.ones((NG, NG)), -1).ravel()])
    sel = np.zeros((4, 32, QC, P))
    for c in range(QC):
        sel[:, [c, QC + c], c, :] = 1
    lower = np.tril(np.ones((NE, NE)), -1).ravel()
    return {"lower": lower, "c_sel": sel.reshape(P, QC, P), "leaf_units": leaf_units, "tri": tri, "counts": counts, "dft": dft, "kernel_dft": kd, "idft": idft}


def kernel(**inputs):
    import concourse.bacc as _bacc
    from concourse import mybir as _mybir
    from concourse.bass_utils import run_bass_kernel_spmd as _run

    nc = _bacc.Bacc("TRN2", target_bir_lowering=False, num_devices=1)
    arrays = _layout(inputs)
    arrays.update({k: np.ascontiguousarray(v, dtype=np.float32) for k, v in _tables().items()})
    dram = {}
    feed = {}
    for name, a in arrays.items():
        feed[f"in_{name}"] = a
        dram[name] = nc.dram_tensor(f"in_{name}", a.shape, _mybir.dt.from_np(a.dtype),
                                    kind="ExternalInput").ap()
    dram["out"] = nc.dram_tensor("out_0", _OUT_SHAPE, F32, kind="ExternalOutput").ap()
    program(nc, dram)
    r = _run(nc, [feed], core_ids=[0])
    return r.results[0]["out_0"]
```

```python
from contextlib import ExitStack

import numpy as np

import concourse.bass as bass
from concourse import mybir

ALU = mybir.AluOpType
ACT = mybir.ActivationFunctionType
AX_X = mybir.AxisListType.X
F32 = mybir.dt.float32
BF16 = mybir.dt.bfloat16
I32 = mybir.dt.int32
U8 = mybir.dt.uint8

P = 128
B = 8
S = 256
D = 256
DCTX = 192
CP = DCTX // 2
ST = S // P
DC = D // P
NT = B * ST
H0, DH0, TOPK = 4, 32, 32
HID = 4 * D
HC = HID // P
NSTATE = 64
NA, NCP = 32, 8
NEG_MASK = -1e30
NEG_TAKEN = -3e38
EPS = 1e-5
NN, NL, LW, DEPTH = 255, 256, 16, 8
H1, DH1 = 16, 16
NE, EI, TOPE = 8, 128, 4
SI = 512

LOG2E = 1.4426950408889634
LN2_HI, LN2_LO = 0.693145751953125, 1.42860682030941723e-6
ROUND = 12582912.0
INV_2PI = 0.15915494309189535
PI2_A, PI2_B = 6.28125, 0.0019340515136718750
PI2_C = 6.283185307179586 - PI2_A - PI2_B

SLOTS = 3
assert (B - 2) % SLOTS == 0
GL = 16
NG = NL // GL
GH = GL * LW
TMAX = (B * S + NG * (P - 1)) // P
TILES = TMAX + -TMAX % 4
PLACES = TILES * P
W1COLS = DC * GH + GH // P
XW = D + GL
ZERO_FILLS = 4


class Signal:

    def __init__(self, handle, per=1):
        self.s = handle
        self.per = per


def reached(eng, signal, i, k=None):
    eng.wait_ge(signal.s, i * signal.per + (signal.per if k is None else k))


def reached_apart(eng, signal, i, k=None):
    wait_apart(eng, signal.s, i * signal.per + (signal.per if k is None else k))


def released(eng, signal, i):
    eng.wait_ge(signal.s, i * signal.per)


def wait_apart(eng, handle, value):
    eng.to_reg(value)
    eng.wait_ge(handle, 1)
    eng.wait_ge(handle, value)


def in_turns(eng, step, count=B):
    with eng.Fori(0, count - 1) as i:
        step(i, i + 1)
    step(count - 1, None)


def in_slots(eng, step):
    with eng.Fori(0, (B - 2) // SLOTS) as k:
        for n in range(SLOTS):
            i = k * SLOTS + n
            step(i, i + 1, i + 2, n)
    step(B - 2, B - 1, None, (B - 2) % SLOTS)
    step(B - 1, None, None, (B - 1) % SLOTS)


class Chain:

    def __init__(self, eng, handle, turn=0, per=0):
        self.eng, self.s, self.base, self.per, self.n = eng, handle, turn * per, per, 0

    def mark(self, ins):
        self.n += 1
        ins.then_inc(self.s, 1)
        return self.n

    def wait(self, n=None):
        self.eng.wait_ge(self.s, self.base + (self.n if n is None else n))

    def __call__(self, ins):
        self.mark(ins)
        self.wait()

    def wait_apart(self):
        wait_apart(self.eng, self.s, self.base + self.n)

    def end(self):
        assert self.n == self.per, f"the turn has {self.n} steps"


class Core:

    def __init__(self, nc, ctx, dram):
        self.nc, self.ctx, self.dram, self.own = nc, ctx, dram, []
        self.x = self.sb(ctx, "x_tokens", [P, NT, D])
        self.ctxT = self.sb(ctx, "ctx_T", [CP, 2, B * S])
        self.ident = self.sb(ctx, "identity", [P, P])
        self.ones_bf = self.sb(ctx, "ones_row_bf16", [P, P], BF16)
        self.minus_half = self.sb(ctx, "minus_half", [P, ST])
        self.plus_half = self.sb(ctx, "plus_half", [P, ST])
        self.loads = [self.sem("x_loaded"), self.sem("ctx_loaded")]
        self.setup = self.sem("constants_set")
        self.zeroed = self.sem("places_zeroed")
        self.sorted_x = {f: nc.dram_tensor(f"sorted_x_{f}", (PLACES, XW), F32, kind="Internal").ap()
                         for f in "qkvf"}
        self.sorted_y = {f: nc.dram_tensor(f"sorted_y_{f}", (PLACES, D), F32, kind="Internal").ap()
                         for f in "qkvf"}
        self.zero = self.sb(ctx, "zero_row", [P, XW])

    def sb(self, ctx, name, shape, dt=F32):
        return ctx.enter_context(self.nc.sbuf_tensor(name, shape, dt))

    def ps(self, ctx, name, shape, dt=F32):
        return ctx.enter_context(self.nc.psum_tensor(name, shape, dt))

    def sem(self, name):
        handle = self.nc.alloc_semaphore(name=name)
        self.own.append(handle)
        return handle

    def lasting_sem(self, name):
        return self.nc.alloc_semaphore(name=name)

    def phase(self, stage, *args, **kwargs):
        self.own = []
        stage(self, *args, **kwargs)
        self.nc.clear_and_free_semaphores(self.own)
        self.nc.all_engine_barrier()

    def flag(self, name, per=1):
        return Signal(self.sem(name), per)


def row(ap):
    return ap.rearrange("(a n) -> a n", a=1)


def rstd_of(pool, steps, out, var, minus_half):
    steps(pool.tensor_scalar(out, var, EPS, None, ALU.add))
    return pool.tensor_tensor(out, out, minus_half, ALU.pow)


def spectrum(core, ctx, kr, ki, ahead):
    nc, dram = core.nc, core.dram
    with ExitStack() as own:
        HD = D // 2
        logdt = core.sb(own, "s4_logdt", [P, HD])
        are = core.sb(own, "s4_A_re", [P, HD])
        aim = core.sb(own, "s4_A_im", [P, HD])
        cre = core.sb(own, "s4_C_re", [P, HD])
        cim = core.sb(own, "s4_C_im", [P, HD])
        dskip = core.sb(own, "s4_D_skip", [1, D])
        kdft = core.sb(own, "s4_kernel_dft", [P, NCP // 4, 2, S])
        tmp = [core.sb(own, f"s4_t{n}", [P, HD]) for n in range(8)]
        tint = core.sb(own, "s4_int", [P, HD], I32)
        dt = core.sb(own, "s4_dt", [P, HD])
        ea = core.sb(own, "s4_exp_a", [P, HD])
        em1 = core.sb(own, "s4_expm1_a", [P, HD])
        s_half = core.sb(own, "s4_sin_half", [P, HD])
        s_quart = core.sb(own, "s4_sin_quarter", [P, HD])
        bhalf = core.sb(own, "s4_b_half", [P, HD])
        dcr = core.sb(own, "s4_dC_re", [P, HD])
        dci = core.sb(own, "s4_dC_im", [P, HD])
        zr = core.sb(own, "s4_Z_re", [P, NCP, HD])
        zi = core.sb(own, "s4_Z_im", [P, NCP, HD])
        gr = core.sb(own, "s4_G_re", [P, 2, NCP, HD])
        gi = core.sb(own, "s4_minus_G_im", [P, 2, NCP, HD])
        g_part = [core.sb(own, f"s4_G_product{n}", [P, NCP, HD]) for n in range(2)]
        wr = core.sb(own, "s4_W_re", [P, NA, HD])
        wi = core.sb(own, "s4_W_im", [P, NA, HD])
        sq = [core.sb(own, f"s4_square{n}", [P, 2, HD]) for n in range(2)]
        part = [core.sb(own, f"s4_product{n}", [P, NA // 2, HD]) for n in range(2)]
        ksb = core.sb(own, "s4_K", [P, D, NCP // 4])
        pk = core.ps(own, "s4_K_ps", [NA, HD, 2, NCP])
        pf = core.ps(own, "s4_spectrum_ps", [P, 2, 2 * S])
        zero = core.zero
        loaded, chain = core.sem("s4_loaded"), core.sem("s4_steps")
        asked, given = core.sem("s4_act_asked"), core.sem("s4_act_given")
        z_ready, g_steps, g_ready = (core.sem(f"s4_{n}") for n in ("Z_ready", "G_steps", "G_ready"))
        khalf = core.sem("s4_K_half")
        tables, kdone, kevac, fdone = (core.sem(f"s4_{n}") for n in ("tables", "k", "k_evac", "f"))

        def k_part(n, q):
            d = slice(n * HD // 2, (n + 1) * HD // 2)
            return (ksb[NA * q:NA * (q + 1)].rearrange("a (h d) c -> a h d c", h=2)[:, :, d],
                    pk[:, d, :, 2 * q:2 * q + 2].rearrange("a d h c -> a h d c"))

        with nc.Block() as block:
            @block.sync
            def _(sp):
                for h in range(2):
                    sp.dma_start(logdt[64 * h:64 * h + 64, :],
                                 dram["L0_xattn_log_dt"][h * HD:(h + 1) * HD]
                                 .partition_broadcast(64)).then_inc(loaded, 16)
                for t, name in ((are, "A_reT"), (aim, "A_imT"), (cre, "C_reT"), (cim, "C_imT")):
                    sp.dma_start(t[:], dram[name]).then_inc(loaded, 16)
                sp.dma_start(dskip[:], row(dram["L0_xattn_D_skip"])).then_inc(loaded, 16)
                sp.dma_start(kdft[:], dram["kernel_dft"]).then_inc(loaded, 16)
                sp.dma_start(core.x[:], dram["x"].rearrange("b (t p) d -> p (b t) d", p=P)
                             ).then_inc(core.loads[0], 16)
                for c in range(2):
                    sp.dma_start(core.ctxT[:, c, :].rearrange("p (b s) -> p b s", b=B),
                                 dram["ctxT"][:, c * CP:(c + 1) * CP, :].rearrange("b p s -> p b s")
                                 ).then_inc(core.loads[1], 16)

                ahead.load(sp)
                sp.wait_ge(core.setup, 5)
                for t in core.sorted_x.values():
                    sp.dma_start(t.rearrange("(p r) c -> p r c", p=P),
                                 zero[:].unsqueeze(1).to_broadcast([P, TILES, XW])
                                 ).then_inc(core.zeroed, 16)

            @block.gpsimd
            def _(pool):
                pool.memset(zero[:], 0.0).then_inc(core.setup, 1)
                pool.memset(core.ident[:], 0.0).then_inc(core.setup, 1)
                pool.memset(core.ones_bf[:], 1.0).then_inc(core.setup, 1)
                pool.memset(core.minus_half[:], -0.5).then_inc(core.setup, 1)
                pool.memset(core.plus_half[:], 0.5).then_inc(core.setup, 1)
                pool.wait_ge(core.setup, 5)
                pool.affine_select(out=core.ident[:], in_=core.ident[:], compare_op=ALU.not_equal,
                                   fill=1.0, base=0, pattern=[[-1, P]], channel_multiplier=1
                                   ).then_inc(core.setup, 1)
                do = Chain(pool, g_steps)
                do(pool.memset(gr[:], 0.0))
                do(pool.memset(gi[:], 0.0))
                wide = [P, NCP, HD]
                t0, t1 = (t[:] for t in g_part)
                cr, nci = (t[:].unsqueeze(1).to_broadcast(wide) for t in (dcr, dci))
                pool.wait_ge(z_ready, 1)
                do(pool.tensor_tensor(t0, zr[:], cr, ALU.mult))
                do(pool.tensor_tensor(t1, zi[:], nci, ALU.mult))
                for h in range(2):
                    q = slice(64 * h, 64 * h + 64)
                    do(pool.tensor_tensor(gr[q, h], t0[q], t1[q], ALU.add))
                do(pool.tensor_tensor(t0, zr[:], nci, ALU.mult))
                do(pool.tensor_tensor(t1, zi[:], cr, ALU.mult))
                for h in range(2):
                    q = slice(64 * h, 64 * h + 64)
                    do(pool.tensor_tensor(gi[q, h], t0[q], t1[q], ALU.subtract))
                pool.tensor_copy(t0, t0).then_inc(g_ready, 1)

            @block.scalar
            def _(act):
                act.wait_ge(asked, 1)
                act.activation(em1[:], tmp[6][:], ACT.Tanh, scale=0.5).then_inc(given, 1)
                act.wait_ge(asked, 2)
                act.activation(s_half[:], bhalf[:], ACT.Sin).then_inc(given, 1)
                act.activation(s_quart[:], bhalf[:], ACT.Sin, scale=0.5).then_inc(given, 1)
                act.wait_ge(kdone, 2)
                for q in range(4):
                    out, src = k_part(1, q)
                    act.activation(out, src, ACT.Copy).then_inc(khalf, 1)
                act.wait_ge(fdone, 1)
                act.activation(ki[:].rearrange("p k d -> p (k d)"), pf[:, 1, :], ACT.Copy
                               ).then_inc(khalf, 1)

            @block.vector
            def _(dve):
                do = Chain(dve, chain)

                def exp(out, x):
                    c, n, r, p = (t[:] for t in tmp[:4])
                    do(dve.tensor_scalar(c, x, -87.0, 88.0, ALU.max, ALU.min))
                    do(dve.tensor_scalar(n, c, LOG2E, ROUND, ALU.mult, ALU.add))
                    do(dve.tensor_scalar(n, n, ROUND, None, ALU.subtract))
                    do(dve.scalar_tensor_tensor(r, n, -LN2_HI, c, ALU.mult, ALU.add))
                    do(dve.scalar_tensor_tensor(r, n, -LN2_LO, r, ALU.mult, ALU.add))
                    do(dve.tensor_scalar(p, r, 1 / 5040, 1 / 720, ALU.mult, ALU.add))
                    for k in (1 / 120, 1 / 24, 1 / 6, 0.5, 1.0, 1.0):
                        do(dve.tensor_tensor(p, p, r, ALU.mult))
                        do(dve.tensor_scalar(p, p, k, None, ALU.add))
                    do(dve.tensor_scalar(tint[:], n, 127.0, float(1 << 23), ALU.add, ALU.mult))
                    do(dve.tensor_tensor(out, p, tint[:].bitcast(F32), ALU.mult))

                def cmul(outr, outi, ar, ai, br, bi, t0, t1):
                    do(dve.tensor_tensor(t0, ar, br, ALU.mult))
                    do(dve.tensor_tensor(t1, ai, bi, ALU.mult))
                    do(dve.tensor_tensor(outr, t0, t1, ALU.subtract))
                    do(dve.tensor_tensor(t0, ar, bi, ALU.mult))
                    do(dve.tensor_tensor(t1, ai, br, ALU.mult))
                    do(dve.tensor_tensor(outi, t0, t1, ALU.add))

                dve.wait_ge(loaded, 16 * 8)
                exp(dt[:], logdt[:])
                a, b = tmp[6][:], tmp[7][:]
                do(dve.tensor_tensor(a, dt[:], are[:], ALU.mult))
                dve.tensor_tensor(b, dt[:], aim[:], ALU.mult).then_inc(asked, 1)
                dve.wait_ge(asked, 1)
                exp(ea[:], a)
                n, r = tmp[0][:], bhalf[:]
                do(dve.tensor_scalar(b, b, 0.5, None, ALU.mult))
                do(dve.tensor_scalar(n, b, INV_2PI, ROUND, ALU.mult, ALU.add))
                do(dve.tensor_scalar(n, n, ROUND, None, ALU.subtract))
                do(dve.scalar_tensor_tensor(r, n, -PI2_A, b, ALU.mult, ALU.add))
                do(dve.scalar_tensor_tensor(r, n, -PI2_B, r, ALU.mult, ALU.add))
                do(dve.scalar_tensor_tensor(r, n, -PI2_C, r, ALU.mult, ALU.add))
                dve.tensor_scalar(r, r, 3.1415925, -3.1415925, ALU.min, ALU.max).then_inc(asked, 1)
                dve.wait_ge(given, 3)
                do(dve.scalar_tensor_tensor(em1[:], ea[:], 1.0, em1[:], ALU.add, ALU.mult))
                sh, sq_, cm1, cosb, sinb, er, ei, den = (t[:] for t in tmp)
                do(dve.tensor_tensor(sq_, s_quart[:], s_quart[:], ALU.mult))
                do(dve.tensor_scalar(sh, sq_, -2.0, 1.0, ALU.mult, ALU.add))
                do(dve.scalar_tensor_tensor(sinb, s_half[:], 2.0, sh, ALU.mult, ALU.mult))
                do(dve.scalar_tensor_tensor(cm1, s_half[:], -2.0, s_half[:], ALU.mult, ALU.mult))
                do(dve.tensor_scalar(cosb, cm1, 1.0, None, ALU.add))
                do(dve.tensor_tensor(zr[:, 1, :], ea[:], cosb, ALU.mult))
                do(dve.tensor_tensor(zi[:, 1, :], ea[:], sinb, ALU.mult))
                do(dve.tensor_tensor(er, em1[:], cosb, ALU.mult))
                do(dve.tensor_tensor(er, er, cm1, ALU.add))
                do(dve.tensor_tensor(den, are[:], are[:], ALU.mult))
                do(dve.tensor_tensor(sh, aim[:], aim[:], ALU.mult))
                do(dve.tensor_tensor(den, den, sh, ALU.add))
                do(dve.reciprocal(den, den))
                do(dve.tensor_tensor(sh, er, are[:], ALU.mult))
                do(dve.tensor_tensor(sq_, zi[:, 1, :], aim[:], ALU.mult))
                do(dve.tensor_tensor(sh, sh, sq_, ALU.add))
                do(dve.tensor_tensor(ei, zi[:, 1, :], are[:], ALU.mult))
                do(dve.tensor_tensor(sq_, er, aim[:], ALU.mult))
                do(dve.tensor_tensor(ei, ei, sq_, ALU.subtract))
                do(dve.tensor_tensor(er, sh, den, ALU.mult))
                do(dve.tensor_tensor(ei, ei, den, ALU.mult))
                cmul(dcr[:], dci[:], cre[:], cim[:], er, ei, sh, sq_)
                do(dve.tensor_scalar(dci[:], dci[:], -1.0, None, ALU.mult))

                def powers(tr, ti, count, base):
                    br, bi = base
                    have, cur = 1, 0
                    while have < count:
                        s = sq[cur]
                        if have == 1:
                            do(dve.tensor_copy(tr[:, 1, :], br))
                            do(dve.tensor_copy(ti[:, 1, :], bi))
                            br, bi = tr[:, 1, :], ti[:, 1, :]
                        else:
                            wide = [P, have, HD]
                            cmul(tr[:, have:2 * have, :], ti[:, have:2 * have, :],
                                 tr[:, 0:have, :], ti[:, 0:have, :],
                                 br.unsqueeze(1).to_broadcast(wide),
                                 bi.unsqueeze(1).to_broadcast(wide),
                                 part[0][:, 0:have, :], part[1][:, 0:have, :])
                        have *= 2
                        cmul(s[:, 0, :], s[:, 1, :], br, bi, br, bi, sh, sq_)
                        br, bi = s[:, 0, :], s[:, 1, :]
                        cur = 1 - cur
                    return br, bi

                for t in (zr, wr):
                    do(dve.memset(t[:, 0, :], 1.0))
                for t in (zi, wi):
                    do(dve.memset(t[:, 0, :], 0.0))
                do(dve.tensor_copy(cosb, zr[:, 1, :]))
                do(dve.tensor_copy(sinb, zi[:, 1, :]))
                z8 = powers(zr, zi, NCP, (cosb, sinb))
                do(dve.tensor_copy(cosb, z8[0]))
                dve.tensor_copy(sinb, z8[1]).then_inc(z_ready, 1)
                dve.wait_ge(z_ready, 1)
                powers(wr, wi, NA, (cosb, sinb))
                dve.tensor_copy(sh, sq_).then_inc(tables, 1)
                dve.wait_ge(kdone, 1)
                for q in range(4):
                    do(dve.tensor_copy(*k_part(0, q)))
                dve.wait_ge(khalf, 4)
                k0 = ksb[0:1, :, 0]
                dve.scalar_tensor_tensor(k0, dskip[:], 0.5, k0, ALU.mult, ALU.add
                                         ).then_inc(kevac, 1)
                dve.wait_ge(fdone, 1)
                do(dve.tensor_copy(kr[:].rearrange("p k d -> p (k d)"), pf[:, 0, :]))

            @block.tensor
            def _(pe):
                pe.wait_ge(tables, 1)
                pe.wait_ge(g_ready, 1)
                for d in range(HD):
                    pe.matmul(pk[:, d], wr[:, :, d], gr[:, :, :, d], start=True, stop=False)
                    last = pe.matmul(pk[:, d], wi[:, :, d], gi[:, :, :, d],
                                     start=False, stop=True)
                    if d in (HD // 2 - 1, HD - 1):
                        last.then_inc(kdone, 1)
                pe.wait_ge(kevac, 1)
                for comp in range(2):
                    for kc in range(2):
                        for c in range(NCP // 4):
                            last = pe.matmul(pf[:, comp, kc * D:(kc + 1) * D],
                                             kdft[:, c, comp, kc * P:(kc + 1) * P], ksb[:, :, c],
                                             start=(c == 0), stop=(c == NCP // 4 - 1))
                last.then_inc(fdone, 1)


class FirstWeights:
    LOADS, LATE = 16, 6

    def __init__(self, core, ctx):
        self.dram = core.dram

        def sb(name, shape, dt=F32):
            return core.sb(ctx, "a_" + name, shape, dt)

        wq = sb("wq", [P, DC, P])
        wk = sb("wk", [CP, 2, P])
        wv = sb("wv", [CP, 2, D])
        film = [sb("film_in", [P, DC, 2 * D]), sb("film_out", [P, DC, 2 * D])]
        film_b = [sb("film_in_b", [P, 2 * D]), sb("film_out_b", [P, 2 * D])]
        gate = sb("mod_gate", [P, 1])
        g_in, b_in = sb("g_in", [P, D]), sb("b_in", [P, D])
        g_out, b_out = sb("g_out", [P, D]), sb("b_out", [P, D])
        g_ffn, b_ffn = sb("g_ffn", [P, DC]), sb("b_ffn", [P, DC])
        w1, b1 = sb("w1", [P, DC, HID]), sb("b1", [P, HC])
        w2, b2 = sb("w2", [P, HC, D]), sb("b2", [P, D])
        dft, idft = sb("dft", [P, ST, 2, S]), sb("idft", [P, 2, 2, S])
        vmask8 = sb("vmask8", [P, B * S], U8)
        tmask8 = sb("tmask8", [P, NT], U8)
        self.buffers = (wq, wk, wv, film, film_b, gate, g_in, b_in, g_out, b_out, g_ffn, b_ffn, w1,
                        b1, w2, b2, dft, idft, vmask8, tmask8)
        self.loaded, self.late = core.lasting_sem("a_loaded"), core.lasting_sem("a_late_loaded")

    def load(self, sp):
        (wq, wk, wv, film, film_b, gate, g_in, b_in, g_out, b_out, g_ffn, b_ffn, w1, b1, w2, b2, dft,
         idft, vmask8, tmask8) = self.buffers

        def load(out, in_, signal=self.loaded):
            sp.dma_start(out, in_).then_inc(signal, 16)

        def split(name, p=P):
            return self.dram["L0_xattn_" + name].rearrange("(c p) n -> p c n", p=p)

        def spread(name, n=P):
            return self.dram["L0_xattn_" + name].partition_broadcast(n)

        load(wq[:], split("Wq"))
        load(wk[:], split("Wk", CP))
        load(wv[:], split("Wv", CP))
        load(vmask8[:], self.dram["mask_BxS2_bf1"].rearrange("b s -> (b s)")
             .partition_broadcast(P))
        load(tmask8[:], self.dram["mask_BxS_bf1"])
        load(gate[:], spread("mod_gate"))
        for n, name in enumerate(("b_film_in", "b_film_out")):
            load(film_b[n][:], spread(name))
        for t, name in ((g_in, "g_norm_in"), (b_in, "b_norm_in"), (g_out, "g_norm_out"),
                        (b_out, "b_norm_out"), (b2, "b2")):
            load(t[:], spread(name))
        for t, name in ((g_ffn, "g_ffn"), (b_ffn, "b_ffn"), (b1, "b1")):
            load(t[:], self.dram["L0_xattn_" + name])
        for n, name in enumerate(("W_film_in", "W_film_out")):
            load(film[n][:], split(name), self.late)
        load(dft[:], self.dram["dft"], self.late)
        load(idft[:], self.dram["idft"], self.late)
        load(w1[:], split("W1"), self.late)
        load(w2[:], split("W2"), self.late)


def first_attention(core, ctx, kr, ki, weights):
    nc, dram = core.nc, core.dram
    with ExitStack() as own:
        def sb(name, shape, dt=F32):
            return core.sb(own, "a_" + name, shape, dt)

        (wq, wk, wv, film, film_b, gate, g_in, b_in, g_out, b_out, g_ffn, b_ffn, w1, b1, w2, b2, dft,
         idft, vmask8, tmask8) = weights.buffers
        loaded, late = weights.loaded, weights.late
        N_LOADS, N_LATE = weights.LOADS, weights.LATE
        vmask, tmask = sb("vmask", [P, B * S], BF16), sb("tmask", [P, NT])
        ctxw = sb("ctx", [CP, 2, S])
        maskw = sb("mask", [P, S], BF16)
        x_st, x_mv = sb("x_stats", [P, ST, 6]), sb("x_mean_var", [P, ST, 2])
        x_rstd, x_var2 = sb("x_rstd", [P, 2, ST]), sb("x_norm_var", [P, ST])
        st, mv = sb("stats", [P, ST, 6]), sb("mean_var", [P, 2, ST, 2])
        rstd = sb("rstd", [P, 2, ST])
        xn, u, v = ([sb(f"{n}{slot}", [P, ST, D]) for slot in range(SLOTS)]
                    for n in ("xn", "u", "v"))
        xnT, xr = sb("xnT", [P, DC, S]), sb("residual", [P, ST, D])
        qk = sb("qk", [P, 2, S])
        score = sb("score", [P, H0 * ST, S])
        rest = sb("rest", [P, H0 * ST, S])
        top = sb("top", [P, H0 * ST, TOPK])
        nmax = sb("nmax", [P, H0 * ST])
        prob = sb("prob", [P, H0 * ST, S])
        etop, esum = sb("etop", [P, H0 * ST, TOPK]), sb("esum", [P, H0 * ST])
        mean = sb("mean", [P, ST, S])
        attnT, ctT = sb("attnT", [P, ST, S]), sb("ctT", [P, DC, S])
        f_in, f_out = sb("f_in", [P, ST, 2 * D]), sb("f_out", [P, ST, 2 * D])
        x1 = sb("x1", [P, ST, D])
        spec = sb("spec", [P, 2, 2 * S])
        prod = sb("prod", [P, 4, 2 * S])
        yspec = sb("yspec", [P, 2, 2 * S])
        xt = sb("xt", [P, ST, D])
        hT = sb("hT", [P, DC, S])
        act1 = sb("act1", [P, HC, S])
        pS = core.ps(own, "a_scores", [P, H0, ST, S])
        pT = core.ps(own, "a_psT", [P, DC, S])
        pA = core.ps(own, "a_psA", [P, 2, S])
        pB = core.ps(own, "a_psB", [P, 2 * D])
        pC = core.ps(own, "a_psC", [P, 2 * D])

        ready = core.sem("a_ready")
        sig = core.flag
        x_var, x_rs = sig("a_x_var"), sig("a_x_rstd")
        ctx_in, norm, u_ready = sig("a_ctx_in", 2), sig("a_norm"), sig("a_u")
        xT_ps, xT_sb = sig("a_xT_ps"), sig("a_xT_sb")
        proj_ps, proj_sb = sig("a_proj_ps", 2), sig("a_proj_sb", 2)
        scores, score_sb = sig("a_scores_ready"), sig("a_scores_sb")
        first8, left, taken = sig("a_max_ready"), sig("a_left"), sig("a_taken")
        exps, sums, mean_sb = sig("a_exps"), sig("a_sums"), sig("a_mean")
        var_b, rs_b = sig("a_var_b", 2), sig("a_rstd_b", 2)
        at_ps, at_sb = sig("a_at_ps"), sig("a_at_sb")
        ct_ps, ct_sb = sig("a_ct_ps"), sig("a_ct_sb")
        film_ps, film_sb = sig("a_film_ps", 4), sig("a_film_sb", 4)
        x1_ready = sig("a_x1")
        spec_ps, spec_sb = sig("a_spec_ps"), sig("a_spec_sb")
        yi_ready, yr_ready = sig("a_yi"), sig("a_yr")
        y_ps, xt_pre, xt_ready = sig("a_y_ps"), sig("a_xt_pre"), sig("a_xt")
        h_norm, resid = sig("a_h_norm"), sig("a_resid")
        hT_ps, hT_sb = sig("a_hT_ps"), sig("a_hT_sb")
        u_ps, u_act = sig("a_up_ps", HC), sig("a_up_act", HC)
        dn_ps, dn_sb, done = sig("a_down_ps"), sig("a_down_sb"), sig("a_done")
        nchain, tchain, bchain, pfchain, pbchain = (core.sem("a_" + n) for n in (
            "dve_norms", "dve_top", "dve_back", "pool_front", "pool_back"))
        TOP_STEPS = 2 * TOPK // 8 * H0 * ST - 2
        NORM_STEPS, MEAN_STEPS, BACK_STEPS = ST, TOP_STEPS + 6, 2 * ST + 6
        POOL_FRONT, POOL_BACK = 7, 5

        with nc.Block() as block:
            @block.gpsimd
            def _(pool):
                wide = [P, ST, D]

                def root(do, signal, signal_rs, b, n, k):
                    reached_apart(pool, signal, b, k)
                    rstd_of(pool, do, rstd[:, n, :], mv[:, n, :, 1], core.minus_half[:]
                            ).then_inc(signal_rs.s, 1)

                def front_factors(do, b):
                    reached_apart(pool, x_var, b)
                    r1, r2 = x_rstd[:, 0, :], x_rstd[:, 1, :]
                    do(rstd_of(pool, do, r1, x_mv[:, :, 1], core.minus_half[:]))
                    do(pool.tensor_tensor(x_var2[:], x_mv[:, :, 1], r1, ALU.mult))
                    do.mark(pool.tensor_tensor(x_var2[:], x_var2[:], r1, ALU.mult))
                    do.wait_apart()
                    do(rstd_of(pool, do, r2, x_var2[:], core.minus_half[:]))
                    pool.tensor_tensor(r2, r2, r1, ALU.mult).then_inc(x_rs.s, 1)

                def front_context(b):
                    released(pool, proj_ps, b)
                    released(pool, scores, b)
                    pool.tensor_copy(maskw[:], vmask[:, bass.ds(b * S, S)]).then_inc(ctx_in.s, 1)
                    pool.tensor_copy(ctxw[:], core.ctxT[:, :, bass.ds(b * S, S)]
                                     ).then_inc(ctx_in.s, 1)

                def front_gain(do, b, slot):
                    reached(pool, norm, b)
                    do(pool.tensor_tensor(u[slot][:], u[slot][:], g_in[:].unsqueeze(1)
                                          .to_broadcast(wide), ALU.mult))
                    pool.tensor_tensor(u[slot][:], u[slot][:], b_in[:].unsqueeze(1)
                                       .to_broadcast(wide), ALU.add).then_inc(u_ready.s, 1)
                    do.end()

                def step(i, b, f, slot):
                    do = Chain(pool, pbchain, i, POOL_BACK)
                    if f is not None:
                        front = Chain(pool, pfchain, f, POOL_FRONT)
                        front_factors(front, f)
                        front_context(f)
                    reached(pool, film_sb, i)
                    pool.tensor_tensor(f_out[:, :, D:2 * D], f_out[:, :, D:2 * D], xn[slot][:],
                                       ALU.add).then_inc(xt_pre.s, 1)
                    if f is not None:
                        front_gain(front, f, (slot + 2) % SLOTS)
                    reached(pool, spec_sb, i)
                    k_re = kr[:].rearrange("p k d -> p (k d)")
                    k_im = ki[:].rearrange("p k d -> p (k d)")
                    do.mark(pool.tensor_tensor(prod[:, 2, :], spec[:, 0, :], k_im, ALU.mult))
                    do(pool.tensor_tensor(prod[:, 3, :], spec[:, 1, :], k_re, ALU.mult))
                    released(pool, y_ps, i)
                    pool.tensor_tensor(yspec[:, 1, :], prod[:, 2, :], prod[:, 3, :], ALU.add
                                       ).then_inc(yi_ready.s, 1)
                    root(do, var_b, rs_b, i, 0, 1)
                    reached(pool, xt_ready, i)
                    released(pool, done, i)
                    do(pool.tensor_tensor(xr[:], xt[:], b2[:].unsqueeze(1).to_broadcast(wide),
                                          ALU.add))
                    x_i = core.x[:, bass.ds(i * ST, ST), :]
                    pool.tensor_tensor(x_i, x_i, b_out[:].unsqueeze(1).to_broadcast(wide),
                                       ALU.add).then_inc(resid.s, 1)
                    root(do, var_b, rs_b, i, 1, 2)
                    do.end()

                pool.wait_ge(core.setup, 6)
                pool.wait_ge(core.loads[1], 32)
                pool.wait_ge(ready, 6)
                pool.wait_ge(loaded, 16 * (N_LOADS))
                for b in range(2):
                    front = Chain(pool, pfchain, b, POOL_FRONT)
                    front_factors(front, b)
                    front_context(b)
                    front_gain(front, b, b)
                in_slots(pool, step)

            @block.scalar
            def _(act):
                scale = float(DH0) ** -0.5

                def front_xT(b):
                    reached(act, xT_ps, b)
                    act.activation(xnT[:], pT[:], ACT.Copy).then_inc(xT_sb.s, 1)

                def front_proj(b):
                    reached(act, proj_ps, b, 1)
                    act.activation(qk[:], pA[:], ACT.Copy).then_inc(proj_sb.s, 1)

                def front_value(b, slot):
                    reached(act, proj_ps, b, 2)
                    act.activation(v[slot][:].rearrange("p g d -> p (g d)"), pB[:], ACT.Copy
                                   ).then_inc(proj_sb.s, 1)

                def front_scores(b):
                    reached(act, scores, b)
                    released(act, left, b)
                    released(act, exps, b)
                    act.activation(score[:].rearrange("p (h t) s -> p h t s", h=H0), pS[:],
                                   ACT.Copy).then_inc(score_sb.s, 1)

                def front_exps(b):
                    reached(act, first8, b)
                    released(act, mean_sb, b)
                    for j in range(H0 * ST):
                        last = act.activation(prob[:, j, :], score[:, j, :], ACT.Exp,
                                              bias=nmax[:, j:j + 1], scale=scale)
                    last.then_inc(exps.s, 1)

                def front_sums(b):
                    reached(act, taken, b)
                    released(act, mean_sb, b)
                    for j in range(H0 * ST):
                        last = act.activation(etop[:, j, :], top[:, j, :], ACT.Exp,
                                              bias=nmax[:, j:j + 1], scale=scale,
                                              accum_out=esum[:, j:j + 1])
                    last.then_inc(sums.s, 1)

                def step(i, b, f, slot):
                    reached(act, at_ps, i)
                    act.activation(attnT[:].rearrange("p g t -> p (g t)"), pC[:], ACT.Copy
                                   ).then_inc(at_sb.s, 1)
                    reached(act, ct_ps, i)
                    act.activation(ctT[:], pT[:], ACT.Copy).then_inc(ct_sb.s, 1)
                    if f is not None:
                        front_xT(f)
                        front_proj(f)
                    if b is not None:
                        front_exps(b)
                    reached(act, spec_ps, i)
                    act.activation(spec[:, 0, :], pA[:].rearrange("p a b -> p (a b)"), ACT.Copy)
                    act.activation(spec[:, 1, :], pC[:], ACT.Copy).then_inc(spec_sb.s, 1)
                    if f is not None:
                        front_scores(f)
                        front_value(f, (slot + 2) % SLOTS)
                    reached(act, hT_ps, i)
                    for c in range(DC):
                        last = act.activation(hT[:, c, :], pT[:, c, :], ACT.Identity,
                                              bias=b_ffn[:, c:c + 1], scale=g_ffn[:, c:c + 1])
                    last.then_inc(hT_sb.s, 1)
                    for c in range(HC):
                        reached(act, u_ps, i, c // 2 * 2 + 2)
                        act.activation(act1[:, c, :], pS[:, c // 2, c % 2, :], ACT.Gelu,
                                       bias=b1[:, c:c + 1]).then_inc(u_act.s, 1)
                    if b is not None:
                        front_sums(b)

                act.wait_ge(core.loads[0], 16)
                act.wait_ge(loaded, 16 * (N_LOADS))
                front_xT(0)
                front_proj(0)
                front_scores(0)
                front_value(0, 0)
                front_exps(0)
                front_xT(1)
                front_proj(1)
                front_scores(1)
                front_value(1, 1)
                front_sums(0)
                in_slots(act, step)

            @block.vector
            def _(dve):
                dve.wait_ge(loaded, 16 * (N_LOADS))
                n = Chain(dve, ready)
                n(dve.tensor_scalar(vmask[:], vmask8[:], -NEG_MASK, NEG_MASK, ALU.mult, ALU.add))
                n(dve.tensor_scalar(tmask[:], tmask8[:], 1.0 / H0, None, ALU.mult))
                for f in film_b:
                    n(dve.tensor_scalar(f[:, 0:D], f[:, 0:D], gate[:, 0:1], 1.0, ALU.mult, ALU.add))
                    n(dve.tensor_scalar(f[:, D:], f[:, D:], gate[:, 0:1], None, ALU.mult))

                def stats(do, n, signal, src):
                    for t in range(ST):
                        do.mark(dve.bn_stats(st[:, t, :], src(t)))
                    do.wait_apart()
                    for t in range(ST):
                        last = dve.bn_aggr(mv[:, n, t, :], st[:, t, :])
                    last.then_inc(signal.s, 1)

                def normal(n, dst, src):
                    for t in range(ST):
                        last = dve.tensor_scalar(dst[:, t, :], src(t), mv[:, n, t, 0:1],
                                                 rstd[:, n, t:t + 1], ALU.subtract, ALU.mult)
                    return last

                def tile_of(buffer):
                    return lambda t: buffer[:, t, :]

                def x_tile(b, t):
                    return core.x[:, bass.ds(b * ST + t, 1), :].rearrange("p a d -> p (a d)")

                def front_stats(do, b):
                    released(dve, norm, b)
                    for t in range(ST):
                        do.mark(dve.bn_stats(x_st[:, t, :], x_tile(b, t)))
                    do.wait_apart()
                    for t in range(ST):
                        last = dve.bn_aggr(x_mv[:, t, :], x_st[:, t, :])
                    last.then_inc(x_var.s, 1)

                def front_norms(b, slot):
                    reached(dve, x_var, b)
                    reached(dve, x_rs, b)
                    for n, dst in enumerate((xn[slot], u[slot])):
                        for t in range(ST):
                            last = dve.tensor_scalar(dst[:, t, :], x_tile(b, t), x_mv[:, t, 0:1],
                                                     x_rstd[:, n, t:t + 1], ALU.subtract, ALU.mult)
                    last.then_inc(norm.s, 1)

                R = H0 * ST

                def row_in(r, j):
                    return score[:, j, :] if r == 0 else rest[:, j, :]

                def eight(do, b, r):
                    if r == 0:
                        reached_apart(dve, score_sb, b)
                        released(dve, sums, b)
                    elif r == 1:
                        reached_apart(dve, left, b)
                    else:
                        do.wait_apart()
                    for j in range(R):
                        do.mark(dve.max(top[:, j, 8 * r:8 * r + 8], row_in(r, j)))
                    if r == 0:
                        do.wait()
                        dve.tensor_scalar(nmax[:], top[:, :, 0], -float(DH0) ** -0.5, None,
                                          ALU.mult).then_inc(first8.s, 1)

                def take(do, r):
                    do.wait_apart()
                    for j in range(R):
                        last = dve.match_replace(rest[:, j, :], top[:, j, 8 * r:8 * r + 8],
                                                 row_in(r, j), NEG_TAKEN)
                        if j < R - 1 or 0 < r < TOPK // 8 - 1:
                            do.mark(last)
                    if r == 0:
                        last.then_inc(left.s, 1)
                    if r == TOPK // 8 - 1:
                        last.then_inc(taken.s, 1)

                def front_taken(do, b):
                    reached(dve, exps, b)
                    reached(dve, taken, b)
                    do(dve.scalar_tensor_tensor(prob[:], rest[:], NEG_TAKEN, prob[:],
                                                ALU.is_equal, ALU.mult))

                def front_mean(do, b):
                    reached(dve, sums, b)
                    do(dve.reciprocal(esum[:], esum[:]))
                    tm = tmask[:, bass.ds(b * ST, ST)].unsqueeze(1).to_broadcast([P, H0, ST])
                    e3 = esum[:].rearrange("p (h t) -> p h t", h=H0)
                    do(dve.tensor_tensor(e3, e3, tm, ALU.mult))
                    released(dve, at_ps, b)
                    for h in range(H0):
                        for t in range(ST):
                            j = ST * h + t
                            if h == 0:
                                last = dve.tensor_scalar(mean[:, t, :], prob[:, j, :],
                                                         esum[:, j:j + 1], None, ALU.mult)
                            else:
                                last = dve.scalar_tensor_tensor(
                                    mean[:, t, :], prob[:, j, :], esum[:, j:j + 1], mean[:, t, :],
                                    ALU.mult, ALU.add)
                        if h < H0 - 1:
                            do(last)
                    last.then_inc(mean_sb.s, 1)
                    do.end()

                def x1_of(do, i, slot):
                    reached(dve, u_ready, i)
                    reached(dve, film_sb, i, ST)
                    released(dve, hT_ps, i)
                    do(dve.tensor_tensor(x1[:], u[slot][:], f_in[:, :, 0:D], ALU.mult))
                    dve.tensor_tensor(x1[:], x1[:], f_in[:, :, D:2 * D], ALU.add
                                      ).then_inc(x1_ready.s, 1)

                def step(i, b, f, slot):
                    do = Chain(dve, bchain, i, BACK_STEPS)
                    if f is not None:
                        norms = Chain(dve, nchain, f, NORM_STEPS)
                        front_stats(norms, f)
                        norms.end()
                    if b is not None:
                        front = Chain(dve, tchain, b, MEAN_STEPS)
                    for n, (out, bias) in enumerate(((f_in, film_b[0]), (f_out, film_b[1]))):
                        for t in range(ST):
                            reached(dve, film_ps, i, ST * n + t + 1)
                            dve.scalar_tensor_tensor(out[:, t, :], pB[:] if t % 2 == 0 else pC[:],
                                                     gate[:, 0:1], bias[:], ALU.mult, ALU.add
                                                     ).then_inc(film_sb.s, 1)
                        if n == 0:
                            x1_of(do, i, slot)
                            if f is not None:
                                front_norms(f, (slot + 2) % SLOTS)
                            if b is not None:
                                eight(front, b, 0)
                    if b is not None:
                        take(front, 0)
                        eight(front, b, 1)
                    reached(dve, spec_sb, i)
                    k_re = kr[:].rearrange("p k d -> p (k d)")
                    k_im = ki[:].rearrange("p k d -> p (k d)")
                    do.mark(dve.tensor_tensor(prod[:, 0, :], spec[:, 0, :], k_re, ALU.mult))
                    do(dve.tensor_tensor(prod[:, 1, :], spec[:, 1, :], k_im, ALU.mult))
                    dve.tensor_tensor(yspec[:, 0, :], prod[:, 0, :], prod[:, 1, :], ALU.subtract
                                      ).then_inc(yr_ready.s, 1)
                    if b is not None:
                        take(front, 1)
                        eight(front, b, 2)
                    reached(dve, y_ps, i)
                    reached(dve, xt_pre, i)
                    do(dve.tensor_tensor(xt[:], pA[:], f_out[:, :, 0:D], ALU.mult))
                    dve.tensor_tensor(xt[:], xt[:], f_out[:, :, D:2 * D], ALU.add
                                      ).then_inc(xt_ready.s, 1)
                    reached(dve, xt_ready, i)
                    stats(do, 0, var_b, tile_of(xt))
                    reached(dve, rs_b, i, 1)
                    normal(0, x1, tile_of(xt)).then_inc(h_norm.s, 1)
                    if b is not None:
                        take(front, 2)
                        eight(front, b, 3)
                        take(front, 3)
                        front_taken(front, b)
                        front_mean(front, b)
                    reached(dve, dn_ps, i)
                    reached(dve, resid, i)
                    dve.tensor_tensor(xr[:].rearrange("p t d -> p (t d)"),
                                      xr[:].rearrange("p t d -> p (t d)"), pB[:], ALU.add
                                      ).then_inc(dn_sb.s, 1)
                    reached(dve, dn_sb, i)
                    stats(do, 1, var_b, tile_of(xr))
                    reached(dve, rs_b, i, 2)
                    do(normal(1, xr, tile_of(xr)))
                    do(dve.tensor_tensor(xr[:], xr[:], g_out[:].unsqueeze(1)
                                         .to_broadcast([P, ST, D]), ALU.mult))
                    x_i = core.x[:, bass.ds(i * ST, ST), :]
                    dve.tensor_tensor(x_i, xr[:], x_i, ALU.add).then_inc(done.s, 1)
                    do.end()

                dve.wait_ge(core.loads[0], 16)
                for b in range(2):
                    norms = Chain(dve, nchain, b, NORM_STEPS)
                    front_stats(norms, b)
                    norms.end()
                    front_norms(b, b)
                front = Chain(dve, tchain, 0, MEAN_STEPS)
                for r in range(TOPK // 8):
                    eight(front, 0, r)
                    take(front, r)
                front_taken(front, 0)
                front_mean(front, 0)
                in_slots(dve, step)

            @block.tensor
            def _(pe):
                def transposes(dst, src):
                    for t in range(ST):
                        for c in range(DC):
                            last = pe.transpose(dst[:, c, t * P:(t + 1) * P],
                                                src[:, t, c * P:(c + 1) * P], core.ident[:])
                    return last

                def front_xT(b, slot):
                    reached(pe, norm, b)
                    transposes(pT, xn[slot]).then_inc(xT_ps.s, 1)

                def front_proj(b):
                    reached(pe, xT_sb, b)
                    reached(pe, ctx_in, b)
                    released(pe, proj_sb, b)
                    for c in range(DC):
                        pe.matmul(pA[:, 0, :], wq[:, c, :], xnT[:, c, :], start=(c == 0),
                                  stop=(c == DC - 1))
                    for c in range(2):
                        last = pe.matmul(pA[:, 1, :], wk[:, c, :], ctxw[:, c, :], start=(c == 0),
                                         stop=(c == 1))
                    last.then_inc(proj_ps.s, 1)

                def front_value(b):
                    for g in range(ST):
                        for c in range(2):
                            last = pe.matmul(pB[:, g * D:(g + 1) * D], ctxw[:, c, g * P:(g + 1) * P],
                                             wv[:, c, :], start=(c == 0), stop=(c == 1))
                    last.then_inc(proj_ps.s, 1)

                def front_scores(b):
                    reached(pe, proj_sb, b, 1)
                    released(pe, score_sb, b)
                    for t in range(ST):
                        for h in range(H0):
                            r = slice(DH0 * h, DH0 * (h + 1))
                            q = slice(DH0 * h, DH0 * h + 1)
                            pe.matmul(pS[:, h, t, :], core.ones_bf[q, :], maskw[q, :],
                                      start=True, stop=False)
                            last = pe.matmul(pS[:, h, t, :], qk[r, 0, t * P:(t + 1) * P],
                                             qk[r, 1, :], start=False, stop=True)
                    last.then_inc(scores.s, 1)

                def step(i, b, f, slot):
                    reached(pe, mean_sb, i)
                    released(pe, spec_sb, i)
                    for t in range(ST):
                        for g in range(ST):
                            last = pe.transpose(pC[:, g * S + t * P:g * S + (t + 1) * P],
                                                mean[:, t, g * P:(g + 1) * P], core.ident[:])
                    last.then_inc(at_ps.s, 1)
                    released(pe, hT_sb, i)
                    reached(pe, at_sb, i)
                    reached(pe, proj_sb, i, 2)
                    for c in range(DC):
                        for g in range(ST):
                            last = pe.matmul(pT[:, c, :], v[slot][:, g, c * P:(c + 1) * P],
                                             attnT[:, g, :], start=(g == 0), stop=(g == ST - 1))
                    last.then_inc(ct_ps.s, 1)
                    released(pe, dn_sb, i)
                    reached(pe, ct_sb, i)
                    for n in range(2):
                        for t in range(ST):
                            if n:
                                reached(pe, film_sb, i, t + 1)
                            out = pB[:] if t % 2 == 0 else pC[:]
                            for c in range(DC):
                                last = pe.matmul(out, ctT[:, c, t * P:(t + 1) * P],
                                                 film[n][:, c, :], start=(c == 0),
                                                 stop=(c == DC - 1))
                            last.then_inc(film_ps.s, 1)
                    released(pe, xt_ready, i)
                    if f is not None:
                        front_xT(f, (slot + 2) % SLOTS)
                        front_proj(f)
                        reached(pe, proj_sb, f, 1)
                    reached(pe, film_sb, i)
                    reached(pe, x1_ready, i)
                    for part in range(2):
                        for k in range(2):
                            out = pA[:, k, :] if part == 0 else pC[:, k * D:(k + 1) * D]
                            for t in range(ST):
                                last = pe.matmul(out, dft[:, t, part, k * P:(k + 1) * P],
                                                 x1[:, t, :], start=(t == 0), stop=(t == ST - 1))
                    last.then_inc(spec_ps.s, 1)
                    if f is not None:
                        front_scores(f)
                    reached(pe, spec_sb, i)
                    reached(pe, yr_ready, i)
                    reached(pe, yi_ready, i)
                    for t in range(ST):
                        for part in range(2):
                            for k in range(2):
                                last = pe.matmul(pA[:, t, :], idft[:, k, part, t * P:(t + 1) * P],
                                                 yspec[:, part, k * D:(k + 1) * D],
                                                 start=(part == 0 and k == 0),
                                                 stop=(part == 1 and k == 1))
                    last.then_inc(y_ps.s, 1)
                    if f is not None:
                        front_value(f)
                    reached(pe, h_norm, i)
                    transposes(pT, x1).then_inc(hT_ps.s, 1)
                    reached(pe, hT_sb, i)
                    if f is not None:
                        reached(pe, score_sb, f)
                        reached(pe, proj_sb, f, 2)
                    for c in range(HC):
                        for k in range(DC):
                            last = pe.matmul(pS[:, c // 2, c % 2, :], w1[:, k, c * P:(c + 1) * P],
                                             hT[:, k, :], start=(k == 0), stop=(k == DC - 1))
                        last.then_inc(u_ps.s, 1)
                    for t in range(ST):
                        for c in range(HC):
                            if t == 0:
                                reached(pe, u_act, i, c + 1)
                            last = pe.matmul(pB[:, t * D:(t + 1) * D], act1[:, c, t * P:(t + 1) * P],
                                             w2[:, c, :], start=(c == 0), stop=(c == HC - 1))
                    last.then_inc(dn_ps.s, 1)

                pe.wait_ge(loaded, 16 * (N_LOADS))
                pe.wait_ge(ready, 6)
                for b in range(2):
                    front_xT(b, b)
                    front_proj(b)
                    front_scores(b)
                    front_value(b)
                pe.wait_ge(late, 16 * N_LATE)
                in_slots(pe, step)


def leaf_masks(dve, do, bits, m, keep_groups):
    do(dve.memset(m[0][:, :, 0:1], 1.0))
    for level in range(DEPTH):
        n = 1 << level
        here = m[level % 2][:, :, 0:n]
        if n == NG:
            keep_groups(here)
        kids = m[1 - level % 2][:, :, 0:2 * n].rearrange("p j (n c) -> p j n c", c=2)
        do(dve.tensor_tensor(kids[:, :, :, 1], here, bits[:, :, n - 1:2 * n - 1], ALU.mult))
        do(dve.tensor_tensor(kids[:, :, :, 0], here, kids[:, :, :, 1], ALU.subtract))
    return m[DEPTH % 2]


def place_tokens(core, name, group_all, nf, first, slot_i, tile_group_i):
    nc = core.nc
    W = nf * NG
    with ExitStack() as own:
        def sb(n, shape, dt=F32):
            return core.sb(own, f"{name}_{n}", shape, dt)

        tri, ones = sb("tri", [P, P], BF16), sb("ones", [P, P], BF16)
        cst = sb("cst", [P, NT + TILES + NG * NG])
        trif = sb("trif", [P, P])
        total = sb("total", [P, NT, W])
        before = sb("before", [P, NT + 1, W])
        pre = sb("pre", [P, NT, W])
        cmp = sb("cmp", [P, W, max(NG, NT)])
        used, start, end = sb("used", [P, W]), sb("start", [P, W]), sb("end", [P, W])
        slot = sb("slot", [P, NT, nf])
        cmp2 = sb("cmp2", [P, nf, TILES, NG])
        tg = sb("tile_group", [P, nf, TILES])
        psP = core.ps(own, f"{name}_psP", [P, 2, 512])
        psT = core.ps(own, f"{name}_psT", [P, 2, 512])
        loaded, ready = core.sem(name + "_loaded"), core.sem(name + "_ready")
        counted, chain = core.sem(name + "_counted"), core.sem(name + "_steps")
        half = NT // 2 * W
        with nc.Block() as block:
            @block.sync
            def _(sp):
                sp.dma_start(trif[:], core.dram["tri"]).then_inc(loaded, 16)
                sp.dma_start(cst[:], core.dram["counts"].partition_broadcast(P)
                             ).then_inc(loaded, 16)

            @block.tensor
            def _(pe):
                pe.wait_ge(ready, 2)
                for h in range(2):
                    g = group_all[:, h * half:(h + 1) * half]
                    pe.matmul(psP[:, h, 0:half], tri[:], g, start=True, stop=True)
                    last = pe.matmul(psT[:, h, 0:half], ones[:], g, start=True, stop=True)
                last.then_inc(counted, 1)

            @block.vector
            def _(dve):
                do = Chain(dve, chain)
                dve.wait_ge(loaded, 32)
                dve.tensor_copy(tri[:], trif[:]).then_inc(ready, 1)
                dve.memset(ones[:], 1.0).then_inc(ready, 1)
                do.mark(dve.memset(before[:, 0, :], 0.0))
                dve.wait_ge(counted, 1)
                for h in range(2):
                    do(dve.tensor_copy(total[:, h * NT // 2:(h + 1) * NT // 2, :]
                                       .rearrange("p t w -> p (t w)"), psT[:, h, 0:half]))
                for t in range(NT):
                    do(dve.tensor_tensor(before[:, t + 1, :], before[:, t, :], total[:, t, :],
                                         ALU.add))
                count = before[:, NT, :]
                wide = [P, W, NT]
                do(dve.tensor_tensor(cmp[:, :, 0:NT], count.unsqueeze(2).to_broadcast(wide),
                                     cst[:, 0:NT].unsqueeze(1).to_broadcast(wide), ALU.is_gt))
                do(dve.tensor_reduce(used[:], cmp[:, :, 0:NT], AX_X, ALU.add))
                below = cst[:, NT + TILES:].rearrange("p (a b) -> p a b", b=NG)
                for f in range(nf):
                    u = used[:, f * NG:(f + 1) * NG]
                    do(dve.tensor_tensor(cmp[:, f * NG:(f + 1) * NG, 0:NG],
                                         u.unsqueeze(1).to_broadcast([P, NG, NG]), below,
                                         ALU.mult))
                do(dve.tensor_reduce(start[:], cmp[:, :, 0:NG], AX_X, ALU.add))
                do(dve.tensor_tensor(end[:], start[:], used[:], ALU.add))
                do(dve.tensor_scalar(start[:], start[:], float(P), None, ALU.mult))
                for h in range(2):
                    do(dve.tensor_tensor(pre[:, h * NT // 2:(h + 1) * NT // 2, :]
                                         .rearrange("p t w -> p (t w)"), psP[:, h, 0:half],
                                         before[:, h * NT // 2:(h + 1) * NT // 2, :]
                                         .rearrange("p t w -> p (t w)"), ALU.add))
                do(dve.tensor_tensor(pre[:], pre[:], start[:].unsqueeze(1).to_broadcast([P, NT, W]),
                                     ALU.add))
                do(dve.tensor_tensor(pre[:].rearrange("p t w -> p (t w)"),
                                     pre[:].rearrange("p t w -> p (t w)"), group_all, ALU.mult))
                do(dve.tensor_reduce(slot[:], pre[:].rearrange("p t (f s) -> p t f s", f=nf),
                                     AX_X, ALU.add))
                do(dve.tensor_copy(slot_i[:], slot[:]))
                for f in range(nf):
                    wide = [P, TILES, NG]
                    do(dve.tensor_tensor(cmp2[:, f, :, :],
                                         end[:, f * NG:(f + 1) * NG].unsqueeze(1)
                                         .to_broadcast(wide),
                                         cst[:, NT:NT + TILES].unsqueeze(2).to_broadcast(wide),
                                         ALU.is_le))
                    do(dve.tensor_reduce(tg[:, f, :], cmp2[:, f, :, :], AX_X, ALU.add))
                for f in range(nf):
                    do(dve.tensor_scalar(tg[:, f, :], tg[:, f, :], float(NG - 1),
                                         float((first + f) * NG), ALU.min, ALU.add))
                do(dve.tensor_copy(tile_group_i[:], tg[:]))




class LastResults:
    REST = 16 * (NT - ST)

    def __init__(self, core, name, sorted_y, slot_i, f, results):
        self.sorted_y, self.slot_i, self.f, self.results = sorted_y, slot_i, f, results
        self.first, self.rest = (core.lasting_sem(f"{name}_{n}") for n in ("first", "rest"))

    def fetch(self, pool, tiles, signal):
        for t in tiles:
            pool.indirect_dma_start(
                self.results[:, self.f, t, :], None, self.sorted_y,
                bass.IndirectOffsetOnAxis(self.slot_i[:, t, self.f:self.f + 1], 0)
                ).then_inc(signal, 16)

    def fetch_first(self, pool):
        self.fetch(pool, range(ST), self.first)

    def fetch_rest(self, pool):
        self.fetch(pool, range(ST, NT), self.rest)


def group_products(core, name, nf, rows, slot_i, tile_group_i, sorted_x, sorted_y, results,
                   gelu=False):
    nc, dram = core.nc, core.dram
    NB = 4
    TURNS = nf * TILES // NB
    with ExitStack() as own:
        def sb(n, shape, dt=F32):
            return core.sb(own, f"{name}_{n}", shape, dt)

        hold = sb("hold", [GL, GH])
        spread = sb("leaf_units", [GL, GH], BF16)
        xs = [sb(f"x{n}", [P, XW]) for n in range(NB)]
        w12 = [sb(f"w_{n}", [P, W1COLS + GH // P * D]) for n in range(NB)]
        w1 = [w[:, 0:W1COLS] for w in w12]
        w2 = [w[:, W1COLS:].rearrange("p (c d) -> p c d", d=D) for w in w12]
        b2 = [sb(f"b2_{n}", [GL, D]) for n in range(NB)]
        xT = [sb(f"xT{n}", [P, DC, P]) for n in range(NB)]
        leafT = [sb(f"leafT{n}", [GL, P]) for n in range(NB)]
        leafB = [sb(f"leafB{n}", [GL, P], BF16) for n in range(NB)]
        act_h = [sb(f"act{n}", [P, GH // P, P]) for n in range(2)]
        hT = [sb(f"hT{n}", [P, GH // P, P]) for n in range(2)]
        ys = [sb(f"y{n}", [P, D]) for n in range(2)]
        psX = [core.ps(own, f"{name}_psX{n}", [P, 4, P]) for n in range(2)]
        psH = [core.ps(own, f"{name}_psH{n}", [P, 4, P]) for n in range(2)]
        psM = [core.ps(own, f"{name}_psM{n}", [P, 4, P]) for n in range(2)]
        psY = [core.ps(own, f"{name}_psY{n}", [P, 2 * D]) for n in range(2)]
        loaded, ready = core.sem(name + "_loaded"), core.sem(name + "_ready")
        placed = [core.sem(f"{name}_placed{f}") for f in range(nf)]
        fetched = core.sem(name + "_fetched")
        tile_in = [core.sem(f"{name}_tile_in{n}") for n in range(NB)]
        worked = [core.sem(f"{name}_worked{n}") for n in range(NB)]
        stored = [core.sem(f"{name}_stored{n}") for n in range(2)]
        x_ps, xT_sb, h_ps, h_act, h_sb, y_sb = (
            core.sem(f"{name}_{n}") for n in ("x_ps", "xT_sb", "h_ps", "h_act", "h_sb", "y_sb"))

        def on(i, n, j):
            return i + (n + j) // NB, (n + j) % NB

        def turns(eng, step):
            with eng.Fori(0, TURNS - 1) as i:
                for n in range(NB):
                    step(i, n, False)
            for n in range(NB):
                step(TURNS - 1, n, True)

        with nc.Block() as block:
            @block.gpsimd
            def _(pool):
                pool.wait_ge(core.zeroed, 16 * ZERO_FILLS)
                for f in range(nf):
                    for t in range(NT):
                        pool.indirect_dma_start(
                            sorted_x[f], bass.IndirectOffsetOnAxis(slot_i[:, t, f:f + 1], 0),
                            rows[:, f, t, :], None).then_inc(placed[f], 16)
                for f in range(nf):
                    for n in range(2):
                        pool.wait_ge(stored[n], 16 * (f + 1) * TILES // 2)
                    for t in range(NT if f < nf - 1 else 0):
                        pool.indirect_dma_start(
                            results[:, f, t, :], None, sorted_y[f],
                            bass.IndirectOffsetOnAxis(slot_i[:, t, f:f + 1], 0)
                            ).then_inc(fetched, 16)
                if nf > 1:
                    pool.wait_ge(fetched, 16 * NT * (nf - 1))

            @block.sync
            def _(sp):
                sp.dma_start(hold[:], dram["leaf_units"]).then_inc(loaded, 16)
                for f in range(nf):
                    sp.wait_ge(placed[f], 16 * NT)
                    with sp.Fori(f * TILES // NB, (f + 1) * TILES // NB) as i:
                        for n in range(NB):
                            tile = i * NB + n
                            g = sp.value_load(tile_group_i[0:1, bass.ds(tile, 1)], min_val=0,
                                              max_val=4 * NG - 1)
                            sp.wait_ge(worked[n], i)
                            for out, in_ in (
                                    (xs[n][:], sorted_x[f][bass.ds((tile - f * TILES) * P, P), :]),
                                    (w12[n][:], dram["group_w"][bass.ds(g * P, P), :]),
                                    (b2[n][:], dram["group_b2"][bass.ds(g * GL, GL), :])):
                                sp.dma_start(out, in_).then_inc(tile_in[n], 16)

            @block.scalar
            def _(act):
                def activate(i, n):
                    tile, k = i * NB + n, n % 2
                    act.wait_ge(h_ps, tile + 1)
                    for c in range(GH // P):
                        b1 = w1[n][:, DC * GH + c:DC * GH + c + 1]
                        last = act.activation(act_h[k][:, c, :], psH[k][:, c, :],
                                              ACT.Gelu if gelu else ACT.Relu, bias=b1)
                    last.then_inc(h_act, 1)

                def store(f, i, n):
                    tile, k = i * NB + n, n % 2
                    act.wait_ge(worked[n], i + 1)
                    act.wait_ge(stored[k], i * 32 + (16 if n >= 2 else 0))
                    act.activation(ys[k][:], psY[k][:, 0:D], ACT.Copy).then_inc(y_sb, 1)
                    act.wait_ge(y_sb, tile + 1)
                    act.dma_start(sorted_y[f][bass.ds((tile - f * TILES) * P, P), :], ys[k][:]
                                  ).then_inc(stored[k], 16)

                activate(0, 0)
                for f in range(nf):
                    first, end = f * TILES // NB, (f + 1) * TILES // NB
                    with act.Fori(first, end - (f == nf - 1)) as i:
                        for n in range(NB):
                            activate(*on(i, n, 1))
                            store(f, i, n)
                for n in range(NB):
                    if n < NB - 1:
                        activate(TURNS - 1, n + 1)
                    store(nf - 1, TURNS - 1, n)

            @block.vector
            def _(dve):
                dve.wait_ge(loaded, 16)
                dve.tensor_copy(spread[:], hold[:]).then_inc(ready, 1)

                def transposed(i, n):
                    dve.wait_ge(x_ps, i * NB + n + 1)
                    dve.tensor_copy(leafT[n][:], psX[n % 2][0:GL, DC, :])
                    dve.tensor_copy(leafB[n][:], psX[n % 2][0:GL, DC, :])
                    dve.tensor_copy(xT[n][:], psX[n % 2][:, 0:DC, :]).then_inc(xT_sb, 1)

                def leaf_only(i, n):
                    dve.wait_ge(h_act, i * NB + n + 1)
                    dve.tensor_tensor(hT[n % 2][:], act_h[n % 2][:], psM[n % 2][:, 0:GH // P, :],
                                      ALU.mult).then_inc(h_sb, 1)

                def step(i, n, last):
                    if not (last and n >= NB - 2):
                        transposed(*on(i, n, 2))
                    if not (last and n == NB - 1):
                        leaf_only(*on(i, n, 1))

                transposed(0, 0)
                transposed(0, 1)
                leaf_only(0, 0)
                turns(dve, step)

            @block.tensor
            def _(pe):
                pe.wait_ge(ready, 1)

                def transposes(i, n, first=False):
                    tile, k = i * NB + n, n % 2
                    pe.wait_ge(tile_in[n], 48 * i + 48)
                    if not first:
                        pe.wait_ge(xT_sb, tile - 1)
                    for c in range(DC):
                        pe.transpose(psX[k][:, c, :], xs[n][:, c * P:(c + 1) * P], core.ident[:])
                    pe.transpose(psX[k][0:GL, DC, :], xs[n][:, D:XW], core.ident[:]
                                 ).then_inc(x_ps, 1)

                def hidden(i, n, first=False):
                    tile, k = i * NB + n, n % 2
                    pe.wait_ge(xT_sb, tile + 1)
                    if not first:
                        pe.wait_ge(h_sb, tile - 1)
                    for c in range(GH // P):
                        for d in range(DC):
                            w = w1[n][:, d * GH + c * P:d * GH + (c + 1) * P]
                            pe.matmul(psH[k][:, c, :], w, xT[n][:, d, :], start=(d == 0),
                                      stop=(d == DC - 1))
                    for c in range(GH // P):
                        last = pe.matmul(psM[k][:, c, :], spread[:, c * P:(c + 1) * P],
                                         leafB[n][:], start=True, stop=True)
                    last.then_inc(h_ps, 1)

                def output(i, n):
                    tile, k = i * NB + n, n % 2
                    if n >= 2:
                        pe.wait_ge(y_sb, tile - 1)
                    else:
                        pe.wait_ge(y_sb, i * NB + n)
                    pe.matmul(psY[k][:, 0:D], leafT[n][:], b2[n][:], start=True, stop=False)
                    pe.wait_ge(h_sb, tile + 1)
                    for c in range(GH // P):
                        last = pe.matmul(psY[k][:, 0:D], hT[k][:, c, :], w2[n][:, c, :],
                                         start=False, stop=(c == GH // P - 1))
                    last.then_inc(worked[n], 1)

                def step(i, n, last):
                    if not (last and n == NB - 1):
                        hidden(*on(i, n, 1))
                    if not (last and n >= NB - 2):
                        transposes(*on(i, n, 2))
                    output(i, n)

                transposes(0, 0, first=True)
                transposes(0, 1, first=True)
                hidden(0, 0, first=True)
                turns(pe, step)


def standard_factors(core, pool, do, out, hold, var):
    do(rstd_of(pool, do, out, var, core.minus_half[:]))
    do(pool.tensor_tensor(hold, var, out, ALU.mult))
    do.mark(pool.tensor_tensor(hold, hold, out, ALU.mult))
    do.wait_apart()
    do(pool.tensor_scalar(hold, hold, D / (D - 1), None, ALU.mult))
    do.mark(pool.tensor_tensor(hold, hold, core.plus_half[:], ALU.pow))
    do.wait_apart()
    do(rstd_of(pool, do, hold, hold, core.minus_half[:]))
    return pool.tensor_tensor(out, out, hold, ALU.mult)


def route_qkv(core, ctx, rows, xn_keep, group_all):
    nc, dram = core.nc, core.dram
    NF = 3
    with ExitStack() as own:
        def sb(n, shape, dt=F32):
            return core.sb(own, "r_" + n, shape, dt)

        nw, nb = sb("nw", [P, NF, DC, NN]), sb("nb", [P, NF, NN])
        st, mv = sb("stats", [P, ST, 6]), sb("mean_var", [P, ST, 2])
        factor, hold = sb("factor", [P, ST]), sb("hold", [P, ST])
        xn, xnT = sb("xn", [P, ST, D]), sb("xnT", [P, DC, S])
        bits = sb("bits", [P, NF * ST, NN])
        m = [sb(f"mask{n}", [P, NF * ST, NL]) for n in range(2)]
        psT = core.ps(own, "r_psT", [P, DC, S])
        psL = core.ps(own, "r_psL", [P, NF, ST, S])
        loaded, ready = core.sem("r_loaded"), core.sem("r_ready")
        sig = core.flag
        var, rs, norm, kept = sig("r_var"), sig("r_factor"), sig("r_norm"), sig("r_kept")
        t_ps, t_sb, logits, bits_sb = (sig("r_" + n) for n in ("T_ps", "T_sb", "logits", "bits"))
        rows_in = sig("r_rows")
        nchain, dchain, pchain = core.sem("r_dve_norm"), core.sem("r_dve"), core.sem("r_pool")
        MASK_STEPS, POOL_STEPS = 20, 8
        with nc.Block() as block:
            @block.sync
            def _(sp):
                for n, f in enumerate("qkv"):
                    sp.dma_start(nw[:, n, :, :], dram[f"L0_ffn_{f}_nwT"]
                                 .rearrange("(c p) n -> p c n", p=P)).then_inc(loaded, 16)
                    sp.dma_start(nb[:, n, :], dram[f"L0_ffn_{f}_nb"].partition_broadcast(P)
                                 ).then_inc(loaded, 16)

            @block.gpsimd
            def _(pool):
                with pool.Fori(0, B) as i:
                    do = Chain(pool, pchain, i, POOL_STEPS)
                    reached_apart(pool, var, i)
                    standard_factors(core, pool, do, factor[:], hold[:], mv[:, :, 1]
                                     ).then_inc(rs.s, 1)
                    reached(pool, norm, i)
                    pool.tensor_copy(xn_keep[:, bass.ds(i * ST, ST), :], xn[:]).then_inc(kept.s, 1)
                    do.end()

            @block.scalar
            def _(act):
                with act.Fori(0, B) as i:
                    reached(act, t_ps, i)
                    act.activation(xnT[:], psT[:], ACT.Copy).then_inc(t_sb.s, 1)
                    for f in range(NF):
                        last = act.activation(rows[:, f, bass.ds(i * ST, ST), 0:D], xn[:],
                                              ACT.Copy)
                    last.then_inc(rows_in.s, 1)

            @block.vector
            def _(dve):
                def x_tile(b, t):
                    return core.x[:, bass.ds(b * ST + t, 1), :].rearrange("p a d -> p (a d)")

                def stats(b):
                    do = Chain(dve, nchain, b, ST)
                    released(dve, norm, b)
                    for t in range(ST):
                        do.mark(dve.bn_stats(st[:, t, :], x_tile(b, t)))
                    do.wait_apart()
                    for t in range(ST):
                        last = dve.bn_aggr(mv[:, t, :], st[:, t, :])
                    last.then_inc(var.s, 1)
                    do.end()

                def normal(b):
                    reached(dve, var, b)
                    reached(dve, rs, b)
                    released(dve, t_ps, b)
                    released(dve, kept, b)
                    released(dve, rows_in, b)
                    for t in range(ST):
                        last = dve.tensor_scalar(xn[:, t, :], x_tile(b, t), mv[:, t, 0:1],
                                                 factor[:, t:t + 1], ALU.subtract, ALU.mult)
                    last.then_inc(norm.s, 1)

                def step(i, b, f, slot):
                    do = Chain(dve, dchain, i, MASK_STEPS)
                    if b is not None:
                        normal(b)
                    reached(dve, logits, i)
                    nbw = nb[:].unsqueeze(2).to_broadcast([P, NF, ST, NN])
                    dve.tensor_tensor(bits[:].rearrange("p (f t) n -> p f t n", f=NF),
                                      psL[:, :, :, 0:NN], nbw, ALU.is_gt).then_inc(bits_sb.s, 1)
                    if f is not None:
                        stats(f)
                    reached(dve, bits_sb, i)

                    def keep_groups(here):
                        out = group_all[:, bass.ds(i * ST, ST), :, :]
                        dve.tensor_copy(out.rearrange("p t f s -> p f t s"),
                                        here.rearrange("p (f t) s -> p f t s", f=NF))

                    leaves = leaf_masks(dve, do, bits, m, keep_groups)
                    for n in range(NF):
                        by_leaf = leaves[:, n * ST:(n + 1) * ST, :].rearrange(
                            "p t (g l) -> p t l g", l=GL)
                        do.mark(dve.tensor_reduce(rows[:, n, bass.ds(i * ST, ST), D:XW], by_leaf,
                                                  AX_X, ALU.add))
                    do.end()

                stats(0)
                normal(0)
                stats(1)
                dve.wait_ge(loaded, 16 * 2 * NF)
                dve.tensor_scalar(nb[:], nb[:], -1.0, None, ALU.mult).then_inc(ready, 1)
                dve.wait_ge(ready, 1)
                in_slots(dve, step)

            @block.tensor
            def _(pe):
                pe.wait_ge(loaded, 16 * 2 * NF)
                with pe.Fori(0, B) as i:
                    reached(pe, norm, i)
                    released(pe, t_sb, i)
                    for t in range(ST):
                        for c in range(DC):
                            last = pe.transpose(psT[:, c, t * P:(t + 1) * P],
                                                xn[:, t, c * P:(c + 1) * P], core.ident[:])
                    last.then_inc(t_ps.s, 1)
                    reached(pe, t_sb, i)
                    released(pe, bits_sb, i)
                    for f in range(NF):
                        for t in range(ST):
                            for c in range(DC):
                                last = pe.matmul(psL[:, f, t, 0:NN], xnT[:, c, t * P:(t + 1) * P],
                                                 nw[:, f, c, :], start=(c == 0),
                                                 stop=(c == DC - 1))
                    last.then_inc(logits.s, 1)


class Norms:

    def __init__(self, core, ctx, name, kinds, tiles=ST):
        self.core, self.kinds, self.tiles = core, kinds, tiles
        self.st = core.sb(ctx, name + "_stats", [P, tiles, 6])
        self.mv = core.sb(ctx, name + "_mean_var", [P, kinds, tiles, 2])
        self.rstd = core.sb(ctx, name + "_rstd", [P, kinds, tiles])
        self.half = core.sb(ctx, name + "_minus_half", [P, tiles])
        self.var = core.flag(name + "_var", kinds)
        self.rs = core.flag(name + "_rs", kinds)

    def stats(self, dve, do, n, src):
        for t in range(self.tiles):
            do.mark(dve.bn_stats(self.st[:, t, :], src(t)))
        do.wait_apart()
        for t in range(self.tiles):
            last = dve.bn_aggr(self.mv[:, n, t, :], self.st[:, t, :])
        last.then_inc(self.var.s, 1)

    def root(self, pool, do, i, n):
        reached_apart(pool, self.var, i, n + 1)
        rstd_of(pool, do, self.rstd[:, n, :], self.mv[:, n, :, 1], self.half[:]
                ).then_inc(self.rs.s, 1)

    def normal(self, dve, i, n, dst, src):
        reached(dve, self.var, i, n + 1)
        reached(dve, self.rs, i, n + 1)
        for t in range(self.tiles):
            last = dve.tensor_scalar(dst[:, t, :], src(t), self.mv[:, n, t, 0:1],
                                     self.rstd[:, n, t:t + 1], ALU.subtract, ALU.mult)
        return last


def token_attention(core, results, v_last, xn_keep, rows, group_all):
    nc, dram = core.nc, core.dram
    with ExitStack() as own:
        def sb(n, shape, dt=F32):
            return core.sb(own, "t_" + n, shape, dt)

        nw, nb = sb("nw", [P, DC, NN]), sb("nb", [P, NN])
        qk = sb("qk", [P, 2, ST, D])
        qkT = sb("qkT", [P, 2, DC, S])
        mx, nmx, total = sb("max", [P, ST]), sb("minus_max", [P, ST]), sb("total", [P, ST])
        p, pT = sb("p", [P, ST, S]), sb("pT", [P, ST, S])
        y, yT = sb("y", [P, ST, D]), sb("yT", [P, DC, S])
        bits = sb("bits", [P, ST, NN])
        m = [sb(f"mask{n}", [P, ST, NL]) for n in range(2)]
        psQ = core.ps(own, "t_psQ", [P, 2, DC, S])
        psS, psP = core.ps(own, "t_psS", [P, ST, S]), core.ps(own, "t_psP", [P, ST, S])
        psO, psY = core.ps(own, "t_psO", [P, ST, D]), core.ps(own, "t_psY", [P, DC, S])
        psL = core.ps(own, "t_psL", [P, ST, S])
        loaded, ready = core.sem("t_loaded"), core.sem("t_ready")
        sig = core.flag
        (qk_in, q_ps, q_sb, s_ps, m_sb, p_sb, pT_ps, pT_sb, o_ps, y_sb, y_kept, yT_ps, yT_sb,
         l_ps, bits_sb, row_in) = (
            sig("t_" + n) for n in ("qk_in", "q_ps", "q_sb", "s_ps", "m_sb", "p_sb", "pT_ps",
                                    "pT_sb", "o_ps", "y_sb", "y_kept", "yT_ps", "yT_sb", "l_ps",
                                    "bits", "row_in"))
        dchain, mchain = core.sem("t_dve"), core.sem("t_dve_max")
        DVE_STEPS = 19
        with nc.Block() as block:
            @block.sync
            def _(sp):
                sp.dma_start(nw[:], dram["L0_ffn_f_nwT"].rearrange("(c p) n -> p c n", p=P)
                             ).then_inc(loaded, 16)
                sp.dma_start(nb[:], dram["L0_ffn_f_nb"].partition_broadcast(P)
                             ).then_inc(loaded, 16)

            @block.gpsimd
            def _(pool):
                def step(i, b):
                    reached(pool, y_sb, i)
                    xs = core.x[:, bass.ds(i * ST, ST), :]
                    pool.tensor_tensor(xs, xs, y[:], ALU.add).then_inc(y_kept.s, 1)

                v_last.fetch_first(pool)
                v_last.fetch_rest(pool)
                in_turns(pool, step)

            @block.scalar
            def _(act):
                def front_in(b):
                    released(act, q_ps, b)
                    for n in range(2):
                        last = act.activation(qk[:, n, :, :], results[:, n, bass.ds(b * ST, ST), :],
                                              ACT.Copy)
                    last.then_inc(qk_in.s, 1)

                def front_transposed(b):
                    reached(act, q_ps, b)
                    act.activation(qkT[:], psQ[:], ACT.Copy).then_inc(q_sb.s, 1)

                def front_probs(b):
                    reached(act, m_sb, b)
                    for t in range(ST):
                        last = act.activation(p[:, t, :], psS[:, t, :], ACT.Exp,
                                              bias=nmx[:, t:t + 1], scale=float(D) ** -0.5,
                                              accum_out=total[:, t:t + 1])
                    last.then_inc(p_sb.s, 1)

                def step(i, b):
                    if b is not None:
                        front_in(b)
                    reached(act, pT_ps, i)
                    act.activation(pT[:], psP[:], ACT.Copy).then_inc(pT_sb.s, 1)
                    if b is not None:
                        front_transposed(b)
                        front_probs(b)
                    reached(act, yT_ps, i)
                    act.activation(yT[:], psY[:], ACT.Copy).then_inc(yT_sb.s, 1)
                    reached(act, y_sb, i)
                    act.activation(rows[:, 0, bass.ds(i * ST, ST), 0:D], y[:], ACT.Copy
                                   ).then_inc(row_in.s, 1)

                front_in(0)
                front_transposed(0)
                front_probs(0)
                in_turns(act, step)

            @block.vector
            def _(dve):
                def front_max(b):
                    do = Chain(dve, mchain, b, 1)
                    reached(dve, s_ps, b)
                    do(dve.tensor_reduce(mx[:], psS[:], AX_X, ALU.max))
                    dve.tensor_scalar(nmx[:], mx[:], -float(D) ** -0.5, None, ALU.mult
                                      ).then_inc(m_sb.s, 1)
                    do.end()

                def step(i, b):
                    do = Chain(dve, dchain, i, DVE_STEPS)
                    reached(dve, p_sb, i)
                    do(dve.reciprocal(total[:], total[:]))
                    reached(dve, o_ps, i)
                    released(dve, y_kept, i)
                    released(dve, row_in, i)
                    for t in range(ST):
                        xn = xn_keep[:, bass.ds(i * ST + t, 1), :].rearrange("p a d -> p (a d)")
                        last = dve.scalar_tensor_tensor(y[:, t, :], psO[:, t, :],
                                                        total[:, t:t + 1], xn, ALU.mult, ALU.add)
                    last.then_inc(y_sb.s, 1)
                    if b is not None:
                        front_max(b)
                    reached(dve, l_ps, i)
                    dve.tensor_tensor(bits[:], psL[:, :, 0:NN],
                                      nb[:].unsqueeze(1).to_broadcast([P, ST, NN]), ALU.is_gt
                                      ).then_inc(bits_sb.s, 1)
                    reached(dve, bits_sb, i)

                    def keep_groups(here):
                        dve.tensor_copy(group_all[:, bass.ds(i * ST, ST), :], here)

                    leaves = leaf_masks(dve, do, bits, m, keep_groups)
                    do.mark(dve.tensor_reduce(rows[:, 0, bass.ds(i * ST, ST), D:XW],
                                              leaves.rearrange("p t (g l) -> p t l g", l=GL),
                                              AX_X, ALU.add))
                    do.end()

                dve.wait_ge(loaded, 32)
                dve.tensor_scalar(nb[:], nb[:], -1.0, None, ALU.mult).then_inc(ready, 1)
                dve.wait_ge(ready, 1)
                front_max(0)
                in_turns(dve, step)

            @block.tensor
            def _(pe):
                def transposes(dst, src):
                    for t in range(ST):
                        for c in range(DC):
                            last = pe.transpose(dst[:, c, t * P:(t + 1) * P],
                                                src(t)[:, c * P:(c + 1) * P], core.ident[:])
                    return last

                def value(b, t):
                    return results[:, 2, bass.ds(b * ST + t, 1), :].rearrange("p a d -> p (a d)")

                def front_transposes(b):
                    reached(pe, qk_in, b)
                    released(pe, q_sb, b)
                    for n in range(2):
                        last = transposes(psQ[:, n, :, :], lambda t: qk[:, n, t, :])
                    last.then_inc(q_ps.s, 1)

                def front_scores(b):
                    reached(pe, q_sb, b)
                    released(pe, p_sb, b)
                    for t in range(ST):
                        for c in range(DC):
                            last = pe.matmul(psS[:, t, :], qkT[:, 0, c, t * P:(t + 1) * P],
                                             qkT[:, 1, c, :], start=(c == 0), stop=(c == DC - 1))
                    last.then_inc(s_ps.s, 1)

                def step(i, b):
                    reached(pe, p_sb, i)
                    released(pe, pT_sb, i)
                    transposes(psP, lambda t: p[:, t, :]).then_inc(pT_ps.s, 1)
                    if b is not None:
                        front_transposes(b)
                    reached(pe, pT_sb, i)
                    released(pe, y_sb, i)
                    for t in range(ST):
                        for c in range(ST):
                            last = pe.matmul(psO[:, t, :], pT[:, c, t * P:(t + 1) * P],
                                             value(i, c), start=(c == 0), stop=(c == ST - 1))
                    last.then_inc(o_ps.s, 1)
                    if b is not None:
                        front_scores(b)
                    reached(pe, y_sb, i)
                    released(pe, yT_sb, i)
                    transposes(psY, lambda t: y[:, t, :]).then_inc(yT_ps.s, 1)
                    reached(pe, yT_sb, i)
                    released(pe, bits_sb, i)
                    for t in range(ST):
                        for c in range(DC):
                            last = pe.matmul(psL[:, t, 0:NN], yT[:, c, t * P:(t + 1) * P],
                                             nw[:, c, :], start=(c == 0), stop=(c == DC - 1))
                    last.then_inc(l_ps.s, 1)
                    pe.wait_ge(v_last.rest, v_last.REST)

                front_transposes(0)
                front_scores(0)
                pe.wait_ge(v_last.first, 16 * ST)
                pe.wait_ge(loaded, 32)
                in_turns(pe, step)


QC = H1 // 4
PAIRS = H1 // 2


def second_attention(core, results, f_last, ahead):
    nc, dram = core.nc, core.dram
    with ExitStack() as own:
        def sb(n, shape, dt=F32):
            return core.sb(own, "c_" + n, shape, dt)

        wq, wk = sb("wq", [P, DC, QC * P]), sb("wk", [CP, 2, QC * P])
        wv, wo = sb("wv", [CP, 2, D]), sb("wo", [P, QC, D])
        bq, bk = sb("bq", [P, QC]), sb("bk", [P, QC])
        bv, bo = sb("bv", [P, D]), sb("bo", [P, D])
        ctxw = sb("ctx", [CP, 2, S])
        xn, xnT = sb("xn", [P, ST, D]), sb("xnT", [P, DC, S])
        qT, kT = sb("qT", [P, QC, S]), sb("kT", [P, QC, S])
        v = sb("v", [P, ST, H1, 32])
        top, shift = (sb(n, [P, 2, 2, ST]) for n in ("max", "minus_max"))
        prob, probT = ([sb(f"{w}{n}", [P, 2, ST, S]) for n in range(2)]
                       for w in ("prob", "probT"))
        total = sb("total", [P, 2, 2, ST])
        attT = sb("attT", [P, QC, S])
        norms = Norms(core, own, "c", 1)
        psS = [core.ps(own, f"c_psS{n}", [P, 2, ST, S]) for n in range(2)]
        psP = [core.ps(own, f"c_psP{n}", [P, ST, S]) for n in range(2)]
        psO = core.ps(own, "c_psO", [P, QC, S])
        loaded, ready = core.sem("c_loaded"), core.sem("c_ready")
        sig = core.flag
        (x_in, ctx_in, norm, xT_ps, xT_sb, q_ps, k_ps, q_sb, k_sb, v_ps, v_sb, heads,
         aT_sb, f_ps, bias_in, done) = (
            sig("c_" + n) for n in ("x_in", "ctx_in", "norm", "xT_ps", "xT_sb", "q_ps", "k_ps",
                                    "q_sb", "k_sb", "v_ps", "v_sb", "heads", "aT_sb",
                                    "f_ps", "bias_in", "done"))
        scores, shifts, probs, sums, shares, pT_ps, pT_sb = (
            sig("c_" + n, PAIRS) for n in ("scores", "shifts", "probs", "sums", "shares", "probT_ps",
                                           "probT_sb"))
        nchain, dchain, pchain = (core.sem("c_" + n) for n in ("dve_norm", "dve", "pool"))
        NORM_STEPS, DVE_STEPS, POOL_STEPS = 2, PAIRS, 1
        N_LOADS = 8

        with nc.Block() as block:
            @block.sync
            def _(sp):
                def load(out, in_):
                    sp.dma_start(out, in_).then_inc(loaded, 16)

                load(wq[:], dram["c_wq"].rearrange("(c p) n -> p c n", p=P))
                load(wk[:], dram["c_wk"].rearrange("(c p) n -> p c n", p=CP))
                load(wv[:], dram["L1_xattn_wv"].rearrange("(c p) n -> p c n", p=CP))
                load(wo[:], dram["c_wo"].rearrange("(c p) n -> p c n", p=P))
                load(bq[:], dram["c_bq"])
                load(bk[:], dram["c_bk"])
                load(bv[:], dram["L1_xattn_bv"].partition_broadcast(P))
                load(bo[:], dram["L1_xattn_bo"].partition_broadcast(P))
                sp.wait_ge(f_last.rest, f_last.REST)
                ahead.load(sp)

            @block.gpsimd
            def _(pool):
                f_last.fetch_first(pool)
                pool.memset(norms.half[:], -0.5).then_inc(ready, 1)
                pool.memset(v[:], 0.0).then_inc(ready, 1)
                pool.wait_ge(ready, 2)

                def tiles(b):
                    return core.x[:, bass.ds(b * ST, ST), :]

                def front(b):
                    pool.tensor_tensor(tiles(b), tiles(b), results[:, 0, bass.ds(b * ST, ST), :],
                                       ALU.add).then_inc(x_in.s, 1)
                    released(pool, k_ps, b)
                    pool.tensor_copy(ctxw[:], core.ctxT[:, :, bass.ds(b * S, S)]
                                     ).then_inc(ctx_in.s, 1)

                def front_root(b):
                    do = Chain(pool, pchain, b, POOL_STEPS)
                    norms.root(pool, do, b, 0)
                    do.end()

                def front_bias(b):
                    reached_apart(pool, norm, b)
                    pool.tensor_tensor(tiles(b), tiles(b),
                                       bo[:].unsqueeze(1).to_broadcast([P, ST, D]),
                                       ALU.add).then_inc(bias_in.s, 1)

                def step(i, b):
                    for p in range(PAIRS):
                        reached(pool, sums, i, p + 1)
                        pr = prob[p % 2][:]
                        pool.tensor_tensor(pr, pr, total[:, p % 2, :, :].unsqueeze(3)
                                           .to_broadcast([P, 2, ST, S]), ALU.mult
                                           ).then_inc(shares.s, 1)
                        if b is not None:
                            if p == 1:
                                pool.wait_ge(f_last.rest, f_last.REST)
                                front(b)
                            if p == 3:
                                front_root(b)
                            if p == 6:
                                front_bias(b)

                pool.wait_ge(f_last.first, 16 * ST)
                front(0)
                front_root(0)
                pool.wait_ge(loaded, 16 * N_LOADS)
                front_bias(0)
                f_last.fetch_rest(pool)
                in_turns(pool, step)

            @block.scalar
            def _(act):
                def project(b):
                    reached(act, xT_ps, b)
                    act.activation(xnT[:], psP[0][:], ACT.Copy).then_inc(xT_sb.s, 1)

                def queries(b):
                    reached(act, q_ps, b)
                    for c in range(QC):
                        last = act.activation(qT[:, c, :], psS[0][:, c // 2, c % 2, :],
                                              ACT.Identity, bias=bq[:, c:c + 1])
                    last.then_inc(q_sb.s, 1)

                def step(i, ahead):
                    for p in range(PAIRS):
                        reached(act, shifts, i, p + 1)
                        for r in range(2):
                            for t in range(ST):
                                last = act.activation(
                                    prob[p % 2][:, r, t, :], psS[p % 2][:, r, t, :], ACT.Exp,
                                    bias=shift[:, p % 2, r, t:t + 1], scale=float(DH1) ** -0.5,
                                    accum_out=total[:, p % 2, r, t:t + 1])
                        last.then_inc(probs.s, 1)
                    if ahead is not None:
                        project(ahead)
                    reached(act, heads, i)
                    act.activation(attT[:], psO[:], ACT.Copy).then_inc(aT_sb.s, 1)
                    if ahead is not None:
                        queries(ahead)

                act.wait_ge(loaded, 16 * N_LOADS)
                project(0)
                queries(0)
                in_turns(act, step)

            @block.vector
            def _(dve):
                def rows_of(b):
                    return lambda t: core.x[:, bass.ds(b * ST + t, 1), :].rearrange(
                        "p a d -> p (a d)")

                def statistics(b):
                    reached(dve, x_in, b)
                    do = Chain(dve, nchain, b, NORM_STEPS)
                    norms.stats(dve, do, 0, rows_of(b))
                    do.end()

                def normalise(b):
                    released(dve, xT_ps, b)
                    norms.normal(dve, b, 0, xn, rows_of(b)).then_inc(norm.s, 1)

                def values(b):
                    reached(dve, v_ps, b)
                    heads_of = [t.rearrange("p t (h d) -> p t h d", h=H1) for t in (
                        psP[1][:], bv[:].unsqueeze(1).to_broadcast([P, ST, D]))]
                    dve.tensor_tensor(v[:, :, :, 0:DH1], *heads_of, ALU.add).then_inc(v_sb.s, 1)

                def keys(b):
                    reached(dve, k_ps, b)
                    dve.tensor_tensor(kT[:], psS[1][:].rearrange("p a b s -> p (a b) s"),
                                      bk[:].unsqueeze(2).to_broadcast([P, QC, S]), ALU.add
                                      ).then_inc(k_sb.s, 1)

                def transposed(i, p):
                    reached(dve, pT_ps, i, p + 1)
                    for r in range(2):
                        last = dve.tensor_copy(probT[p % 2][:, r, :, :], psP[r][:])
                    last.then_inc(pT_sb.s, 1)

                def step(i, ahead):
                    do = Chain(dve, dchain, i, DVE_STEPS)
                    for p in range(PAIRS):
                        reached(dve, scores, i, p + 1)
                        do(dve.tensor_reduce(top[:, p % 2, :, :], psS[p % 2][:], AX_X, ALU.max))
                        dve.tensor_scalar(shift[:, p % 2, :, :], top[:, p % 2, :, :],
                                          -float(DH1) ** -0.5, None, ALU.mult
                                          ).then_inc(shifts.s, 1)
                        reached(dve, probs, i, p + 1)
                        of_pair = total[:, p % 2, :, :]
                        dve.reciprocal(of_pair, of_pair).then_inc(sums.s, 1)
                        if p:
                            transposed(i, p - 1)
                        if ahead is not None and p == 2:
                            statistics(ahead)
                        if ahead is not None and p == 4:
                            normalise(ahead)
                    transposed(i, PAIRS - 1)
                    if ahead is not None:
                        values(ahead)
                        keys(ahead)
                    reached(dve, f_ps, i)
                    reached(dve, bias_in, i)
                    x_i = core.x[:, bass.ds(i * ST, ST), :]
                    dve.tensor_tensor(x_i, psP[0][:], x_i, ALU.add).then_inc(done.s, 1)
                    do.end()

                dve.wait_ge(loaded, 16 * N_LOADS)
                dve.wait_ge(ready, 2)
                statistics(0)
                normalise(0)
                values(0)
                keys(0)
                in_turns(dve, step)

            @block.tensor
            def _(pe):
                def transposes(dst, src):
                    for t in range(ST):
                        for c in range(DC):
                            last = pe.transpose(dst[:, c, t * P:(t + 1) * P],
                                                src[:, t, c * P:(c + 1) * P], core.ident[:])
                    return last

                def x_transposed(b):
                    reached(pe, norm, b)
                    transposes(psP[0], xn).then_inc(xT_ps.s, 1)

                def value_product(b):
                    reached(pe, ctx_in, b)
                    for g in range(ST):
                        for k in range(2):
                            last = pe.matmul(psP[1][:, g, :], ctxw[:, k, g * P:(g + 1) * P],
                                             wv[:, k, :], start=(k == 0), stop=(k == 1))
                    last.then_inc(v_ps.s, 1)

                def head_product(out, w, src, ready_):
                    for c in range(QC):
                        for k in range(2):
                            last = pe.matmul(out[:, c // 2, c % 2, :], w[:, k, c * P:(c + 1) * P],
                                             src[:, k, :], start=(k == 0), stop=(k == 1))
                    last.then_inc(ready_.s, 1)

                def score_product(p):
                    c = p // 2
                    for r in range(2):
                        head = 32 * (2 * (p % 2) + r)
                        q = slice(head, head + DH1)
                        for t in range(ST):
                            last = pe.matmul(psS[p % 2][:, r, t, :], qT[q, c, t * P:(t + 1) * P],
                                             kT[q, c, :], start=True, stop=True)
                    last.then_inc(scores.s, 1)

                def value_sum(i, p):
                    reached(pe, pT_sb, i, p + 1)
                    for r in range(2):
                        h = 2 * p + r
                        out = psO[32 * (h % 4):32 * (h % 4) + 32, h // 4, :]
                        for g in range(ST):
                            last = pe.matmul(out, v[:, g, h, :], probT[p % 2][:, r, g, :],
                                             start=(g == 0), stop=(g == ST - 1))
                    return last

                def step(i, ahead):
                    reached(pe, q_sb, i)
                    reached(pe, k_sb, i)
                    score_product(0)
                    score_product(1)
                    released(pe, done, i)
                    reached(pe, v_sb, i)
                    for p in range(PAIRS):
                        reached(pe, shares, i, p + 1)
                        if p:
                            reached(pe, pT_sb, i, p)
                        else:
                            released(pe, pT_sb, i)
                        for r in range(2):
                            for t in range(ST):
                                for g in range(ST):
                                    last = pe.transpose(psP[r][:, g, t * P:(t + 1) * P],
                                                        prob[p % 2][:, r, t, g * P:(g + 1) * P],
                                                        core.ident[:])
                        last.then_inc(pT_ps.s, 1)
                        if p + 2 < PAIRS:
                            score_product(p + 2)
                        if p:
                            value_sum(i, p - 1)
                    reached(pe, pT_sb, i)
                    if ahead is not None:
                        x_transposed(ahead)
                    value_sum(i, PAIRS - 1).then_inc(heads.s, 1)
                    if ahead is not None:
                        value_product(ahead)
                        reached(pe, xT_sb, ahead)
                        head_product(psS[0], wq, xnT, q_ps)
                        head_product(psS[1], wk, ctxw, k_ps)
                    reached(pe, aT_sb, i)
                    for t in range(ST):
                        for c in range(QC):
                            last = pe.matmul(psP[0][:, t, :], attT[:, c, t * P:(t + 1) * P],
                                             wo[:, c, :], start=(c == 0), stop=(c == QC - 1))
                    last.then_inc(f_ps.s, 1)

                pe.wait_ge(loaded, 16 * N_LOADS)
                x_transposed(0)
                value_product(0)
                reached(pe, xT_sb, 0)
                head_product(psS[0], wq, xnT, q_ps)
                head_product(psS[1], wk, ctxw, k_ps)
                in_turns(pe, step)


MT = 4
MS = MT * P
NH = SI // P
NU = NH + NE


class MoeWeights:
    LOADS = 13

    def __init__(self, core, ctx):
        self.dram = core.dram

        def sb(n, shape, dt=F32):
            return core.sb(ctx, "m_" + n, shape, dt)

        gate, up = sb("gate", [P, NU, DC, P]), sb("up", [P, NU, DC, P])
        down = sb("down", [P, NU, D])
        router = sb("router", [P, DC, NE])
        bias = sb("router_bias", [P, 1])
        lower = sb("lower", [P, NE, NE])
        self.buffers = gate, up, down, router, bias, lower
        self.loaded = core.lasting_sem("m_loaded")

    def load(self, sp):
        gate, up, down, router, bias, lower = self.buffers

        def load(out, in_):
            sp.dma_start(out, in_).then_inc(self.loaded, 16)

        def split(name):
            return self.dram["L1_ffn_" + name].rearrange("(c p) n -> p c n", p=P)

        load(router[:], split("router_w"))
        load(bias[:], self.dram["L1_ffn_router_bias"].partition_broadcast(P))
        load(lower[:].rearrange("p a b -> p (a b)"), self.dram["lower"].partition_broadcast(P))
        for t, name in ((gate, "gate_w"), (up, "up_w")):
            for c in range(DC):
                load(t[:, NH:NU, c, :], self.dram["L1_ffn_" + name][:, c * P:(c + 1) * P, :]
                     .rearrange("e p n -> p e n"))
                load(t[:, 0:NH, c, :], self.dram["L1_ffn_s_" + name][c * P:(c + 1) * P, :]
                     .rearrange("p (u n) -> p u n", n=P))
        load(down[:, NH:NU, :], self.dram["L1_ffn_down_w"].rearrange("e p n -> p e n"))
        load(down[:, 0:NH, :], split("s_down_w"))


def moe(core, weights):
    nc, dram = core.nc, core.dram
    TURNS = B * S // MS
    with ExitStack() as own:
        def sb(n, shape, dt=F32):
            return core.sb(own, "m_" + n, shape, dt)

        gate, up, down, router, bias, lower = weights.buffers
        loaded, N_LOADS = weights.loaded, weights.LOADS
        xn, xnT = sb("xn", [P, MT, D]), sb("xnT", [P, DC, MS])
        top = sb("max", [P, MT])
        score, corr, wt = (sb(n, [P, MT, NE]) for n in ("score", "corrected", "weight"))
        total = sb("total", [P, MT])
        above, equal = sb("above", [P, MT, NE, NE]), sb("equal", [P, MT, NE, NE])
        silu = [sb(f"silu{n}", [P, MS]) for n in range(2)]
        act_u = [sb(f"act{n}", [P, MS]) for n in range(2)]
        acc = sb("acc", [P, MT, D])
        norms = Norms(core, own, "m", 1, MT)
        psG = [core.ps(own, f"m_psG{n}", [P, MS]) for n in range(2)]
        psU = [core.ps(own, f"m_psU{n}", [P, MS]) for n in range(2)]
        psD = core.ps(own, "m_psD", [P, MT, D])
        psX = core.ps(own, "m_psX", [P, MT, D])
        ready = core.sem("m_ready")
        sig = core.flag
        norm, t_ps, t_sb, r_ps, cen, exps, weights, shared, out_sb = (
            sig("m_" + n) for n in ("norm", "t_ps", "t_sb", "r_ps", "centred", "exps", "weights",
                                    "shared", "out_sb"))
        g_ps, g_sb, a_sb, d_ps = (sig("m_" + n, NU) for n in ("g_ps", "g_sb", "a_sb", "d_ps"))
        d_sb = sig("m_d_sb", NE - 1)
        stored = core.sem("m_stored")
        nchain, dchain, pchain = core.sem("m_dve_norm"), core.sem("m_dve"), core.sem("m_pool")
        DVE_STEPS, POOL_STEPS = 21, 1
        out = dram["out"].rearrange("b (t p) d -> p (b t) d", p=P)
        with nc.Block() as block:
            @block.sync
            def _(sp):
                with sp.Fori(0, TURNS) as i:
                    reached(sp, out_sb, i)
                    sp.dma_start(out[:, bass.ds(i * MT, MT), :], acc[:]).then_inc(stored, 16)
                sp.wait_ge(stored, 16 * TURNS)

            @block.gpsimd
            def _(pool):
                pool.memset(norms.half[:], -0.5).then_inc(ready, 1)
                pool.wait_ge(ready, 1)
                with pool.Fori(0, TURNS) as i:
                    do = Chain(pool, pchain, i, POOL_STEPS)
                    norms.root(pool, do, i, 0)
                    do.end()

            @block.scalar
            def _(act):
                def transposed(b):
                    reached(act, t_ps, b)
                    released(act, g_ps, b)
                    act.activation(xnT[:].rearrange("p c s -> p (c s)"),
                                   psX[:].rearrange("p t d -> p (t d)"), ACT.Copy
                                   ).then_inc(t_sb.s, 1)

                def step(i, b):
                    for u in range(NU):
                        if u == 1:
                            reached(act, cen, i)
                            act.activation(score[:], score[:], ACT.Exp).then_inc(exps.s, 1)
                        reached(act, g_ps, i, u + 1)
                        if u >= 2:
                            reached(act, a_sb, i, u - 1)
                        else:
                            released(act, a_sb, i)
                        act.activation(silu[u % 2][:], psG[u % 2][:], ACT.Silu).then_inc(g_sb.s, 1)
                    if b is not None:
                        transposed(b)

                transposed(0)
                in_turns(act, step, TURNS)

            @block.vector
            def _(dve):
                def x_tiles(b):
                    return lambda t: core.x[:, bass.ds(b * MT + t, 1), :].rearrange(
                        "p a d -> p (a d)")

                def statistics(b):
                    do = Chain(dve, nchain, b, MT)
                    norms.stats(dve, do, 0, x_tiles(b))
                    do.end()

                def normalise(b):
                    released(dve, t_ps, b)
                    norms.normal(dve, b, 0, xn, x_tiles(b)).then_inc(norm.s, 1)

                def router_logits(do, i):
                    reached(dve, r_ps, i)
                    lg = psD[:, 0, 0:MT * NE].rearrange("p (t e) -> p t e", e=NE)
                    do(dve.tensor_reduce(top[:], lg, AX_X, ALU.max))
                    dve.tensor_tensor(score[:], lg, top[:].unsqueeze(2).to_broadcast(e8),
                                      ALU.subtract).then_inc(cen.s, 1)

                e8 = [P, MT, NE]

                def router_weights(do, i):
                    reached(dve, exps, i)
                    do(dve.tensor_reduce(total[:], score[:], AX_X, ALU.add))
                    do(dve.reciprocal(total[:], total[:]))
                    do(dve.tensor_tensor(score[:], score[:],
                                         total[:].unsqueeze(2).to_broadcast(e8), ALU.mult))
                    do(dve.tensor_scalar(corr[:], score[:], bias[:, 0:1], None, ALU.add))
                    for t in range(MT):
                        mine = corr[:, t, :].unsqueeze(2).to_broadcast([P, NE, NE])
                        other = corr[:, t, :].unsqueeze(1).to_broadcast([P, NE, NE])
                        do.mark(dve.tensor_tensor(above[:, t, :, :], other, mine, ALU.is_gt))
                        do.mark(dve.tensor_tensor(equal[:, t, :, :], other, mine, ALU.is_equal))
                    do.wait()
                    do(dve.tensor_tensor(equal[:], equal[:],
                                         lower[:].unsqueeze(1).to_broadcast([P, MT, NE, NE]),
                                         ALU.mult))
                    do(dve.tensor_tensor(above[:], above[:], equal[:], ALU.add))
                    do(dve.tensor_reduce(wt[:], above[:], AX_X, ALU.add))
                    do(dve.tensor_scalar(wt[:], wt[:], TOPE - 0.5, None, ALU.is_lt))
                    do(dve.tensor_tensor(wt[:], wt[:], score[:], ALU.mult))
                    do(dve.tensor_reduce(total[:], wt[:], AX_X, ALU.add))
                    do(dve.tensor_scalar(total[:], total[:], 1e-20, None, ALU.add))
                    do(dve.reciprocal(total[:], total[:]))
                    dve.tensor_tensor(wt[:], wt[:], total[:].unsqueeze(2).to_broadcast(e8),
                                      ALU.mult).then_inc(weights.s, 1)

                def product(i, u):
                    reached(dve, g_sb, i, u + 1)
                    if u >= 2:
                        reached(dve, d_ps, i, u - 1)
                    else:
                        released(dve, d_ps, i)
                    dve.tensor_tensor(act_u[u % 2][:], silu[u % 2][:], psU[u % 2][:], ALU.mult
                                      ).then_inc(a_sb.s, 1)

                def step(i, b):
                    do = Chain(dve, dchain, i, DVE_STEPS)
                    product(i, 0)
                    for u in range(NU):
                        if u == 0:
                            router_logits(do, i)
                        if u + 1 < NU:
                            product(i, u + 1)
                        if u == 1:
                            router_weights(do, i)
                        if u == NH - 1:
                            reached(dve, d_ps, i, NH)
                            dve.wait_ge(stored, 16 * i)
                            dve.tensor_tensor(acc[:], psX[:], core.x[:, bass.ds(i * MT, MT), :],
                                              ALU.add).then_inc(shared.s, 1)
                            reached(dve, shared, i)
                            reached(dve, weights, i)
                        if u >= NH:
                            e = u - NH
                            reached(dve, d_ps, i, u + 1)
                            for t in range(MT):
                                last = dve.scalar_tensor_tensor(
                                    acc[:, t, :], psD[:, t, :], wt[:, t, e:e + 1], acc[:, t, :],
                                    ALU.mult, ALU.add)
                            last.then_inc(out_sb.s if e == NE - 1 else d_sb.s, 1)
                            if e < NE - 1:
                                reached(dve, d_sb, i, e + 1)
                        if b is not None and u == NH + 1:
                            statistics(b)
                        if b is not None and u == NH + 3:
                            normalise(b)
                    do.end()

                dve.wait_ge(loaded, 16 * N_LOADS)
                statistics(0)
                normalise(0)
                in_turns(dve, step, TURNS)

            @block.tensor
            def _(pe):
                def transposes(b):
                    reached(pe, norm, b)
                    px = psX[:].rearrange("p t d -> p (t d)")
                    for c in range(DC):
                        for t in range(MT):
                            last = pe.transpose(px[:, c * MS + t * P:c * MS + (t + 1) * P],
                                                xn[:, t, c * P:(c + 1) * P], core.ident[:])
                    last.then_inc(t_ps.s, 1)

                def router_product(i):
                    released(pe, out_sb, i)
                    for t in range(MT):
                        for c in range(DC):
                            last = pe.matmul(psD[:, 0, t * NE:(t + 1) * NE],
                                             xnT[:, c, t * P:(t + 1) * P], router[:, c, :],
                                             start=(c == 0), stop=(c == DC - 1))
                    last.then_inc(r_ps.s, 1)

                def gate_up(i, u):
                    if u >= 2:
                        reached(pe, a_sb, i, u - 1)
                    else:
                        released(pe, a_sb, i)
                    for w, o in ((gate, psG), (up, psU)):
                        for c in range(DC):
                            last = pe.matmul(o[u % 2][:], w[:, u, c, :], xnT[:, c, :],
                                             start=(c == 0), stop=(c == DC - 1))
                    last.then_inc(g_ps.s, 1)

                def down_product(i, u):
                    reached(pe, a_sb, i, u + 1)
                    if u == NH:
                        reached(pe, weights, i)
                    if u > NH:
                        reached(pe, d_sb, i, u - NH)
                    for t in range(MT):
                        if u >= NH:
                            last = pe.matmul(psD[:, t, :], act_u[u % 2][:, t * P:(t + 1) * P],
                                             down[:, u, :], start=True, stop=True)
                        else:
                            last = pe.matmul(psX[:, t, :], act_u[u % 2][:, t * P:(t + 1) * P],
                                             down[:, u, :], start=(u == 0 and t % 2 == 0),
                                             stop=(u == NH - 1), skip_group_check=True)
                    last.then_inc(d_ps.s, 1)

                def step(i, b):
                    reached(pe, t_sb, i)
                    gate_up(i, 0)
                    router_product(i)
                    for u in range(1, NU):
                        gate_up(i, u)
                        if b is not None and u == NH + 6:
                            reached(pe, shared, i)
                            transposes(b)
                        down_product(i, u - 1)
                    down_product(i, NU - 1)

                pe.wait_ge(loaded, 16 * N_LOADS)
                transposes(0)
                in_turns(pe, step, TURNS)


def program(nc, dram):
    with ExitStack() as ctx:
        core = Core(nc, ctx, dram)
        with ExitStack() as first:
            kr = core.sb(first, "kernel_re", [P, 2, D])
            ki = core.sb(first, "kernel_im", [P, 2, D])
            weights = FirstWeights(core, first)
            core.phase(spectrum, first, kr, ki, weights)
            core.phase(first_attention, first, kr, ki, weights)
        slots = core.sb(ctx, "qkv_slots", [P, NT, 3], I32)
        tile_group = core.sb(ctx, "qkv_tile_group", [P, 3, TILES], I32)
        results = core.sb(ctx, "qkv_results", [P, 3, NT, D])
        with ExitStack() as ffn:
            xn_keep = core.sb(ffn, "xn_keep", [P, NT, D])
            with ExitStack() as placing:
                rows = core.sb(placing, "qkv_rows", [P, 3, NT, XW])
                groups = core.sb(placing, "qkv_groups", [P, NT, 3, NG], BF16)
                core.phase(route_qkv, placing, rows, xn_keep, groups)
                core.phase(place_tokens, "pq", groups[:].rearrange("p t f g -> p (t f g)"), 3, 0,
                           slots, tile_group)
                core.phase(group_products, "gq", 3, rows, slots,
                           tile_group[:].rearrange("p f t -> p (f t)"),
                           [core.sorted_x[f] for f in "qkv"],
                           [core.sorted_y[f] for f in "qkv"], results)
            rows = core.sb(ffn, "f_rows", [P, 1, NT, XW])
            groups = core.sb(ffn, "f_groups", [P, NT, NG], BF16)
            v_last = LastResults(core, "v_results", core.sorted_y["v"], slots, 2, results)
            core.phase(token_attention, results, v_last, xn_keep, rows, groups)
            core.phase(place_tokens, "pf", groups[:].rearrange("p t g -> p (t g)"), 1, 3,
                       slots[:, :, 0:1], tile_group[:, 0:1, :])
            core.phase(group_products, "gf", 1, rows, slots,
                       tile_group[:].rearrange("p f t -> p (f t)"),
                       [core.sorted_x["f"]], [core.sorted_y["f"]], results, gelu=True)
        experts = MoeWeights(core, ctx)
        f_last = LastResults(core, "f_results", core.sorted_y["f"], slots, 0, results)
        core.phase(second_attention, results, f_last, experts)
        core.phase(moe, experts)




_OUT_SHAPE = (B, S, D)


def _layout(inputs):
    a = {k: np.ascontiguousarray(v) for k, v in inputs.items()}

    def halves(m):
        return np.ascontiguousarray(m.T.reshape(NSTATE, 2, D // 2).transpose(1, 0, 2)
                                    .reshape(P, D // 2))

    for n in ("A_re", "A_im", "C_re", "C_im"):
        a[n + "T"] = halves(a.pop("L0_xattn_" + n))
    a["ctxT"] = np.ascontiguousarray(a.pop("ctx_768").transpose(0, 2, 1))
    for f in "qkvf":
        a[f"L0_ffn_{f}_nwT"] = np.ascontiguousarray(a.pop(f"L0_ffn_{f}_nw").T)
    gw, gb2 = [], []
    for f in "qkvf":
        w1 = a.pop(f"L0_ffn_{f}_w1").reshape(NG, GL, DC, P, LW).transpose(0, 3, 2, 1, 4)
        b1 = a.pop(f"L0_ffn_{f}_b1").reshape(NG, GH // P, P).transpose(0, 2, 1)
        w2 = a.pop(f"L0_ffn_{f}_w2").reshape(NG, GH // P, P, D).transpose(0, 2, 1, 3)
        gw.append(np.concatenate([w1.reshape(NG * P, DC * GH), b1.reshape(NG * P, GH // P),
                                  w2.reshape(NG * P, GH // P * D)], 1))
        gb2.append(a.pop(f"L0_ffn_{f}_b2"))
    a["group_w"], a["group_b2"] = np.concatenate(gw), np.concatenate(gb2)

    def columns(v):
        return np.ascontiguousarray(v.reshape(-1, P).T)

    for n in ("L0_xattn_g_ffn", "L0_xattn_b_ffn", "L0_xattn_b1", "mask_BxS_bf1"):
        a[n] = columns(a[n])

    def padded(w):
        out = np.zeros((w.shape[0], H1, 32), w.dtype)
        out[:, :, 0:DH1] = w.reshape(-1, H1, DH1)
        return out.reshape(-1, H1 * 32)

    for n in "qk":
        a["c_w" + n] = padded(a.pop("L1_xattn_w" + n))
        a["c_b" + n] = columns(padded(a.pop("L1_xattn_b" + n)[None, :]))
    a["c_wo"] = np.ascontiguousarray(padded(a.pop("L1_xattn_wo").T).T)
    for n in ("mask_BxS_bf1", "mask_BxS2_bf1"):
        a[n] = a[n].view(np.uint8)
    for n in ("L0_xattn_mod_gate", "L1_ffn_router_bias"):
        a[n] = a[n].reshape(1)
    return a


def _tables():
    w = 2 * np.pi * (np.arange(S) + 0.5) / (2 * S)
    t = np.arange(S)
    ang = w[:, None] * t[None, :]
    fwd = np.stack([np.cos(ang), -np.sin(ang)])
    dft = fwd.transpose(2, 0, 1).reshape(ST, P, 2, S).transpose(1, 0, 2, 3)
    kd = fwd.transpose(2, 0, 1).reshape(NA, 4, NCP // 4, 2, S).transpose(1, 0, 2, 3, 4)
    kd = kd.reshape(P, NCP // 4, 2, S) * (2.0 * 2.0 / (2 * S))
    idft = fwd.transpose(1, 0, 2).reshape(2, P, 2, S).transpose(1, 0, 2, 3)
    leaf_units = np.repeat(np.eye(GL), LW, axis=1)
    tri = np.triu(np.ones((P, P)), 1)
    counts = np.concatenate([P * np.arange(NT), np.arange(TILES),
                             np.tril(np.ones((NG, NG)), -1).ravel()])
    lower = np.tril(np.ones((NE, NE)), -1).ravel()
    return {"dft": dft, "idft": idft, "kernel_dft": kd, "leaf_units": leaf_units, "tri": tri,
            "counts": counts, "lower": lower}


def kernel(**inputs):
    import concourse.bacc as _bacc
    from concourse import mybir as _mybir
    from concourse.bass_utils import run_bass_kernel_spmd as _run

    nc = _bacc.Bacc("TRN2", target_bir_lowering=False, num_devices=1)
    arrays = _layout(inputs)
    arrays.update({k: np.ascontiguousarray(v, dtype=np.float32) for k, v in _tables().items()})
    dram = {}
    feed = {}
    for name, a in arrays.items():
        feed[f"in_{name}"] = a
        dram[name] = nc.dram_tensor(f"in_{name}", a.shape, _mybir.dt.from_np(a.dtype),
                                    kind="ExternalInput").ap()
    dram["out"] = nc.dram_tensor("out_0", _OUT_SHAPE, F32, kind="ExternalOutput").ap()
    program(nc, dram)
    r = _run(nc, [feed], core_ids=[0])
    return r.results[0]["out_0"]
```
